# Optimizing a Trainium2 kernel written in Bass

```python
import numpy as np
import jax
import jax.numpy as jnp

def _softmax(x, axis=-1):
    return jax.nn.softmax(x, axis=axis)

def _gelu(x):
    return jax.nn.gelu(x, approximate=True)

def _silu(x):
    return jax.nn.silu(x)

def _sigmoid(x):
    return jax.nn.sigmoid(x)

def _layernorm(x, axis=-1, eps=1e-05):
    m = jnp.mean(x, axis=axis, keepdims=True)
    v = jnp.var(x, axis=axis, keepdims=True)
    return (x - m) / jnp.sqrt(v + eps)

def _scatter_add(tgt, idx, src, axis=0):
    return tgt.at[idx].add(src)

def _segment_sum(src, seg, n):
    return jax.ops.segment_sum(src, seg, n)
kernel_name = 'mk_early_fusion_d1_tok_img768_r4_4d7e29'

def setup_inputs(seed: int=0):
    np.random.seed(seed)
    _w = jnp.asarray

    def _rec_inputs():
        import jax
        import jax.numpy as jnp
        _rk = jax.random.key(seed)
        x = -0.000147625 + 0.999875 * jax.random.normal(jax.random.fold_in(_rk, 1), (64, 12, 224, 224), jnp.float32)
        txt = -0.0221329 + 10 * jax.random.normal(jax.random.fold_in(_rk, 2), (64, 32, 192), jnp.float32)
        return (x, txt)
    x, txt = _rec_inputs()

    def _L0_tok_setup():
        import jax, jax.numpy as jnp
        import numpy as np
        IMG = 224
        PATCH = 16
        EMBED = 192
        C = 12
        B = 64
        key = jax.random.key(seed)
        k1, k2 = jax.random.split(key)
        x = jax.random.normal(k1, (B, C, IMG, IMG), dtype=jnp.float32)
        channel_weights = jax.random.normal(k2, (C, EMBED), dtype=jnp.float32)
        return {'x': x, 'channel_weights': channel_weights}
    _L0_tok_all = _L0_tok_setup()
    _L0_tok_in = {k: v for k, v in _L0_tok_all.items() if k in ('channel_weights',)}
    del _L0_tok_all

    def _L0_attn_setup():
        import jax, jax.numpy as jnp
        import numpy as np
        NUM_HEADS = 12
        BITS = 8
        BN_EPS = 1e-05

        def fake_quant(x, bits=BITS):
            qmax = float(2 ** (bits - 1) - 1)
            scale = jnp.maximum(jnp.max(jnp.abs(x)), 1e-08) / qmax
            q = jnp.clip(jnp.round(x / scale), -qmax, qmax) * scale
            return x + jax.lax.stop_gradient(q - x)
        key = jax.random.key(seed)
        k1, k2, k3 = jax.random.split(key, 3)
        B, S, D = (4, 512, 192)
        x = jax.random.normal(k1, (B, S, D), dtype=jnp.float32)
        w_in = jax.random.normal(k2, (3 * D, D), dtype=jnp.float32) * 0.02
        w_out = jax.random.normal(k3, (D, D), dtype=jnp.float32) * 0.02
        return {'x': x, 'w_in': w_in, 'w_out': w_out}
    _L0_attn_all = _L0_attn_setup()
    _L0_attn_in = {k: v for k, v in _L0_attn_all.items() if k in ('w_in', 'w_out')}
    del _L0_attn_all

    def _L0_ffn_setup():
        import math
        import jax, jax.numpy as jnp
        import numpy as np
        B, L, D = (8, 1024, 192)
        E = 16
        TOP_K = 2
        F_EXP = 4 * D
        F_SH = F_EXP * 2 // 4
        key = jax.random.key(seed)
        ks = jax.random.split(key, 8)
        s = lambda fan_in: 1.0 / math.sqrt(fan_in)
        return {'hidden_states': jax.random.normal(ks[0], (B, L, D), jnp.float32), 'gate_weight': jax.random.uniform(ks[1], (E, D), jnp.float32, -s(D), s(D)), 'Wg': jax.random.uniform(ks[2], (E, F_EXP, D), jnp.float32, -s(D), s(D)), 'Wu': jax.random.uniform(ks[3], (E, F_EXP, D), jnp.float32, -s(D), s(D)), 'Wd': jax.random.uniform(ks[4], (E, D, F_EXP), jnp.float32, -s(F_EXP), s(F_EXP)), 'Ws_g': jax.random.uniform(ks[5], (F_SH, D), jnp.float32, -s(D), s(D)), 'Ws_u': jax.random.uniform(ks[6], (F_SH, D), jnp.float32, -s(D), s(D)), 'Ws_d': jax.random.uniform(ks[7], (D, F_SH), jnp.float32, -s(F_SH), s(F_SH))}
    _L0_ffn_all = _L0_ffn_setup()
    _L0_ffn_in = {k: v for k, v in _L0_ffn_all.items() if k in ('gate_weight', 'Wg', 'Wu', 'Wd', 'Ws_g', 'Ws_u', 'Ws_d')}
    del _L0_ffn_all
    return {'x': x, 'txt': txt, 'L0_tok_channel_weights': _L0_tok_in['channel_weights'], 'L0_attn_w_in': _L0_attn_in['w_in'], 'L0_attn_w_out': _L0_attn_in['w_out'], 'L0_ffn_gate_weight': _L0_ffn_in['gate_weight'], 'L0_ffn_Wg': _L0_ffn_in['Wg'], 'L0_ffn_Wu': _L0_ffn_in['Wu'], 'L0_ffn_Wd': _L0_ffn_in['Wd'], 'L0_ffn_Ws_g': _L0_ffn_in['Ws_g'], 'L0_ffn_Ws_u': _L0_ffn_in['Ws_u'], 'L0_ffn_Ws_d': _L0_ffn_in['Ws_d']}

def reference(x, txt, L0_tok_channel_weights, L0_attn_w_in, L0_attn_w_out, L0_ffn_gate_weight, L0_ffn_Wg, L0_ffn_Wu, L0_ffn_Wd, L0_ffn_Ws_g, L0_ffn_Ws_u, L0_ffn_Ws_d):
    import jax
    import jax.numpy as jnp

    def _L0_tok_ref(x, channel_weights):
        import jax, jax.numpy as jnp
        import numpy as np
        IMG = 224
        PATCH = 16
        EMBED = 192
        C = 12
        B = 64
        Bb, Cc, H, W = x.shape
        K = PATCH
        n = H // K
        pooled = x.reshape(Bb, Cc, n, K, n, K).sum(axis=(3, 5))
        out = jnp.einsum('bcij,ce->bije', pooled, channel_weights)
        return out.reshape(Bb, n * n, EMBED)

    def _L0_attn_ref(x, w_in, w_out):
        import jax, jax.numpy as jnp
        import numpy as np
        NUM_HEADS = 12
        BITS = 8
        BN_EPS = 1e-05

        def fake_quant(x, bits=BITS):
            qmax = float(2 ** (bits - 1) - 1)
            scale = jnp.maximum(jnp.max(jnp.abs(x)), 1e-08) / qmax
            q = jnp.clip(jnp.round(x / scale), -qmax, qmax) * scale
            return x + jax.lax.stop_gradient(q - x)
        B, S, D = x.shape
        H = NUM_HEADS
        Dh = D // H
        wq_in = fake_quant(w_in)
        wq_out = fake_quant(w_out)
        qkv = jnp.einsum('bsd,ed->bse', x, wq_in)
        q, k, v = jnp.split(qkv, 3, axis=-1)

        def to_heads(t):
            return t.reshape(B, S, H, Dh).transpose(0, 2, 1, 3)
        q = fake_quant(to_heads(q))
        k = fake_quant(to_heads(k))
        v = fake_quant(to_heads(v))
        scores = jnp.einsum('bhqd,bhkd->bhqk', q, k) / jnp.sqrt(jnp.float32(Dh))
        scores = fake_quant(scores)
        attn = fake_quant(jax.nn.softmax(scores, -1))
        ctx = jnp.einsum('bhqk,bhkd->bhqd', attn, v)
        ctx = ctx.transpose(0, 2, 1, 3).reshape(B, S, D)
        ctx = fake_quant(ctx)
        y = jnp.einsum('bsd,ed->bse', ctx, wq_out)
        r = fake_quant(y) + fake_quant(x)
        mean = r.mean(axis=(0, 1))
        var = r.var(axis=(0, 1))
        rn = (r - mean) / jnp.sqrt(var + BN_EPS)
        return fake_quant(rn)

    def _L0_ffn_ref(hidden_states, gate_weight, Wg, Wu, Wd, Ws_g, Ws_u, Ws_d):
        import math
        import jax, jax.numpy as jnp
        import numpy as np
        B, L, D = (8, 1024, 192)
        E = 16
        TOP_K = 2
        F_EXP = 4 * D
        F_SH = F_EXP * 2 // 4
        b, l, d = hidden_states.shape
        n = b * l
        x = hidden_states.reshape(n, d)
        scores = jax.nn.sigmoid(x @ gate_weight.T)
        capacity = math.ceil(n / E * TOP_K)
        topk_score, topk_ids = jax.lax.top_k(scores.T, capacity)
        xg = x[topk_ids]
        gate = jax.nn.silu(jnp.einsum('ecd,efd->ecf', xg, Wg))
        up = jnp.einsum('ecd,efd->ecf', xg, Wu)
        out = jnp.einsum('ecf,edf->ecd', gate * up, Wd)
        out = out * topk_score[..., None]
        y = jnp.zeros((n, d), x.dtype).at[topk_ids.reshape(-1)].add(out.reshape(-1, d))
        y = y.reshape(b, l, d)
        shared = jax.nn.silu(hidden_states @ Ws_g.T) * (hidden_states @ Ws_u.T) @ Ws_d.T
        return y + shared
    h = _L0_tok_ref(x, L0_tok_channel_weights)
    h = jnp.concatenate([h, txt], axis=1)
    h = h + _L0_attn_ref(_layernorm(h, axis=-1), L0_attn_w_in, L0_attn_w_out)
    h = h + _L0_ffn_ref(_layernorm(h, axis=-1), L0_ffn_gate_weight, L0_ffn_Wg, L0_ffn_Wu, L0_ffn_Wd, L0_ffn_Ws_g, L0_ffn_Ws_u, L0_ffn_Ws_d)
    return h

_drawn_inputs = setup_inputs


def setup_inputs(seed=0):
    import zlib

    import numpy as np

    out = dict(_drawn_inputs(seed))
    spreads = {}
    factors = {'L0_attn_w_in': 8.0,
     'L0_attn_w_out': 8.0,
     'L0_ffn_gate_weight': 8.0,
     'L0_ffn_Wg': 8.0,
     'L0_ffn_Wu': 8.0,
     'L0_ffn_Wd': 8.0,
     'L0_ffn_Ws_g': 8.0,
     'L0_ffn_Ws_u': 8.0,
     'L0_ffn_Ws_d': 8.0}
    for name, (base, spread) in spreads.items():
        noise = np.random.default_rng([zlib.crc32(name.encode()), seed]).standard_normal(out[name].shape)
        drawn = base * np.exp(spread * noise) if base else spread * noise
        out[name] = jnp.asarray(drawn.astype(out[name].dtype))
    for name, factor in factors.items():
        out[name] = (out[name] * factor).astype(out[name].dtype)
    return out
```

```python
from contextlib import ExitStack

import concourse.bass as bass
from concourse import mybir

F32 = mybir.dt.float32
BF16 = mybir.dt.bfloat16
I16 = mybir.dt.int16
I32 = mybir.dt.int32
ALU = mybir.AluOpType
ACT = mybir.ActivationFunctionType
AX = mybir.AxisListType
RMAX = bass.bass_isa.ReduceOp.max

BATCH, CHAN, IMG, PATCH, D = 64, 12, 224, 16, 192
GRID = IMG // PATCH
NPATCH = GRID * GRID
NTXT = 32
SEQ = NPATCH + NTXT
NTOK = BATCH * SEQ
HALF = SEQ // 2
REST = NPATCH - HALF
PAIR = 2 * SEQ
NPAIR = BATCH // 2
HEADS, DH = 12, 16
KC, KP = 2, 96
QUAD, QT, QP = BATCH // 4, 7, 112
QMAX = 127.0
TINY = 1e-8
EPS = 1e-5

(S_W, S_WO, S_Q, S_K, S_V, C_Q, C_K, C_V, C_X, S_X, C_S, S_S, S_SV, NEG_SS, X1, X2, X3, C_A, S_CTX, C_CTX,
 S_Y, C_Y, S_RN, U_S, U_CTX, U_Y, TMP0, TMP1, TMP2, TMP3, MSUM) = range(31)
NSCAL = 32


def sliding(i, s, g, groups):
    return (i, s, g) if g < groups else (i + s, 1 - s, g - groups)


def turns(engine, pairs, step):
    step(0, 0, True, False)
    with engine.Fori(0, pairs // 2 - 1) as i:
        step(i, 1, False, False)
        step(i + 1, 0, False, False)
    step(pairs // 2 - 1, 1, False, True)


class Share:

    def __init__(self, members, groups):
        self.members, self.groups = members, groups

    def __contains__(self, g):
        return g in self.members

    def done(self, n, g):
        q, r = divmod(g, self.groups)
        return len(self.members) * (n + q + 1) + sum(m <= r for m in self.members)


class Kit:

    def __init__(self, nc, ctx):
        self.nc, self.ctx = nc, ctx
        self.used = []

    def sb(self, ctx, name, shape, dt):
        return ctx.enter_context(self.nc.sbuf_tensor(name, shape, dt))

    def ps(self, ctx, name, shape, dt=F32):
        return ctx.enter_context(self.nc.psum_tensor(name, shape, dt))

    def sem(self, ctx, name):
        self.used.append(ctx.enter_context(self.nc.semaphore(name)))
        return self.used[-1]

    def clear_semaphores(self):
        with self.nc.Block() as block:
            @block.sync
            def _(sp):
                for sem in self.used:
                    sp.sem_clear(sem)
        self.used = []


def quant_scalars(v, scal, raw_max, unit, scale, factor):
    def col(k):
        return scal[:, k:k + 1]
    v.drain()
    v.tensor_scalar(col(TMP0), raw_max, 1.0 if unit is None else col(unit), TINY, ALU.mult, ALU.max)
    v.drain()
    v.tensor_scalar(col(scale), col(TMP0), 1.0 / QMAX, None, ALU.mult)
    v.drain()
    v.reciprocal(col(TMP1), col(scale))
    v.drain()
    v.tensor_scalar(col(factor), col(TMP1), 1.0 if unit is None else col(unit), None, ALU.mult)
    v.drain()


def setup_phase(kit, w_in_t, w_out_t):
    nc = kit.nc
    with ExitStack() as ctx:
        wraw = kit.sb(ctx, "w_in_raw", [128, KC, 3 * D], F32)
        wint = kit.sb(ctx, "w_in_int16", [128, KC, 3 * D], I16)
        woraw = kit.sb(ctx, "w_out_raw", [128, 3, D], F32)
        woint = kit.sb(ctx, "w_out_int16", [128, 3, D], I16)
        wmax = kit.sb(ctx, "w_max", [128, 2], F32)
        gmax = kit.sb(ctx, "w_max_all", [128, 2], F32)
        zeroed = kit.sem(ctx, "setup_zeroed")
        loaded = kit.sem(ctx, "setup_loaded")
        wmax_ready = kit.sem(ctx, "wmax_ready")
        gmax_ready = kit.sem(ctx, "gmax_ready")
        ident_zero = kit.sem(ctx, "ident_zero")
        block = ctx.enter_context(nc.Block())

        @block.sync
        def _(sp):
            sp.wait_ge(zeroed, 2)
            sp.dma_start(wraw[0:KP], w_in_t.rearrange("(c p) e -> p c e", p=KP)).then_inc(loaded, 16)
            for j in range(4):
                src = w_out_t.rearrange("(c j d) o -> j d c o", c=3, j=4)[j]
                sp.dma_start(woraw[32 * j:32 * j + DH], src).then_inc(loaded, 16)

        @block.gpsimd
        def _(pool):
            nc.gpsimd.memset(kit.ident[:], 0.0).then_inc(ident_zero, 1)
            pool.wait_ge(ident_zero, 1)
            nc.gpsimd.affine_select(out=kit.ident[:], in_=kit.ident[:], compare_op=ALU.not_equal, fill=1.0,
                                    base=0, pattern=[[-1, 128]], channel_multiplier=1).then_inc(ident_zero, 1)
            nc.gpsimd.memset(kit.identb[:], 0.0).then_inc(ident_zero, 1)
            pool.wait_ge(ident_zero, 3)
            nc.gpsimd.affine_select(out=kit.identb[:], in_=kit.identb[:], compare_op=ALU.not_equal, fill=1.0,
                                    base=0, pattern=[[-1, 128]], channel_multiplier=1).then_inc(ident_zero, 1)
            pool.wait_ge(wmax_ready, 1)
            nc.gpsimd.partition_all_reduce(gmax[:], wmax[:], 128, RMAX).then_inc(gmax_ready, 1)
            pool.wait_ge(ident_zero, 4)

        @block.vector
        def _(v):
            nc.vector.memset(wraw[:], 0.0).then_inc(zeroed, 1)
            nc.vector.memset(woraw[:], 0.0).then_inc(zeroed, 1)
            v.wait_ge(loaded, 80)
            v.tensor_reduce(wmax[:, 0:1], wraw[:], AX.XY, ALU.max, apply_absolute_value=True)
            v.tensor_reduce(wmax[:, 1:2], woraw[:], AX.XY, ALU.max, apply_absolute_value=True).then_inc(wmax_ready, 1)
            v.wait_ge(gmax_ready, 1)
            quant_scalars(v, kit.scal, gmax[:, 0:1], None, S_W, TMP2)
            v.tensor_scalar(wint[:], wraw[:], kit.scal[:, TMP2:TMP2 + 1], None, ALU.mult)
            quant_scalars(v, kit.scal, gmax[:, 1:2], None, S_WO, TMP2)
            v.tensor_scalar(woint[:], woraw[:], kit.scal[:, TMP2:TMP2 + 1], None, ALU.mult)
            v.drain()
            v.tensor_copy(kit.w_in[:], wint[:])
            v.tensor_copy(kit.w_out[:], woint[:])


def tokenize_phase(kit, patches, txt, chan_w, h_d, qk_d, v_d, xt_d):
    nc = kit.nc
    with ExitStack() as ctx:
        xin = kit.sb(ctx, "patch_in", [QP, QT, CHAN * 256], F32)
        pooled = kit.sb(ctx, "pooled", [QP, QT, CHAN], F32)
        pooled_t = kit.sb(ctx, "pooled_t", [CHAN, QT * QP], F32)
        cw = kit.sb(ctx, "chan_weights", [CHAN, D], F32)
        w_in = kit.sb(ctx, "w_in_f32", [128, KC, 3 * D], F32)
        h = [kit.sb(ctx, f"h{s}", [HALF, 4, D], F32) for s in range(2)]
        xn = [kit.sb(ctx, f"xn{s}", [HALF, 4, D], F32) for s in range(2)]
        xt = [kit.sb(ctx, f"xt{s}", [KP, KC, PAIR], F32) for s in range(2)]
        qk = [kit.sb(ctx, f"qk{s}", [KP, 4, PAIR], F32) for s in range(2)]
        vv = [kit.sb(ctx, f"vv{s}", [HALF, 4, D], F32) for s in range(2)]
        stats = kit.sb(ctx, "stats", [HALF, 4, 6], F32)
        mv = kit.sb(ctx, "mv", [HALF, 4, 2], F32)
        ve = kit.sb(ctx, "ve", [HALF, 4], F32)
        sd = kit.sb(ctx, "sd", [HALF, 4], F32)
        r0 = kit.sb(ctx, "r0", [HALF, 4], F32)
        r1 = kit.sb(ctx, "r1", [HALF, 4], F32)
        rstd = kit.sb(ctx, "rstd", [HALF, 4], F32)
        mx = kit.sb(ctx, "mx", [128, 4, NPAIR], F32)
        mx4 = kit.sb(ctx, "mx4", [128, 4], F32)
        gmx = kit.sb(ctx, "gmx", [128, 4], F32)
        pt_ps = kit.ps(ctx, "pt_ps", [CHAN, 2, 512])
        h_ps = kit.ps(ctx, "h_ps", [HALF, 2, 512])
        xt_ps = kit.ps(ctx, "xt_ps", [KP, 2, 512])
        qv_ps = kit.ps(ctx, "qv_ps", [HALF, 2, 512])

        sem = lambda name: kit.sem(ctx, name)
        x_in = [sem(f"x_in{t}") for t in range(QT)]
        pooled_ready = sem("pooled_ready")
        pt_ready = sem("pt_ready")
        pt_copied = sem("pt_copied")
        w_loaded, w_ready = sem("w_loaded"), sem("w_ready")
        h_mixed = sem("h_mixed")
        h_copied = sem("h_copied")
        txt_in = [sem(f"txt_in{s}") for s in range(2)]
        var_ready, sd_ready = sem("var_ready"), sem("sd_ready")
        xn_ready = sem("xn_ready")
        xt_ready = sem("xt_ready")
        xt_copied = sem("xt_copied")
        qv_ready = sem("qv_ready")
        qv_copied = sem("qv_copied")
        maxed = sem("maxed")
        h_out, xt_out, qk_out, v_out = [[sem(f"{n}_out{s}") for s in range(2)] for n in ("h", "xt", "qk", "v")]
        mx_ready, gmx_ready = sem("mx_ready"), sem("gmx_ready")
        block = ctx.enter_context(nc.Block())

        patch_tiles = patches.rearrange("(q t p) x -> t q p x", t=QT, p=QP)
        txt_pairs = txt.rearrange("(i s m) t e -> s i t m e", s=2, m=2)
        rows = lambda a: a.rearrange("(i s m t) e -> s i t m e", s=2, m=4, t=HALF)
        cols = lambda a: a.rearrange("(m p) (i s t) -> s i p m t", p=KP, s=2, t=PAIR)

        @block.sync
        def _(sp):
            sp.dma_start(cw[:], chan_w).then_inc(w_loaded, 16)
            with sp.Fori(0, QUAD) as i:
                for t in range(QT):
                    sp.wait_ge(pooled_ready, QT * i + t + 1)
                    sp.dma_start(xin[:, t], patch_tiles[t][i]).then_inc(x_in[t], 16)

        @block.gpsimd
        def _(pool):
            pool.wait_ge(mx_ready, 1)
            nc.gpsimd.partition_all_reduce(gmx[:], mx4[:], 128, RMAX).then_inc(gmx_ready, 1)

        @block.vector
        def _(v):
            v.sem_inc(pooled_ready, QT)
            v.sem_inc(xn_ready, 2)
            v.sem_inc(maxed, 2)
            nc.vector.memset(mx[:], 0.0)
            v.tensor_copy(w_in[0:KP], kit.w_in[0:KP]).then_inc(w_ready, 1)

            def pool_tile(q, t):
                v.wait_ge(x_in[t], 16 * q + 16)
                if t == 0:
                    v.wait_ge(pt_ready, q + 1)
                v.tensor_reduce(pooled[:, t], xin[:, t].rearrange("p (c x) -> p c x", c=CHAN), AX.X, ALU.add)\
                    .then_inc(pooled_ready, 1)

            def norm_stats(i, s):
                v.wait_ge(h_copied, 2 * i + s + 2)
                v.wait_ge(txt_in[s], 16 * i + 16)
                for m in range(4):
                    v.bn_stats(stats[:, m], h[s][:, m])
                v.drain()
                for m in range(4):
                    v.bn_aggr(mv[:, m], stats[:, m])
                v.drain()
                v.tensor_scalar(ve[:], mv[:, :, 1], EPS, None, ALU.add).then_inc(var_ready, 1)

            def norm_rows(i, s):
                v.wait_ge(sd_ready, 2 * i + s + 1)
                v.reciprocal(r0[:], sd[:])
                v.drain()
                v.tensor_tensor(r1[:], r0[:], r0[:], ALU.mult)
                v.drain()
                v.tensor_tensor(r1[:], r1[:], ve[:], ALU.mult)
                v.drain()
                v.tensor_scalar(r1[:], r1[:], -0.5, 1.5, ALU.mult, ALU.add)
                v.drain()
                v.tensor_tensor(rstd[:], r0[:], r1[:], ALU.mult)
                v.drain()
                v.wait_ge(xt_ready, 2 * i + s + 1)
                for m in range(4):
                    ins = v.tensor_scalar(xn[s][:, m], h[s][:, m], mv[:, m, 0:1], rstd[:, m:m + 1],
                                          ALU.subtract, ALU.mult)
                ins.then_inc(xn_ready, 1)

            def maxima(i, s):
                def col(k, p):
                    return mx[0:p, k].rearrange("p (i s) -> p s i", s=2)[:, s, bass.ds(i, 1)]
                v.wait_ge(qv_copied, 6 * (2 * i + s) + 6 + 2)
                v.tensor_reduce(col(0, KP), qk[s][:, 0:2], AX.XY, ALU.max, apply_absolute_value=True)
                v.tensor_reduce(col(1, KP), qk[s][:, 2:4], AX.XY, ALU.max, apply_absolute_value=True)
                v.tensor_reduce(col(2, HALF), vv[s][:], AX.XY, ALU.max, apply_absolute_value=True)
                v.tensor_reduce(col(3, HALF), xn[s][:], AX.XY, ALU.max, apply_absolute_value=True).then_inc(maxed, 1)

            for t in range(QT):
                pool_tile(0, t)

            def turn(i, more):
                if more:
                    for t in range(3):
                        pool_tile(i + 1, t)
                norm_stats(i, 0)
                if more:
                    pool_tile(i + 1, 3)
                norm_rows(i, 0)
                if more:
                    pool_tile(i + 1, 4)
                    pool_tile(i + 1, 5)
                norm_stats(i, 1)
                if more:
                    pool_tile(i + 1, 6)
                norm_rows(i, 1)
                maxima(i, 0)
                maxima(i, 1)

            with v.Fori(0, QUAD - 1) as i:
                turn(i, True)
            turn(QUAD - 1, False)
            v.drain()
            v.tensor_reduce(mx4[:], mx[:], AX.X, ALU.max).then_inc(mx_ready, 1)
            v.wait_ge(gmx_ready, 1)
            for k, (unit, scale, factor) in enumerate([(S_W, S_Q, C_Q), (S_W, S_K, C_K), (S_W, S_V, C_V),
                                                       (None, S_X, C_X)]):
                quant_scalars(v, kit.scal, gmx[:, k:k + 1], unit, scale, factor)

        @block.tensor
        def _(pe):
            def transpose_pooled(q):
                pe.wait_ge(pt_copied, q + 1)
                for t in range(QT):
                    pe.wait_ge(pooled_ready, QT * q + t + 1 + QT)
                    mm = pe.transpose(pt_ps[:, t // 4, t % 4 * QP:t % 4 * QP + QP], pooled[:, t],
                                      kit.ident[0:QP, 0:QP])
                mm.then_inc(pt_ready, 1)

            def mix(i, s):
                pe.wait_ge(pt_copied, i + 2)
                pe.wait_ge(h_copied, 2 * i + s + 1)
                for m in range(4):
                    a = NPATCH * (2 * s + m // 2) + HALF * (m % 2)
                    k = REST if m % 2 else HALF
                    mm = pe.matmul(h_ps[0:k, m // 2, m % 2 * D:m % 2 * D + D], pooled_t[:, a:a + k], cw[:],
                                   start=True, stop=True)
                mm.then_inc(h_mixed, 1)

            def transpose_x(i, s):
                pe.wait_ge(xn_ready, 2 * i + s + 1 + 2)
                pe.wait_ge(xt_copied, 2 * i + s + 1)
                for m in range(4):
                    for c in range(KC):
                        mm = pe.transpose(xt_ps[:, c, m * HALF:m * HALF + HALF], xn[s][:, m, c * KP:c * KP + KP],
                                          kit.ident[0:HALF, 0:HALF])
                mm.then_inc(xt_ready, 1)

            def project(i, s):
                use = 6 * (2 * i + s)
                pe.wait_ge(xt_copied, 2 * i + s + 1 + 1)
                for m in range(4):
                    pe.wait_ge(qv_copied, use + m + 1)
                    for c in range(KC):
                        mm = pe.matmul(qv_ps[0:KP, m % 2, 0:PAIR], w_in[0:KP, c, m * KP:m * KP + KP], xt[s][:, c],
                                       start=(c == 0), stop=(c == KC - 1))
                    mm.then_inc(qv_ready, 1)
                for m in range(4):
                    if m % 2 == 0:
                        pe.wait_ge(qv_copied, use + 4 + m // 2 + 1)
                    for c in range(KC):
                        mm = pe.matmul(qv_ps[:, m // 2, m % 2 * D:m % 2 * D + D],
                                       xt[s][:, c, m * HALF:m * HALF + HALF],
                                       w_in[0:KP, c, 2 * D:3 * D], start=(c == 0), stop=(c == KC - 1))
                    if m % 2:
                        mm.then_inc(qv_ready, 1)

            def turn(i, more):
                mix(i, 0)
                transpose_x(i, 0)
                project(i, 0)
                mix(i, 1)
                if more:
                    transpose_pooled(i + 1)
                transpose_x(i, 1)
                project(i, 1)

            pe.sem_inc(pt_ready, 1)
            pe.sem_inc(xt_ready, 2)
            pe.wait_ge(w_loaded, 16)
            pe.wait_ge(w_ready, 1)
            transpose_pooled(0)
            with pe.Fori(0, QUAD - 1) as i:
                turn(i, True)
            turn(QUAD - 1, False)

        @block.scalar
        def _(act):
            def copy_pooled(q):
                act.wait_ge(pt_ready, q + 1 + 1)
                act.copy(pooled_t[:, 0:4 * QP], pt_ps[:, 0, 0:4 * QP])
                act.copy(pooled_t[:, 4 * QP:], pt_ps[:, 1, 0:3 * QP]).then_inc(pt_copied, 1)

            def copy_h(i, s):
                n = 2 * i + s
                act.wait_ge(h_out[s], 16 * i + 16)
                act.wait_ge(xn_ready, n + 1)
                act.dma_start(h[s][REST:HALF, 1:4:2], txt_pairs[s][i]).then_inc(txt_in[s], 16)
                act.wait_ge(h_mixed, n + 1)
                hp = h_ps[:, :, 0:2 * D].rearrange("p b (m e) -> p b m e", m=2)
                act.copy(h[s][:, 0:4:2], hp[:, :, 0])
                act.copy(h[s][0:REST, 1:4:2], hp[0:REST, :, 1]).then_inc(h_copied, 1)

            def store_h(i, s):
                act.wait_ge(h_copied, 2 * i + s + 2)
                act.wait_ge(txt_in[s], 16 * i + 16)
                act.dma_start(rows(h_d)[s][i], h[s][:]).then_inc(h_out[s], 16)

            def root(i, s):
                act.wait_ge(var_ready, 2 * i + s + 1)
                act.activation(sd[:], ve[:], ACT.Sqrt).then_inc(sd_ready, 1)

            def copy_xt(i, s):
                act.wait_ge(xt_ready, 2 * i + s + 1 + 2)
                act.wait_ge(xt_out[s], 16 * i + 16)
                act.copy(xt[s][:, 0], xt_ps[:, 0, 0:PAIR])
                act.copy(xt[s][:, 1], xt_ps[:, 1, 0:PAIR]).then_inc(xt_copied, 1)
                act.wait_ge(xt_copied, 2 * i + s + 2)
                act.dma_start(cols(xt_d)[s][i], xt[s][:]).then_inc(xt_out[s], 16)

            def copy_qkv(i, s):
                n = 2 * i + s
                act.wait_ge(maxed, n + 1)
                act.wait_ge(qk_out[s], 16 * i + 16)
                for m in range(4):
                    act.wait_ge(qv_ready, 6 * n + m + 1)
                    act.copy(qk[s][:, m], qv_ps[0:KP, m % 2, 0:PAIR]).then_inc(qv_copied, 1)
                act.wait_ge(qv_copied, 6 * n + 4 + 2)
                act.dma_start(cols(qk_d)[s][i], qk[s][:]).then_inc(qk_out[s], 16)
                act.wait_ge(v_out[s], 16 * i + 16)
                for m in range(2):
                    act.wait_ge(qv_ready, 6 * n + 4 + m + 1)
                    act.copy(vv[s][:, 2 * m:2 * m + 2].rearrange("p m e -> p (m e)"), qv_ps[:, m, 0:2 * D])\
                        .then_inc(qv_copied, 1)
                act.wait_ge(qv_copied, 6 * n + 6 + 2)
                act.dma_start(rows(v_d)[s][i], vv[s][:]).then_inc(v_out[s], 16)

            def turn(i, more):
                copy_h(i, 0)
                root(i, 0)
                store_h(i, 0)
                copy_xt(i, 0)
                copy_qkv(i, 0)
                copy_h(i, 1)
                root(i, 1)
                store_h(i, 1)
                if more:
                    copy_pooled(i + 1)
                copy_xt(i, 1)
                copy_qkv(i, 1)

            for o in (h_out, xt_out, qk_out, v_out):
                for s in range(2):
                    act.sem_inc(o[s], 16)
            act.sem_inc(pt_copied, 1)
            act.sem_inc(h_copied, 1)
            act.sem_inc(xt_copied, 1)
            act.sem_inc(qv_copied, 2)
            copy_pooled(0)
            with act.Fori(0, QUAD - 1) as i:
                turn(i, True)
            turn(QUAD - 1, False)
            for o in (h_out, xt_out, qk_out, v_out):
                for s in range(2):
                    act.wait_ge(o[s], 16 * (QUAD + 1))


def score_range_phase(kit, qk_d, v_d, qb_d, kb_d, vb_d, mneg_d):
    nc = kit.nc
    W3 = 3 * PAIR
    with ExitStack() as ctx:
        qf = [kit.sb(ctx, f"qf{s}", [128, 3, PAIR], F32) for s in range(2)]
        kf = [kit.sb(ctx, f"kf{s}", [128, 3, PAIR], F32) for s in range(2)]
        vf = [kit.sb(ctx, f"vf{s}", [HALF, 4, D], F32) for s in range(2)]
        q16 = kit.sb(ctx, "q16", [128, 3, PAIR], I16)
        k16 = kit.sb(ctx, "k16", [128, 3, PAIR], I16)
        v16 = kit.sb(ctx, "v16", [HALF, 4, D], I16)
        qb = [kit.sb(ctx, f"qb{s}", [128, 3, PAIR], BF16) for s in range(2)]
        kb = [kit.sb(ctx, f"kb{s}", [128, 3, PAIR], BF16) for s in range(2)]
        vb = [kit.sb(ctx, f"vb{s}", [HALF, 4, HEADS, 32], BF16) for s in range(2)]
        rowmax = kit.sb(ctx, "rowmax", [HALF, NPAIR, 3, 4, 2, 2], F32)
        absmax = kit.sb(ctx, "absmax", [HALF, NPAIR, 3, 4, 2, 2], F32)
        amax1 = kit.sb(ctx, "amax1", [128, 1], F32)
        gamax = kit.sb(ctx, "gamax", [128, 1], F32)
        xb = kit.sb(ctx, "xb", [128, 3], BF16)
        m16 = kit.sb(ctx, "m16", [HALF, NPAIR * 48], I16)
        mb = kit.sb(ctx, "mb", [HALF, NPAIR * 48], BF16)
        mt = kit.sb(ctx, "mt", [48, NPAIR, HALF], BF16)
        xrow = kit.sb(ctx, "xrow", [NPAIR, 3, W3], BF16)
        sem = lambda name: kit.sem(ctx, name)
        qk_in, v_in, qkv_out = [[sem(f"{n}{s}") for s in range(2)] for n in ("qk_in", "v_in", "qkv_out")]
        zeroed, pool_turn = sem("zeroed"), sem("pool_turn")
        rounded = sem("rounded")
        cast = sem("cast")
        scored = sem("scored")
        s_ready = sem("s_ready")
        s_used = sem("s_used")
        amax_ready, gamax_ready, mb_ready, mt_psum, mt_ready, mt_out, pads_out, xrow_ready = [sem(n) for n in (
            "amax_ready", "gamax_ready", "mb_ready", "mt_psum", "mt_ready", "mt_out", "pads_out", "xrow_ready")]
        with ExitStack() as pctx:
            s_ps = [kit.ps(pctx, f"s_ps{b}", [HALF, 4, 512]) for b in range(2)]
            block = pctx.enter_context(nc.Block())

            heads = qk_d.rearrange("(w c j d) (i s t) -> w j s i d c t", w=2, c=3, j=4, s=2, t=PAIR)
            vrows = v_d.rearrange("(i s m t) e -> s i t m e", s=2, m=4, t=HALF)
            by_pair = lambda a: a.rearrange("(i s) p x -> s i p x", s=2)

            @block.sync
            def _(sp):
                def load(i, s):
                    sp.wait_ge(rounded, 3 * (2 * i + s) + 3)
                    for w, dst in enumerate((qf, kf)):
                        for j in range(4):
                            sp.dma_start(dst[s][32 * j:32 * j + DH], heads[w, j, s][i]).then_inc(qk_in[s], 16)
                    sp.dma_start(vf[s][:], vrows[s][i]).then_inc(v_in[s], 16)

                def store(i, s):
                    sp.wait_ge(cast, 3 * (2 * i + s) + 3 + 3)
                    sp.dma_start(by_pair(qb_d)[s][i], qb[s][:].rearrange("p c t -> p (c t)")).then_inc(qkv_out[s], 16)
                    sp.dma_start(by_pair(kb_d)[s][i], kb[s][:].rearrange("p c t -> p (c t)")).then_inc(qkv_out[s], 16)
                    sp.dma_start(by_pair(vb_d)[s][i], vb[s][:].rearrange("p m h d -> p (m h d)"))\
                        .then_inc(qkv_out[s], 16)

                for s in range(2):
                    sp.sem_inc(qkv_out[s], 48)
                sp.wait_ge(zeroed, 4)
                load(0, 0)
                with sp.Fori(0, NPAIR // 2 - 1) as i:
                    load(i, 1)
                    store(i, 0)
                    load(i + 1, 0)
                    store(i, 1)
                load(NPAIR // 2 - 1, 1)
                store(NPAIR // 2 - 1, 0)
                store(NPAIR // 2 - 1, 1)
                for s in range(2):
                    sp.wait_ge(qkv_out[s], 48 * (NPAIR // 2 + 1))

            @block.scalar
            def _(act):
                act.sem_inc(rounded, 6)
                sc = lambda k, p=128: kit.scal[0:p, k:k + 1]
                with act.Fori(0, NPAIR // 2) as i:
                    for s in range(2):
                        n = 2 * i + s
                        act.wait_ge(qk_in[s], 128 * i + 128)
                        act.wait_ge(cast, 3 * n + 1)
                        act.activation(q16[:], qf[s][:], ACT.Copy, scale=sc(C_Q)).then_inc(rounded, 1)
                        act.wait_ge(cast, 3 * n + 2)
                        act.activation(k16[:], kf[s][:], ACT.Copy, scale=sc(C_K)).then_inc(rounded, 1)
                        act.wait_ge(v_in[s], 16 * i + 16)
                        act.wait_ge(cast, 3 * n + 3)
                        act.activation(v16[:], vf[s][:], ACT.Copy, scale=sc(C_V, HALF)).then_inc(rounded, 1)

            @block.gpsimd
            def _(pool):
                pool.sem_inc(cast, 3)
                pool.wait_ge(zeroed, 6)
                with pool.Fori(0, NPAIR // 2) as i:
                    for s in range(2):
                        n = 2 * i + s
                        pool.wait_ge(scored, n + 1)
                        pool.wait_ge(qkv_out[s], 48 * i + 48)
                        pool.wait_ge(rounded, 3 * n + 1 + 6)
                        pool.sem_inc(pool_turn, 1)
                        nc.gpsimd.tensor_copy(qb[s][:], q16[:]).then_inc(cast, 1)
                        pool.wait_ge(rounded, 3 * n + 2 + 6)
                        pool.sem_inc(pool_turn, 1)
                        nc.gpsimd.tensor_copy(kb[s][:], k16[:]).then_inc(cast, 1)
                        pool.wait_ge(rounded, 3 * n + 3 + 6)
                        pool.sem_inc(pool_turn, 1)
                        nc.gpsimd.tensor_copy(vb[s][:, :, :, 0:DH],
                                              v16[:].rearrange("p m (h d) -> p m h d", h=HEADS)).then_inc(cast, 1)

            @block.tensor
            def _(pe):
                pe.sem_inc(scored, 2)
                with pe.Fori(0, NPAIR // 2) as i:
                    for s in range(2):
                        n = 2 * i + s
                        pe.wait_ge(cast, 3 * n + 2 + 3)
                        for g in range(6):
                            m, c = g // 3, g % 3
                            pe.wait_ge(s_used, 6 * n + g + 1)
                            for half in range(2):
                                for j in range(4):
                                    r = slice(32 * j, 32 * j + DH)
                                    a = m * SEQ + half * HALF
                                    mm = pe.matmul(s_ps[g % 2][:, j, half * SEQ:half * SEQ + SEQ], qb[s][r, c, a:a + HALF],
                                                   kb[s][r, c, m * SEQ:m * SEQ + SEQ], start=True, stop=True)
                            mm.then_inc(s_ready, 1)
                        pe.wait_ge(s_ready, 6 * n + 6)
                        pe.sem_inc(scored, 1)

            @block.vector
            def _(v):
                for t in (qf, kf, vb):
                    for s in range(2):
                        nc.vector.memset(t[s][:], 0.0).then_inc(zeroed, 1)
                v.sem_inc(s_used, 2)
                with v.Fori(0, NPAIR // 2) as i:
                    for s in range(2):
                        for g in range(6):
                            m, c = g // 3, g % 3
                            v.wait_ge(s_ready, 6 * (2 * i + s) + g + 1)
                            src = s_ps[g % 2][:, :, 0:PAIR].rearrange("p j (h k) -> p j h k", h=2)
                            out = [t[:].rearrange("p (i s) c j m h -> p s c m i j h", s=2)[:, s, c, m][:, bass.ds(i, 1)]
                                   for t in (rowmax, absmax)]
                            v.tensor_reduce(out[0], src, AX.X, ALU.max)
                            v.tensor_reduce(out[1], src, AX.X, ALU.max, apply_absolute_value=True).then_inc(s_used, 1)

        with ExitStack() as pctx:
            mt_ps = [kit.ps(pctx, f"mt_ps{b}", [48, 1024], BF16) for b in range(4)]
            block = pctx.enter_context(nc.Block())

            @block.gpsimd
            def _(pool):
                pool.wait_ge(amax_ready, 1)
                nc.gpsimd.partition_all_reduce(gamax[:], amax1[:], 128, RMAX).then_inc(gamax_ready, 1)

            @block.vector
            def _(v):
                sc = lambda k, p=128: kit.scal[0:p, k:k + 1]
                nc.vector.memset(amax1[:], 0.0)
                nc.vector.memset(xrow[:], 1.0)
                v.drain()
                v.tensor_reduce(amax1[0:HALF], absmax[:].rearrange("p n c j m h -> p (n c j m h)"), AX.X, ALU.max)\
                    .then_inc(amax_ready, 1)
                v.tensor_tensor(sc(U_S), sc(S_Q), sc(S_K), ALU.mult)
                v.drain()
                v.tensor_scalar(sc(U_S), sc(U_S), 0.25, None, ALU.mult)
                v.wait_ge(gamax_ready, 1)
                quant_scalars(v, kit.scal, gamax[:], U_S, S_S, C_S)
                v.tensor_scalar(sc(TMP0), sc(C_S), -1.0, None, ALU.mult)
                v.reciprocal(sc(TMP1), sc(C_S))
                v.drain()
                v.tensor_scalar(m16[:], rowmax[:].rearrange("p n c j m h -> p (n c j m h)"), sc(TMP0, HALF), None,
                                ALU.mult)
                v.drain()
                v.tensor_copy(mb[:], m16[:]).then_inc(mb_ready, 1)
                for k in range(3):
                    v.drain()
                    v.tensor_copy(xb[:, k:k + 1], sc(TMP1))
                    v.drain()
                    v.tensor_copy(sc(TMP2), xb[:, k:k + 1])
                    v.drain()
                    v.tensor_tensor(sc(TMP1), sc(TMP1), sc(TMP2), ALU.subtract)
                    v.tensor_scalar(xrow[:, k], xrow[:, k], sc(TMP2, NPAIR), None, ALU.mult).then_inc(xrow_ready, 1)
                for b in range(4):
                    v.wait_ge(mt_psum, b + 1)
                    v.tensor_copy(mt[:, 8 * b:8 * b + 8].rearrange("p n t -> p (n t)"), mt_ps[b][:, 0:8 * HALF])\
                        .then_inc(mt_ready, 1)

            @block.tensor
            def _(pe):
                pe.wait_ge(mb_ready, 1)
                for n in range(NPAIR):
                    mm = pe.transpose(mt_ps[n // 8][:, n % 8 * HALF:n % 8 * HALF + HALF], mb[:, 48 * n:48 * n + 48],
                                      kit.identb[0:HALF, 0:HALF])
                    if n % 8 == 7:
                        mm.then_inc(mt_psum, 1)

            @block.sync
            def _(sp):
                sp.wait_ge(mt_ready, 4)
                sp.dma_start(mneg_d.rearrange("n a t -> a n t"), mt[:]).then_inc(mt_out, 16)
                sp.wait_ge(mt_out, 16)
                for j in range(4):
                    src = mneg_d.rearrange("n (c j a) t -> j n c (a t)", c=3, j=4)[j]
                    for r in range(3):
                        sp.dma_start(qb_d[:, 32 * j + DH + r].rearrange("n (c t) -> n c t", c=3), src)\
                            .then_inc(pads_out, 16)
                sp.wait_ge(xrow_ready, 3)
                for j in range(4):
                    sp.dma_start(kb_d[:, 32 * j + DH:32 * j + DH + 3], xrow[:]).then_inc(pads_out, 16)
                sp.wait_ge(pads_out, 16 * 16)


def row_sum_phase(kit, qb_d, kb_d, r_d):
    nc = kit.nc
    GROUPS = 6
    by_act, by_dve = Share((0, 1, 3, 4), GROUPS), Share((2, 5), GROUPS)
    with ExitStack() as ctx:
        qb = [kit.sb(ctx, f"rs_qb{s}", [128, 3, PAIR], BF16) for s in range(2)]
        kb = [kit.sb(ctx, f"rs_kb{s}", [128, 3, PAIR], BF16) for s in range(2)]
        t16 = [kit.sb(ctx, f"rs_t{b}", [HALF, 4, PAIR], I16) for b in range(3)]
        e32 = [kit.sb(ctx, f"rs_e{b}", [HALF, 4, PAIR], F32) for b in range(2)]
        rowsum = kit.sb(ctx, "rowsum", [HALF, NPAIR, 3, 4, 2, 2], F32)
        rinv = kit.sb(ctx, "rinv", [HALF, NPAIR * 48], F32)
        pmax1 = kit.sb(ctx, "pmax1", [128, 1], F32)
        pmax = kit.sb(ctx, "pmax", [128, 1], F32)
        rt = kit.sb(ctx, "rt", [48, NPAIR, HALF], F32)
        sem = lambda name: kit.sem(ctx, name)
        qk_in = [sem(f"rs_qk_in{s}") for s in range(2)]
        scored = sem("rs_scored")
        s_ready = sem("rs_s_ready")
        act_rounded = sem("act_rounded")
        dve_rounded = sem("dve_rounded")
        exped = sem("exped")
        summed = sem("summed")
        pmax_ready, pmax_all, r_ready, rt_psum, rt_ready, rt_out = [sem(n) for n in (
            "pmax_ready", "pmax_all", "r_ready", "rt_psum", "rt_ready", "rt_out")]

        def wait_rounded(eng, n, g):
            share, done = (by_act, act_rounded) if g % GROUPS in by_act else (by_dve, dve_rounded)
            eng.wait_ge(done, share.done(n, g))

        with ExitStack() as pctx:
            s_ps = [kit.ps(pctx, f"rs_s_ps{b}", [HALF, 4, 512]) for b in range(2)]
            block = pctx.enter_context(nc.Block())
            by_pair = lambda a: a.rearrange("(i s) p x -> s i p x", s=2)

            @block.sync
            def _(sp):
                with sp.Fori(0, NPAIR // 2) as i:
                    for s in range(2):
                        sp.wait_ge(scored, 2 * i + s + 1)
                        sp.dma_start(qb[s][:].rearrange("p c t -> p (c t)"), by_pair(qb_d)[s][i]).then_inc(qk_in[s], 16)
                        sp.dma_start(kb[s][:].rearrange("p c t -> p (c t)"), by_pair(kb_d)[s][i]).then_inc(qk_in[s], 16)

            @block.tensor
            def _(pe):
                pe.sem_inc(scored, 2)
                with pe.Fori(0, NPAIR // 2) as i:
                    for s in range(2):
                        n = 2 * i + s
                        pe.wait_ge(qk_in[s], 32 * i + 32)
                        for g in range(GROUPS):
                            m, c = g // 3, g % 3
                            wait_rounded(pe, n, g - 2)
                            for half in range(2):
                                for j in range(4):
                                    r = slice(32 * j, 32 * j + DH + 3)
                                    a = m * SEQ + half * HALF
                                    mm = pe.matmul(s_ps[g % 2][:, j, half * SEQ:half * SEQ + SEQ], qb[s][r, c, a:a + HALF],
                                                   kb[s][r, c, m * SEQ:m * SEQ + SEQ], start=True, stop=True)
                            mm.then_inc(s_ready, 1)
                        pe.wait_ge(s_ready, GROUPS * n + GROUPS)
                        pe.sem_inc(scored, 1)

            @block.scalar
            def _(act):
                def round_scores(i, s, g):
                    n = 2 * i + s
                    act.wait_ge(s_ready, GROUPS * n + g + 1)
                    act.wait_ge(exped, GROUPS * n + g + 1)
                    act.activation(t16[g % 3][:], s_ps[g % 2][:, :, 0:PAIR], ACT.Copy, scale=kit.scal[0:HALF, C_S:C_S + 1])\
                        .then_inc(act_rounded, 1)

                def step(i, s, first, last):
                    n = 2 * i + s
                    for g in range(GROUPS):
                        i2, s2, g2 = sliding(i, s, g + 1, GROUPS)
                        if g2 in by_act and not (last and g + 1 == GROUPS):
                            round_scores(i2, s2, g2)
                        wait_rounded(act, n, g)
                        act.wait_ge(summed, GROUPS * n + g + 1)
                        act.activation(e32[g % 2][:], t16[g % 3][:], ACT.Exp, scale=kit.scal[0:HALF, S_S:S_S + 1])\
                            .then_inc(exped, 1)

                act.sem_inc(act_rounded, len(by_act.members))
                act.sem_inc(exped, 3)
                round_scores(0, 0, 0)
                turns(act, NPAIR, step)

            @block.vector
            def _(v):
                def round_scores(i, s, g):
                    n = 2 * i + s
                    v.wait_ge(s_ready, GROUPS * n + g + 1)
                    v.wait_ge(exped, GROUPS * n + g + 1)
                    v.tensor_scalar(t16[g % 3][:], s_ps[g % 2][:, :, 0:PAIR], kit.scal[0:HALF, C_S:C_S + 1], None,
                                    ALU.mult).then_inc(dve_rounded, 1)

                def step(i, s, first, last):
                    for g in range(GROUPS):
                        i2, s2, g2 = sliding(i, s, g + 1, GROUPS)
                        if g2 in by_dve and not (last and g + 1 == GROUPS):
                            round_scores(i2, s2, g2)
                        m, c = g // 3, g % 3
                        v.wait_ge(exped, GROUPS * (2 * i + s) + g + 1 + 3)
                        out = rowsum[:].rearrange("p (i s) c j m h -> p s c m i j h", s=2)[:, s, c, m][:, bass.ds(i, 1)]
                        v.tensor_reduce(out, e32[g % 2][:].rearrange("p j (h k) -> p j h k", h=2), AX.X, ALU.add)\
                            .then_inc(summed, 1)

                v.sem_inc(dve_rounded, len(by_dve.members))
                v.sem_inc(summed, 2)
                turns(v, NPAIR, step)

        with ExitStack() as pctx:
            rt_ps = [kit.ps(pctx, f"rt_ps{b}", [48, 512]) for b in range(8)]
            block = pctx.enter_context(nc.Block())

            @block.gpsimd
            def _(pool):
                pool.wait_ge(pmax_ready, 1)
                nc.gpsimd.partition_all_reduce(pmax[:], pmax1[:], 128, RMAX).then_inc(pmax_all, 1)

            @block.vector
            def _(v):
                sc = lambda k, p=128: kit.scal[0:p, k:k + 1]
                nc.vector.memset(pmax1[:], 0.0)
                v.reciprocal(rinv[:], rowsum[:].rearrange("p n c j m h -> p (n c j m h)"))
                v.drain()
                v.tensor_reduce(pmax1[0:HALF], rinv[:], AX.X, ALU.max).then_inc(pmax_ready, 1)
                v.wait_ge(pmax_all, 1)
                quant_scalars(v, kit.scal, pmax[:], None, U_CTX, C_A)
                v.tensor_tensor(sc(U_CTX), sc(U_CTX), sc(S_V), ALU.mult)
                v.tensor_scalar(rinv[:], rinv[:], sc(C_A, HALF), None, ALU.mult).then_inc(r_ready, 1)
                for b in range(8):
                    v.wait_ge(rt_psum, b + 1)
                    v.tensor_copy(rt[:, 4 * b:4 * b + 4].rearrange("p n t -> p (n t)"), rt_ps[b][:, 0:4 * HALF])\
                        .then_inc(rt_ready, 1)

            @block.tensor
            def _(pe):
                pe.wait_ge(r_ready, 1)
                for n in range(NPAIR):
                    mm = pe.transpose(rt_ps[n // 4][:, n % 4 * HALF:n % 4 * HALF + HALF], rinv[:, 48 * n:48 * n + 48],
                                      kit.ident[0:HALF, 0:HALF])
                    if n % 4 == 3:
                        mm.then_inc(rt_psum, 1)

            @block.sync
            def _(sp):
                sp.wait_ge(rt_ready, 8)
                sp.dma_start(r_d.rearrange("n (a t) -> a n t", t=HALF), rt[:]).then_inc(rt_out, 16)
                sp.wait_ge(rt_out, 16)


def context_phase(kit, qb_d, kb_d, vb_d, r_d, ctx_d):
    nc = kit.nc
    GROUPS = 8
    by_act, by_dve = Share((0, 1, 2, 4, 5, 6), GROUPS), Share((3, 7), GROUPS)
    with ExitStack() as ctx:
        qb = [kit.sb(ctx, f"cx_qb{s}", [128, 3, PAIR], BF16) for s in range(2)]
        kb = [kit.sb(ctx, f"cx_kb{s}", [128, 3, PAIR], BF16) for s in range(2)]
        vb = [kit.sb(ctx, f"cx_vb{s}", [HALF, 4, HEADS, 32], BF16) for s in range(2)]
        rb = [kit.sb(ctx, f"cx_r{s}", [128, HEADS, 2, SEQ], F32) for s in range(2)]
        t16 = [kit.sb(ctx, f"cx_t{b}", [HALF, 3, 2, SEQ], I16) for b in range(4)]
        e32 = [kit.sb(ctx, f"cx_e{b}", [HALF, 3, 2, SEQ], F32) for b in range(2)]
        a16 = [kit.sb(ctx, f"cx_a16{b}", [HALF, 3, 2, SEQ], I16) for b in range(2)]
        ab = [kit.sb(ctx, f"cx_ab{b}", [HALF, 3, 2, SEQ], BF16) for b in range(2)]
        cx = [kit.sb(ctx, f"cx_out{s}", [128, 3, 2, SEQ], F32) for s in range(2)]
        cmax = kit.sb(ctx, "cmax", [128, NPAIR], F32)
        cmax1 = kit.sb(ctx, "cmax1", [128, 1], F32)
        cmaxg = kit.sb(ctx, "cmaxg", [128, 1], F32)
        s_ps = [kit.ps(ctx, f"cx_s_ps{b}", [HALF, 3, 512]) for b in range(2)]
        c_ps = [kit.ps(ctx, f"cx_c_ps{b}", [128, 512]) for b in range(2)]
        sem = lambda name: kit.sem(ctx, name)
        qkv_in = [sem(f"cx_in{s}") for s in range(2)]
        cx_out = [sem(f"cx_stored{s}") for s in range(2)]
        s_ready = sem("cx_s_ready")
        act_rounded, dve_rounded = sem("cx_act_rounded"), sem("cx_dve_rounded")
        sp_turn = sem("sp_turn")
        exped = sem("cx_exped")
        weighted = sem("cx_weighted")
        cast = sem("cx_cast")
        applied = sem("cx_applied")
        c_copied = sem("cx_c_copied")
        measured = sem("cx_measured")
        cmax_ready, cmaxg_ready = sem("cmax_ready"), sem("cmaxg_ready")
        block = ctx.enter_context(nc.Block())
        by_pair = lambda a: a.rearrange("(i s) p x -> s i p x", s=2)
        PAIRG = GROUPS + 2

        def wait_rounded(eng, n, g):
            share, done = (by_act, act_rounded) if g % GROUPS in by_act else (by_dve, dve_rounded)
            eng.wait_ge(done, share.done(n, g))

        @block.sync
        def _(sp):
            def load(i, s):
                n = 2 * i + s
                sp.wait_ge(applied, GROUPS * (n - 2) + GROUPS + PAIRG)
                sp.wait_ge(weighted, GROUPS * (n - 2) + GROUPS + PAIRG)
                sp.sem_inc(sp_turn, 1)
                sp.dma_start(qb[s][:].rearrange("p c t -> p (c t)"), by_pair(qb_d)[s][i]).then_inc(qkv_in[s], 16)
                sp.dma_start(kb[s][:].rearrange("p c t -> p (c t)"), by_pair(kb_d)[s][i]).then_inc(qkv_in[s], 16)
                sp.dma_start(vb[s][:].rearrange("p m h d -> p (m h d)"), by_pair(vb_d)[s][i]).then_inc(qkv_in[s], 16)
                row = r_d.rearrange("(i s) x -> s i x", s=2)[s][bass.ds(i, 1)]
                sp.dma_start(rb[s][:].rearrange("p h m q -> p (h m q)"), row.to_broadcast([128, HEADS * PAIR]))\
                    .then_inc(qkv_in[s], 16)

            def store(i, s):
                sp.wait_ge(c_copied, 6 * (2 * i + s) + 6 + 2)
                sp.sem_inc(sp_turn, 1)
                sp.dma_start(by_pair(ctx_d)[s][i], cx[s][:].rearrange("p c m q -> p (c m q)")).then_inc(cx_out[s], 16)

            for s in range(2):
                sp.sem_inc(cx_out[s], 16)
            load(0, 0)
            with sp.Fori(0, NPAIR // 2 - 1) as i:
                load(i, 1)
                store(i, 0)
                load(i + 1, 0)
                store(i, 1)
            load(NPAIR // 2 - 1, 1)
            store(NPAIR // 2 - 1, 0)
            store(NPAIR // 2 - 1, 1)
            for s in range(2):
                sp.wait_ge(cx_out[s], 16 * (NPAIR // 2 + 1))

        @block.tensor
        def _(pe):
            def scores(i, s, g):
                n = 2 * i + s
                if g == 0:
                    pe.wait_ge(qkv_in[s], 64 * i + 64)
                m = g // 4
                wait_rounded(pe, n, g - 2)
                for half in range(2):
                    for b in range(3):
                        c, j = divmod(3 * (g % 4) + b, 4)
                        r = slice(32 * j, 32 * j + DH + 3)
                        a = m * SEQ + half * HALF
                        mm = pe.matmul(s_ps[g % 2][:, b, half * SEQ:half * SEQ + SEQ], kb[s][r, c, a:a + HALF],
                                       qb[s][r, c, m * SEQ:m * SEQ + SEQ], start=True, stop=True)
                mm.then_inc(s_ready, 1)

            def apply(i, s, g):
                n = 2 * i + s
                m = g // 4
                pe.wait_ge(cast, GROUPS * n + g + 1 + 2)
                for b in range(3):
                    head = 3 * (g % 4) + b
                    c, j = divmod(head, 4)
                    if j == 0:
                        pe.wait_ge(c_copied, 6 * n + 3 * m + c + 1)
                    for half in range(2):
                        mm = pe.matmul(c_ps[(3 * m + c) % 2][32 * j:32 * j + 32, 0:SEQ], vb[s][:, 2 * m + half, head],
                                       ab[g % 2][:, b, half], start=(half == 0), stop=(half == 1))
                mm.then_inc(applied, 1)

            def step(i, s, first, last):
                for g in range(GROUPS):
                    if not (last and g + 2 >= GROUPS):
                        scores(*sliding(i, s, g + 2, GROUPS))
                    apply(i, s, g)

            pe.sem_inc(applied, PAIRG)
            scores(0, 0, 0)
            scores(0, 0, 1)
            turns(pe, NPAIR, step)

        @block.scalar
        def _(act):
            def round_scores(i, s, g):
                act.wait_ge(s_ready, GROUPS * (2 * i + s) + g + 1)
                act.wait_ge(exped, GROUPS * (2 * i + s) + g + 1)
                act.activation(t16[g % 4][:].rearrange("p b h q -> p b (h q)"), s_ps[g % 2][:, :, 0:PAIR], ACT.Copy,
                               scale=kit.scal[0:HALF, C_S:C_S + 1]).then_inc(act_rounded, 1)

            def copy_chunk(n, s, chunk):
                m, c = divmod(chunk, 3)
                act.wait_ge(applied, GROUPS * n + 4 * m + c + 2 + PAIRG)
                act.copy(cx[s][:, c, m], c_ps[chunk % 2][:, 0:SEQ]).then_inc(c_copied, 1)

            def step(i, s, first, last):
                n = 2 * i + s
                for g in range(GROUPS):
                    i2, s2, g2 = sliding(i, s, g + 1, GROUPS)
                    if g2 in by_act and not (last and g + 1 == GROUPS):
                        round_scores(i2, s2, g2)
                    wait_rounded(act, n, g)
                    act.wait_ge(weighted, GROUPS * n + g - 2 + 1 + PAIRG)
                    act.activation(e32[g % 2][:], t16[g % 4][:], ACT.Exp, scale=kit.scal[0:HALF, S_S:S_S + 1])\
                        .then_inc(exped, 1)
                    if g == 1 and not first:
                        copy_chunk(n - 1, 1 - s, 5)
                    if g == 3:
                        act.wait_ge(cx_out[s], 16 * i + 16)
                        act.wait_ge(measured, n + 1)
                    if g in (3, 4, 5, 7):
                        copy_chunk(n, s, (3, 4, 5, 7).index(g))
                    if g == 7:
                        copy_chunk(n, s, 4)

            act.sem_inc(act_rounded, len(by_act.members))
            act.sem_inc(exped, 4)
            act.sem_inc(c_copied, 2)
            round_scores(0, 0, 0)
            turns(act, NPAIR, step)
            copy_chunk(NPAIR - 1, 1, 5)

        @block.vector
        def _(v):
            def round_scores(i, s, g):
                n = 2 * i + s
                v.wait_ge(s_ready, GROUPS * n + g + 1)
                v.wait_ge(exped, GROUPS * n + g + 1)
                v.tensor_scalar(t16[g % 4][:].rearrange("p b h q -> p b (h q)"), s_ps[g % 2][:, :, 0:PAIR],
                                kit.scal[0:HALF, C_S:C_S + 1], None, ALU.mult).then_inc(dve_rounded, 1)

            def measure(i, s):
                n = 2 * i + s
                v.wait_ge(c_copied, 6 * n + 6 + 2)
                v.tensor_reduce(cmax[:].rearrange("p (i s) -> p s i", s=2)[:, s, bass.ds(i, 1)], cx[s][:], AX.XYZ, ALU.max,
                                apply_absolute_value=True).then_inc(measured, 1)

            def step(i, s, first, last):
                n = 2 * i + s
                for g in range(GROUPS):
                    i2, s2, g2 = sliding(i, s, g + 2, GROUPS)
                    if g2 in by_dve and not (last and g + 2 >= GROUPS):
                        round_scores(i2, s2, g2)
                    v.wait_ge(exped, GROUPS * n + g + 1 + 4)
                    v.wait_ge(qkv_in[s], 64 * i + 64)
                    v.wait_ge(cast, GROUPS * n + g + 1)
                    head = 3 * (g % 4)
                    for half in range(2):
                        last_mul = v.tensor_tensor(a16[g % 2][:, :, half], e32[g % 2][:, :, half],
                                                   rb[s][0:HALF, head:head + 3, g // 4], ALU.mult)
                    last_mul.then_inc(weighted, 1)
                    v.wait_ge(weighted, GROUPS * n + g + 1 + PAIRG)
                    v.wait_ge(applied, GROUPS * n + g - 2 + 1 + PAIRG)
                    v.tensor_copy(ab[g % 2][:], a16[g % 2][:]).then_inc(cast, 1)
                    if g == 2 and not first:
                        measure(*((i, 0) if s else (i - 1, 1)))

            v.sem_inc(dve_rounded, len(by_dve.members))
            v.sem_inc(weighted, PAIRG)
            v.sem_inc(cast, 2)
            v.sem_inc(measured, 2)
            nc.vector.memset(cmax1[:], 0.0)
            turns(v, NPAIR, step)
            measure(NPAIR // 2 - 1, 1)
            v.drain()
            v.tensor_reduce(cmax1[:], cmax[:], AX.X, ALU.max).then_inc(cmax_ready, 1)
            v.wait_ge(cmaxg_ready, 1)
            quant_scalars(v, kit.scal, cmaxg[:], U_CTX, S_CTX, C_CTX)

        @block.gpsimd
        def _(pool):
            pool.wait_ge(cmax_ready, 1)
            nc.gpsimd.partition_all_reduce(cmaxg[:], cmax1[:], 128, RMAX).then_inc(cmaxg_ready, 1)



def norm_columns(v, out, var, tmp):
    v.reciprocal(out, out)
    v.drain()
    v.tensor_tensor(tmp, out, out, ALU.mult)
    v.drain()
    v.tensor_tensor(tmp, tmp, var, ALU.mult)
    v.drain()
    v.tensor_scalar(tmp, tmp, -0.5, 1.5, ALU.mult, ALU.add)
    v.drain()
    v.tensor_tensor(out, out, tmp, ALU.mult)
    v.drain()


TU = 3
NTILE = NTOK // 128
NTURN = NTILE // TU
EXPERTS, FEXP, FSH = 16, 4 * D, 2 * D
TOPK = NTOK // EXPERTS * 2
ROW = D + EXPERTS


def mixer_out_phase(kit, ctx_d, xt_d, h_d, gate_wt, x2_d, x2t_d, lt_d, out_d):
    nc = kit.nc
    with ExitStack() as ctx:
        y = kit.sb(ctx, "y_all", [KP, KC, NTOK], F32)
        sem = lambda name: kit.sem(ctx, name)
        sp_turn = sem("mo_sp_turn")
        by_pair = lambda a: a.rearrange("(i s) p x -> s i p x", s=2)
        cols = lambda a: a.rearrange("(m p) (i s t) -> s i p m t", p=KP, s=2, t=PAIR)

        def ycols(i, s, size, c=None):
            t = y[:].rearrange("p c (i s t) -> p s c i t", s=2, t=size)[:, s]
            t = t[:, :, bass.ds(i, 1)] if c is None else t[:, c, bass.ds(i, 1)]
            return t

        with ExitStack() as c1:
            cf = [kit.sb(c1, f"mo_c{s}", [128, 3 * PAIR], F32) for s in range(2)]
            c16 = kit.sb(c1, "mo_c16", [128, 3 * PAIR], I16)
            cb = [kit.sb(c1, f"mo_cb{s}", [128, 3, PAIR], BF16) for s in range(2)]
            ymax = kit.sb(c1, "ymax", [128, NPAIR], F32)
            ymax1 = kit.sb(c1, "ymax1", [128, 1], F32)
            ymaxg = kit.sb(c1, "ymaxg", [128, 1], F32)
            y_ps = [kit.ps(c1, f"y_ps{s}", [KP, KC, 512]) for s in range(2)]
            c_in = [sem(f"mo_c_in{s}") for s in range(2)]
            rounded = sem("mo_rounded")
            cast = sem("mo_cast")
            y_ready = sem("y_ready")
            y_copied = sem("y_copied")
            ymax_ready, ymax_all = sem("ymax_ready"), sem("ymax_all")
            block = c1.enter_context(nc.Block())

            @block.sync
            def _(sp):
                with sp.Fori(0, NPAIR // 2) as i:
                    for s in range(2):
                        sp.wait_ge(rounded, 2 * i + s + 1)
                        sp.sem_inc(sp_turn, 1)
                        sp.dma_start(cf[s][:], by_pair(ctx_d)[s][i]).then_inc(c_in[s], 16)

            @block.scalar
            def _(act):
                act.sem_inc(rounded, 2)
                act.sem_inc(y_copied, 2)
                with act.Fori(0, NPAIR // 2) as i:
                    for s in range(2):
                        n = 2 * i + s
                        act.wait_ge(c_in[s], 16 * i + 16)
                        act.wait_ge(cast, n + 1)
                        act.activation(c16[:], cf[s][:], ACT.Copy, scale=kit.scal[:, C_CTX:C_CTX + 1]).then_inc(rounded, 1)
                        act.wait_ge(y_ready, n + 1 + 2)
                        act.copy(ycols(i, s, PAIR).rearrange("p c i t -> p c (i t)"), y_ps[s][:, :, 0:PAIR])\
                            .then_inc(y_copied, 1)

            @block.vector
            def _(v):
                v.sem_inc(cast, 1)
                nc.vector.memset(ymax[:], 0.0)
                with v.Fori(0, NPAIR // 2) as i:
                    for s in range(2):
                        n = 2 * i + s
                        v.wait_ge(rounded, n + 1 + 2)
                        v.wait_ge(y_ready, n + 1)
                        v.tensor_copy(cb[s][:].rearrange("p c t -> p (c t)"), c16[:]).then_inc(cast, 1)
                        v.wait_ge(y_copied, n + 1 + 2)
                        v.tensor_reduce(ymax[0:KP].rearrange("p (i s) -> p s i", s=2)[:, s, bass.ds(i, 1)],
                                        ycols(i, s, PAIR).rearrange("p c i t -> p c (i t)"), AX.XY, ALU.max,
                                        apply_absolute_value=True)
                v.drain()
                v.tensor_reduce(ymax1[:], ymax[:], AX.X, ALU.max).then_inc(ymax_ready, 1)
                v.wait_ge(ymax_all, 1)
                v.tensor_tensor(kit.scal[:, U_Y:U_Y + 1], kit.scal[:, S_CTX:S_CTX + 1], kit.scal[:, S_WO:S_WO + 1],
                                ALU.mult)
                quant_scalars(v, kit.scal, ymaxg[:], U_Y, S_Y, C_Y)

            @block.tensor
            def _(pe):
                pe.sem_inc(y_ready, 2)
                with pe.Fori(0, NPAIR // 2) as i:
                    for s in range(2):
                        n = 2 * i + s
                        pe.wait_ge(cast, n + 1 + 1)
                        pe.wait_ge(y_copied, n + 1)
                        for o in range(KC):
                            for c in range(3):
                                mm = pe.matmul(y_ps[s][:, o, 0:PAIR], kit.w_out[:, c, o * KP:o * KP + KP], cb[s][:, c],
                                               start=(c == 0), stop=(c == 2))
                        mm.then_inc(y_ready, 1)

            @block.gpsimd
            def _(pool):
                pool.wait_ge(ymax_ready, 1)
                nc.gpsimd.partition_all_reduce(ymaxg[:], ymax1[:], 128, RMAX).then_inc(ymax_all, 1)

        mean = kit.sb(ctx, "bn_mean", [KP, KC, 2], F32)
        amp = kit.sb(ctx, "bn_amp", [KP, KC], F32)
        with ExitStack() as c2:
            xf = [kit.sb(c2, f"mo_x{s}", [KP, KC, PAIR], F32) for s in range(2)]
            x16 = [kit.sb(c2, f"mo_x16{s}", [KP, KC, PAIR], I16) for s in range(2)]
            xs = [kit.sb(c2, f"mo_xs{s}", [KP, KC, PAIR], F32) for s in range(2)]
            y16 = kit.sb(c2, "mo_y16", [KP, KC, PAIR], I16)
            bst = kit.sb(c2, "mo_bst", [KP, KC, NPAIR, 6], F32)
            hi = kit.sb(c2, "mo_hi", [KP, KC, NPAIR], F32)
            lo = kit.sb(c2, "mo_lo", [KP, KC, NPAIR], F32)
            ext = kit.sb(c2, "mo_ext", [KP, 3, KC], F32)
            vep = kit.sb(c2, "mo_vep", [KP, KC], F32)
            tmp = kit.sb(c2, "mo_tmp", [KP, KC], F32)
            rmax1 = kit.sb(c2, "rmax1", [128, 1], F32)
            rmaxg = kit.sb(c2, "rmaxg", [128, 1], F32)
            x_in = [sem(f"mo_x_in{s}") for s in range(2)]
            x_round = sem("mo_x_round")
            x_scaled = sem("mo_x_scaled")
            r_done = sem("mo_r_done")
            vep_ready, root_ready, rmax_ready, rmax_all = sem("vep_ready"), sem("root_ready"), sem("rmax_ready"), sem("rmax_all")
            block = c2.enter_context(nc.Block())

            @block.sync
            def _(sp):
                with sp.Fori(0, NPAIR // 2) as i:
                    for s in range(2):
                        sp.wait_ge(x_round, 2 * i + s + 1)
                        sp.sem_inc(sp_turn, 1)
                        sp.dma_start(xf[s][:], cols(xt_d)[s][i]).then_inc(x_in[s], 16)

            @block.scalar
            def _(act):
                act.sem_inc(x_round, 2)
                with act.Fori(0, NPAIR // 2) as i:
                    for s in range(2):
                        n = 2 * i + s
                        act.wait_ge(x_in[s], 16 * i + 16)
                        act.wait_ge(r_done, n + 1)
                        act.activation(x16[s][:], xf[s][:], ACT.Copy, scale=kit.scal[0:KP, C_X:C_X + 1]).then_inc(x_round, 1)
                        act.wait_ge(x_round, n + 1 + 2)
                        act.activation(xs[s][:], x16[s][:], ACT.Copy, scale=kit.scal[0:KP, S_X:S_X + 1]).then_inc(x_scaled, 1)
                act.wait_ge(vep_ready, 1)
                act.activation(amp[:], vep[:], ACT.Sqrt).then_inc(root_ready, 1)

            @block.vector
            def _(v):
                v.sem_inc(r_done, 2)
                nc.vector.memset(rmax1[:], 0.0)
                with v.Fori(0, NPAIR // 2) as i:
                    for s in range(2):
                        n = 2 * i + s
                        yc = ycols(i, s, PAIR).rearrange("p c i t -> p c (i t)")
                        v.tensor_scalar(y16[:], yc, kit.scal[0:KP, C_Y:C_Y + 1], None, ALU.mult)
                        v.drain()
                        v.wait_ge(x_scaled, n + 1)
                        v.scalar_tensor_tensor(yc, y16[:], kit.scal[0:KP, S_Y:S_Y + 1], xs[s][:], ALU.mult, ALU.add)\
                            .then_inc(r_done, 1)
                        v.drain()
                        for c in range(KC):
                            yi = ycols(i, s, PAIR, c).rearrange("p i t -> p (i t)")
                            v.bn_stats(bst[:, c].rearrange("p (i s) x -> p s i x", s=2)[:, s, bass.ds(i, 1)]
                                       .rearrange("p i x -> p (i x)"), yi)
                        at = lambda t: t[:].rearrange("p c (i s) -> p s c i", s=2)[:, s][:, :, bass.ds(i, 1)]
                        v.tensor_reduce(at(hi), yc, AX.X, ALU.max)
                        v.tensor_reduce(at(lo), yc, AX.X, ALU.min)
                v.drain()
                for c in range(KC):
                    v.bn_aggr(mean[:, c], bst[:, c].rearrange("p n x -> p (n x)"))
                v.tensor_reduce(ext[:, 0], hi[:], AX.X, ALU.max)
                v.tensor_reduce(ext[:, 1], lo[:], AX.X, ALU.min)
                v.drain()
                v.tensor_scalar(vep[:], mean[:, :, 1], EPS, None, ALU.add).then_inc(vep_ready, 1)
                v.tensor_tensor(ext[:, 0], ext[:, 0], mean[:, :, 0], ALU.subtract)
                v.tensor_tensor(ext[:, 1], mean[:, :, 0], ext[:, 1], ALU.subtract)
                v.drain()
                v.tensor_tensor(ext[:, 2], ext[:, 0], ext[:, 1], ALU.max)
                v.wait_ge(root_ready, 1)
                norm_columns(v, amp[:], vep[:], tmp[:])
                v.tensor_tensor(ext[:, 2], ext[:, 2], amp[:], ALU.mult)
                v.drain()
                v.tensor_reduce(rmax1[0:KP], ext[:, 2], AX.X, ALU.max).then_inc(rmax_ready, 1)
                v.wait_ge(rmax_all, 1)
                quant_scalars(v, kit.scal, rmaxg[:], None, S_RN, TMP2)
                v.tensor_scalar(amp[:], amp[:], kit.scal[0:KP, TMP2:TMP2 + 1], None, ALU.mult)

            @block.gpsimd
            def _(pool):
                pool.wait_ge(rmax_ready, 1)
                nc.gpsimd.partition_all_reduce(rmaxg[:], rmax1[:], 128, RMAX).then_inc(rmax_all, 1)

        T = 128 * TU
        with ExitStack() as c3:
            gw = kit.sb(c3, "gate_w", [KP, KC, EXPERTS], F32)
            n16 = kit.sb(c3, "n16", [KP, KC, T], I16)
            nb = [kit.sb(c3, f"nb{s}", [KP, KC, T], BF16) for s in range(2)]
            h1 = [kit.sb(c3, f"h1{s}", [128, TU, D], F32) for s in range(2)]
            hin = [kit.sb(c3, f"hin{s}", [128, TU, D], F32) for s in range(2)]
            x2 = [kit.sb(c3, f"x2{s}", [128, TU, D], F32) for s in range(2)]
            x2t = [kit.sb(c3, f"x2t{s}", [KP, KC, T], F32) for s in range(2)]
            stats = kit.sb(c3, "stats2", [128, TU, 6], F32)
            mv = kit.sb(c3, "mv2", [128, TU, 2], F32)
            ve = kit.sb(c3, "ve2", [128, TU], F32)
            rs = kit.sb(c3, "rs2", [128, TU], F32)
            tmp = kit.sb(c3, "tmp2", [128, TU], F32)
            n_ps = [kit.ps(c3, f"n_ps{s}", [128, TU * D], BF16) for s in range(2)]
            t_ps = [kit.ps(c3, f"t_ps{c}", [KP, 512]) for c in range(KC)]
            g_ps = kit.ps(c3, "g_ps", [EXPERTS, T])
            l_ps = kit.ps(c3, "l_ps", [128, TU * EXPERTS])
            lt = [kit.sb(c3, f"lt{s}", [EXPERTS, T], F32) for s in range(2)]
            h_in = [sem(f"h_in{s}") for s in range(2)]
            gw_in = sem("gw_in")
            nb_ready = sem("nb_ready")
            n_ready = sem("n_ready")
            h1_ready = sem("h1_ready")
            ve_ready, root2 = sem("ve2_ready"), sem("root2")
            x2_ready = sem("x2_ready")
            t_ready = sem("t_ready")
            t_copied = sem("t_copied")
            g_ready = sem("g_ready")
            g_copied = sem("g_copied")
            l_ready = sem("l_ready")
            l_copied = sem("l_copied")
            pe_turn = sem("pe_turn")
            h1_out, x2_out, x2t_out, lt_out = [[sem(f"{n}_out{s}") for s in range(2)] for n in ("h1", "x2", "x2t", "lt")]
            block = c3.enter_context(nc.Block())
            tiles = lambda a: a.rearrange("(i s m p) e -> s i p m e", s=2, m=TU, p=128)

            @block.sync
            def _(sp):
                sp.dma_start(gw[:], gate_wt.rearrange("(c p) e -> p c e", p=KP)).then_inc(gw_in, 16)
                for o in (h1_out, x2_out, x2t_out, lt_out):
                    for s in range(2):
                        sp.sem_inc(o[s], 16)

                def load(i, s):
                    sp.wait_ge(h1_ready, 2 * i + s + 1)
                    sp.sem_inc(sp_turn, 1)
                    sp.dma_start(hin[s][:], tiles(h_d)[s][i]).then_inc(h_in[s], 16)

                def store(i, s):
                    n = 2 * i + s
                    sp.wait_ge(h1_ready, n + 1 + 2)
                    sp.sem_inc(sp_turn, 1)
                    sp.dma_start(tiles(out_d)[s][i], h1[s][:]).then_inc(h1_out[s], 16)
                    sp.wait_ge(x2_ready, n + 1)
                    sp.sem_inc(sp_turn, 1)
                    sp.dma_start(tiles(x2_d)[s][i][:, :, 0:D], x2[s][:]).then_inc(x2_out[s], 16)
                    sp.wait_ge(t_copied, n + 1 + 1)
                    sp.sem_inc(sp_turn, 1)
                    sp.dma_start(x2t_d.rearrange("(m p) (i s t) -> s i p m t", p=KP, s=2, t=T)[s][i], x2t[s][:])\
                        .then_inc(x2t_out[s], 16)
                    sp.wait_ge(g_copied, n + 1 + 2)
                    sp.sem_inc(sp_turn, 1)
                    sp.dma_start(lt_d.rearrange("e (i s t) -> s i e t", s=2, t=T)[s][i], lt[s][:]).then_inc(lt_out[s], 16)

                load(0, 0)
                with sp.Fori(0, NTURN // 2 - 1) as i:
                    load(i, 1)
                    store(i, 0)
                    load(i + 1, 0)
                    store(i, 1)
                load(NTURN // 2 - 1, 1)
                store(NTURN // 2 - 1, 0)
                store(NTURN // 2 - 1, 1)
                for o in (h1_out, x2_out, x2t_out, lt_out):
                    for s in range(2):
                        sp.wait_ge(o[s], 16 * (NTURN // 2 + 1))

            @block.tensor
            def _(pe):
                pe.sem_inc(n_ready, 2)
                pe.sem_inc(t_ready, 2)
                pe.sem_inc(l_ready, 2)
                pe.wait_ge(gw_in, 16)

                def turn_back(i, s):
                    n = 2 * i + s
                    pe.wait_ge(nb_ready, n + 1 + 2)
                    pe.wait_ge(h1_ready, n + 1)
                    for m in range(TU):
                        for c in range(KC):
                            mm = pe.transpose(n_ps[s][:, m * D + c * KP:m * D + c * KP + KP],
                                              nb[s][:, c, m * 128:m * 128 + 128], kit.identb[0:KP, 0:KP])
                    mm.then_inc(n_ready, 1)

                def gate(i, s):
                    n = 2 * i + s
                    pe.wait_ge(x2_ready, n + 1)
                    pe.wait_ge(t_copied, n + 1)
                    for c in range(KC):
                        for m in range(TU):
                            mm = pe.transpose(t_ps[c][:, m * 128:m * 128 + 128], x2[s][:, m, c * KP:c * KP + KP], kit.ident[:])
                    mm.then_inc(t_ready, 1)
                    pe.wait_ge(t_copied, n + 1 + 1)
                    pe.wait_ge(g_copied, n + 1 + 1)
                    for c in range(KC):
                        mm = pe.matmul(g_ps[:], gw[:, c], x2t[s][:, c], start=(c == 0), stop=(c == KC - 1))
                    mm.then_inc(g_ready, 1)
                    pe.wait_ge(g_copied, n + 1 + 2)
                    pe.wait_ge(l_copied, n + 1)
                    pe.sem_inc(pe_turn, 1)
                    for m in range(TU):
                        mm = pe.transpose(l_ps[:, m * EXPERTS:m * EXPERTS + EXPERTS], lt[s][:, m * 128:m * 128 + 128],
                                          kit.ident[0:EXPERTS, 0:EXPERTS])
                    mm.then_inc(l_ready, 1)

                def step(i, s, first, last):
                    if not last:
                        turn_back(*((i, 1) if s == 0 else (i + 1, 0)))
                    gate(i, s)

                turn_back(0, 0)
                turns(pe, NTURN, step)

            @block.scalar
            def _(act):
                act.sem_inc(t_copied, 1)
                act.sem_inc(g_copied, 2)
                act.sem_inc(l_copied, 1)
                with act.Fori(0, NTURN // 2) as i:
                    for s in range(2):
                        n = 2 * i + s
                        act.wait_ge(ve_ready, n + 1)
                        act.activation(rs[:], ve[:], ACT.Sqrt).then_inc(root2, 1)
                        act.wait_ge(t_ready, n + 1 + 2)
                        act.wait_ge(x2t_out[s], 16 * i + 16)
                        for c in range(KC):
                            ins = act.copy(x2t[s][:, c], t_ps[c][:, 0:T])
                        ins.then_inc(t_copied, 1)
                        act.wait_ge(g_ready, n + 1)
                        act.wait_ge(lt_out[s], 16 * i + 16)
                        act.wait_ge(l_ready, n + 1)
                        act.copy(lt[s][:], g_ps[:]).then_inc(g_copied, 1)
                        act.wait_ge(l_ready, n + 1 + 2)
                        lg = kit.logits[:].rearrange("p (i s m) e -> p s i (m e)", s=2, m=TU)[:, s, bass.ds(i, 1)]
                        act.copy(lg.rearrange("p i x -> p (i x)"), l_ps[:]).then_inc(l_copied, 1)

            @block.vector
            def _(v):
                v.sem_inc(nb_ready, 2)
                v.sem_inc(h1_ready, 2)

                def quantise(i, s):
                    n = 2 * i + s
                    for c in range(KC):
                        yi = ycols(i, s, T, c).rearrange("p i t -> p (i t)")
                        v.tensor_scalar(n16[:, c], yi, mean[:, c, 0:1], amp[:, c:c + 1], ALU.subtract, ALU.mult)
                    v.drain()
                    v.wait_ge(n_ready, n + 1)
                    v.tensor_copy(nb[s][:], n16[:]).then_inc(nb_ready, 1)
                    v.drain()

                def step(i, s, first, last):
                    n = 2 * i + s
                    if not last:
                        quantise(*((i, 1) if s == 0 else (i + 1, 0)))
                    v.wait_ge(n_ready, n + 1 + 2)
                    v.wait_ge(h_in[s], 16 * i + 16)
                    v.wait_ge(h1_out[s], 16 * i + 16)
                    v.scalar_tensor_tensor(h1[s][:].rearrange("p m e -> p (m e)"), n_ps[s][:], kit.scal[:, S_RN:S_RN + 1],
                                           hin[s][:].rearrange("p m e -> p (m e)"), ALU.mult, ALU.add).then_inc(h1_ready, 1)
                    v.drain()
                    for m in range(TU):
                        v.bn_stats(stats[:, m], h1[s][:, m])
                    v.drain()
                    for m in range(TU):
                        v.bn_aggr(mv[:, m], stats[:, m])
                    v.drain()
                    v.tensor_scalar(ve[:], mv[:, :, 1], EPS, None, ALU.add).then_inc(ve_ready, 1)
                    v.wait_ge(root2, n + 1)
                    norm_columns(v, rs[:], ve[:], tmp[:])
                    v.wait_ge(x2_out[s], 16 * i + 16)
                    v.wait_ge(t_ready, n + 1)
                    for m in range(TU):
                        ins = v.tensor_scalar(x2[s][:, m], h1[s][:, m], mv[:, m, 0:1], rs[:, m:m + 1],
                                              ALU.subtract, ALU.mult)
                    ins.then_inc(x2_ready, 1)

                quantise(0, 0)
                turns(v, NTURN, step)


SEGS = 128 // EXPERTS
SEG = NTOK // SEGS
HIS = TOPK // HALF
LIFT = 2.0 ** 64
LOWEST = 2.0 ** -63


def sigmoid_scores(v, t):
    v.tensor_scalar(t, t, 3e38, 1.0, ALU.min, ALU.add)
    v.drain()
    v.reciprocal(t, t)
    v.drain()
    v.tensor_scalar(t, t, LIFT, None, ALU.mult)
    v.drain()
    return v.scalar_tensor_tensor(t, t, LOWEST, t, ALU.is_ge, ALU.mult)


def route_phase(kit, lt_d, x2_d, thr_d):
    nc = kit.nc
    with ExitStack() as ctx:
        sc = kit.sb(ctx, "scores", [128, NTILE, EXPERTS], F32)
        thr = kit.sb(ctx, "thresholds", [128, 128, 2], F32)
        with ExitStack() as c1:
            st = kit.sb(c1, "scores_t", [128, SEG], F32)
            mask = kit.sb(c1, "rt_mask", [128, SEG], BF16)
            same = kit.sb(c1, "same_expert", [128, 128], F32)
            cnt = kit.sb(c1, "rt_count", [128, 1], F32)
            res = kit.sb(c1, "rt_result", [128, 2], F32)
            cand = kit.sb(c1, "rt_cand", [128, 1], F32)
            step = kit.sb(c1, "rt_step", [128, 1], F32)
            got = kit.sb(c1, "rt_got", [128, 1], F32)
            tot_ps = kit.ps(c1, "rt_total", [128, 1])
            sem = lambda name: kit.sem(c1, name)
            lt_in, same_ready = sem("rt_lt_in"), sem("rt_same_ready")
            exped, scored, lifted = sem("rt_exped"), sem("rt_scored"), sem("rt_lifted")
            counted, totalled, found = sem("rt_counted"), sem("rt_totalled"), sem("rt_found")
            stored, thr_out, thr_in = sem("rt_stored"), sem("rt_thr_out"), sem("rt_thr_in")
            block = c1.enter_context(nc.Block())
            PROBES = 8 + 23 + 1

            @block.sync
            def _(sp):
                sp.dma_start(st[:], lt_d.rearrange("e (g t) -> (e g) t", g=SEGS)).then_inc(lt_in, 16)
                sp.wait_ge(lifted, 1)
                sp.dma_start(x2_d.rearrange("(t p) e -> p t e", p=128)[:, :, D:ROW], sc[:]).then_inc(stored, 16)
                sp.wait_ge(found, 1)
                sp.dma_start(thr_d, res[:]).then_inc(thr_out, 16)
                sp.wait_ge(thr_out, 16)
                row = thr_d.rearrange("(x p) c -> x (p c)", x=1)
                sp.dma_start(thr[:].rearrange("p e c -> p (e c)"), row.to_broadcast([128, 2 * 128])).then_inc(thr_in, 16)
                sp.wait_ge(thr_in, 16)
                sp.wait_ge(stored, 16)

            @block.gpsimd
            def _(pool):
                nc.gpsimd.memset(same[:], 1.0).then_inc(same_ready, 1)
                pool.wait_ge(same_ready, 1)
                v3 = same[:].rearrange("p (e g) -> p e g", g=SEGS)
                nc.gpsimd.affine_select(out=v3, in_=v3, compare_op=ALU.is_ge, fill=0.0, base=0,
                                        pattern=[[-SEGS, EXPERTS], [0, SEGS]], channel_multiplier=1).then_inc(same_ready, 1)
                pool.wait_ge(same_ready, 2)
                nc.gpsimd.affine_select(out=v3, in_=v3, compare_op=ALU.is_ge, fill=0.0, base=SEGS - 1,
                                        pattern=[[SEGS, EXPERTS], [0, SEGS]], channel_multiplier=-1).then_inc(same_ready, 1)

            @block.scalar
            def _(act):
                act.wait_ge(lt_in, 16)
                act.activation(st[:], st[:], ACT.Exp, scale=-1.0).then_inc(exped, 1)
                act.activation(sc[:].rearrange("p t e -> p (t e)"), kit.logits[:].rearrange("p t e -> p (t e)"), ACT.Exp,
                               scale=-1.0).then_inc(exped, 1)

            @block.tensor
            def _(pe):
                pe.wait_ge(same_ready, 3)
                with pe.Fori(0, PROBES) as i:
                    pe.wait_ge(counted, i + 1)
                    pe.matmul(tot_ps[:], same[:], cnt[:], start=True, stop=True).then_inc(totalled, 1)

            @block.vector
            def _(v):
                v.wait_ge(exped, 2)
                sigmoid_scores(v, st[:]).then_inc(scored, 1)
                sigmoid_scores(v, sc[:].rearrange("p t e -> p (t e)")).then_inc(lifted, 1)
                nc.vector.memset(res[:], 0.0)
                nc.vector.memset(cand[:], LOWEST)
                v.drain()

                def probe(n):
                    v.tensor_scalar(mask[:], st[:], cand[:], None, ALU.is_ge, ALU.add, accum_out=cnt[:]).then_inc(counted, 1)
                    v.wait_ge(totalled, n + 1)
                    v.tensor_scalar(got[:], tot_ps[:], TOPK - 0.5, cand[:], ALU.is_ge, ALU.mult)
                    v.drain()
                    v.tensor_tensor(res[:, 0:1], res[:, 0:1], got[:], ALU.max)
                    v.drain()

                probe(0)
                for k, bits in enumerate((64, 32, 16, 8, 4, 2, 1)):
                    v.tensor_scalar(cand[:], res[:, 0:1], 2.0 ** bits, None, ALU.mult)
                    v.drain()
                    probe(k + 1)
                v.tensor_scalar(step[:], res[:, 0:1], 0.5, None, ALU.mult)
                v.drain()
                with v.Fori(0, 23) as i:
                    v.tensor_tensor(cand[:], res[:, 0:1], step[:], ALU.add)
                    v.drain()
                    v.tensor_scalar(step[:], step[:], 0.5, None, ALU.mult)
                    probe(i + 8)
                v.tensor_scalar(mask[:], st[:], res[:, 0:1], None, ALU.is_gt, ALU.add, accum_out=cnt[:]).then_inc(counted, 1)
                v.wait_ge(totalled, PROBES)
                v.tensor_scalar(res[:, 1:2], tot_ps[:], -1.0, float(TOPK), ALU.mult, ALU.add).then_inc(found, 1)

        kit.clear_semaphores()

        lo1 = kit.sb(ctx, "slot_lo", [128, NTILE, EXPERTS], BF16)
        his = kit.sb(ctx, "slot_hi", [128, NTILE, EXPERTS], BF16)
        with ExitStack() as c2:
            above = kit.sb(c2, "rt_above", [128, NTILE, EXPERTS], BF16)
            tie = kit.sb(c2, "rt_tie", [128, NTILE, EXPERTS], BF16)
            early = kit.sb(c2, "rt_early", [128, NTILE, EXPERTS], BF16)
            hi16 = kit.sb(c2, "rt_hi16", [128, NTILE, EXPERTS], I16)
            tri = kit.sb(c2, "rt_tri", [128, 128], BF16)
            ones = kit.sb(c2, "rt_ones", [128, 128], BF16)
            tot = kit.sb(c2, "rt_tot", [NTILE, EXPERTS], F32)
            before = kit.sb(c2, "rt_before", [NTILE, NTILE, EXPERTS], BF16)
            PIECES, PIECE = 4, NTILE * EXPERTS // 4
            rank_ps = kit.ps(c2, "rank_ps", [128, PIECES, 512])
            t_ps = kit.ps(c2, "rt_tot_ps", [NTILE, EXPERTS])
            sem = lambda name: kit.sem(c2, name)
            tri_ready, masked, summed = sem("rt_tri_ready"), sem("rt_masked"), sem("rt_summed")
            tot_copied, spread, ranked = sem("rt_tot_copied"), sem("rt_spread"), sem("rt_ranked")
            block = c2.enter_context(nc.Block())

            @block.gpsimd
            def _(pool):
                nc.gpsimd.memset(ones[:], 1.0).then_inc(tri_ready, 1)
                nc.gpsimd.memset(tri[:], 1.0).then_inc(tri_ready, 1)
                pool.wait_ge(tri_ready, 2)
                nc.gpsimd.affine_select(out=tri[:], in_=tri[:], compare_op=ALU.is_ge, fill=0.0, base=-1,
                                        pattern=[[1, 128]], channel_multiplier=-1).then_inc(tri_ready, 1)
                for r in range(2):
                    pool.wait_ge(tot_copied, r + 1)
                    nc.gpsimd.affine_select(out=before[:], in_=tot[:, None, :].to_broadcast([NTILE, NTILE, EXPERTS]),
                                            compare_op=ALU.is_ge, fill=0.0, base=-1,
                                            pattern=[[1, NTILE], [0, EXPERTS]], channel_multiplier=-1).then_inc(spread, 1)

            @block.scalar
            def _(act):
                for r in range(2):
                    act.wait_ge(summed, r + 1)
                    act.copy(tot[:], t_ps[:]).then_inc(tot_copied, 1)

            @block.tensor
            def _(pe):
                pe.wait_ge(tri_ready, 3)
                for r, m in enumerate((tie, above)):
                    pe.wait_ge(masked, r + 1)
                    for e in range(EXPERTS):
                        mm = pe.matmul(t_ps[:, e:e + 1], m[:, :, e], ones[:, 0:1], start=True, stop=True)
                    mm.then_inc(summed, 1)
                    pe.wait_ge(spread, r + 1)
                    for b in range(PIECES):
                        w = slice(b * PIECE, b * PIECE + PIECE)
                        pe.matmul(rank_ps[:, b, 0:PIECE], tri[:], m[:].rearrange("p t e -> p (t e)")[:, w],
                                  start=True, stop=False)
                        mm = pe.matmul(rank_ps[:, b, 0:PIECE], ones[0:NTILE], before[:].rearrange("p t e -> p (t e)")[:, w],
                                       start=False, stop=True)
                    mm.then_inc(ranked, 1)

            @block.vector
            def _(v):
                def per_expert(c):
                    one = thr[:].rearrange("p (e g) c -> p g c e", g=SEGS)[:, 0, c:c + 1]
                    return one.to_broadcast([128, NTILE, EXPERTS])
                pieces = lambda t: t[:].rearrange("p t e -> p (t e)").rearrange("p (b w) -> p b w", b=PIECES)
                v.tensor_tensor(tie[:], sc[:], per_expert(0), ALU.is_equal).then_inc(masked, 1)
                v.tensor_tensor(above[:], sc[:], per_expert(0), ALU.is_gt)
                v.wait_ge(ranked, 1)
                v.tensor_copy(pieces(hi16), rank_ps[:, :, 0:PIECE])
                v.drain()
                v.tensor_tensor(early[:], hi16[:], per_expert(1), ALU.is_lt)
                v.drain()
                v.tensor_tensor(early[:], early[:], tie[:], ALU.mult)
                v.drain()
                v.tensor_tensor(above[:], above[:], early[:], ALU.add).then_inc(masked, 1)
                v.wait_ge(ranked, 2)
                v.tensor_scalar(pieces(hi16), rank_ps[:, :, 0:PIECE], 1.0 / HALF, 0.5 / HALF - 0.5, ALU.mult, ALU.add)
                v.drain()
                v.tensor_copy(his[:], hi16[:])
                v.scalar_tensor_tensor(pieces(lo1), pieces(hi16), -float(HALF), rank_ps[:, :, 0:PIECE], ALU.mult, ALU.add)
                v.drain()
                v.scalar_tensor_tensor(lo1[:], lo1[:], 1.0, above[:], ALU.add, ALU.mult)

        kit.clear_semaphores()

        with ExitStack() as c3:
            iota_hi = kit.sb(c3, "iota_hi", [128, EXPERTS, HIS], BF16)
            iota_lo = kit.sb(c3, "iota_lo", [128, HALF], BF16)
            iota_p = kit.sb(c3, "iota_p", [128, 1], F32)
            iota_t = kit.sb(c3, "iota_t", [128, NTILE], F32)
            hot_hi = kit.sb(c3, "hot_hi", [128, EXPERTS, HIS], BF16)
            hot_lo = [kit.sb(c3, f"hot_lo{s}", [128, EXPERTS, HALF], BF16) for s in range(2)]
            val = [kit.sb(c3, f"hot_val{s}", [128, EXPERTS, 2, HIS], BF16) for s in range(2)]
            slotf = kit.sb(c3, "slot_f32", [HALF, EXPERTS, 2, HIS], F32)
            slot_ps = kit.ps(c3, "slot_ps", [HALF, EXPERTS, 2 * HIS])
            sem = lambda name: kit.sem(c3, name)
            iotas, lo_ready, val_ready = sem("rt_iotas"), sem("rt_lo_ready"), sem("rt_val_ready")
            used = sem("rt_used")
            copied = sem("rt_slots_copied")
            block = c3.enter_context(nc.Block())

            def column(t, i, s):
                return t[:].rearrange("p (i s) e -> p s i e", s=2)[:, s, bass.ds(i, 1)].rearrange("p i e -> p (i e)")

            @block.gpsimd
            def _(pool):
                io = dict(allow_small_or_imprecise_dtypes=True)
                nc.gpsimd.iota(iota_hi[:], pattern=[[0, EXPERTS], [1, HIS]], base=0, channel_multiplier=0, **io).then_inc(iotas, 1)
                nc.gpsimd.iota(iota_lo[:], pattern=[[1, HALF]], base=1, channel_multiplier=0, **io).then_inc(iotas, 1)
                nc.gpsimd.iota(iota_p[:], pattern=[[0, 1]], base=0, channel_multiplier=1, **io).then_inc(iotas, 1)
                nc.gpsimd.iota(iota_t[:], pattern=[[1, NTILE]], base=0, channel_multiplier=0, **io).then_inc(iotas, 1)
                pool.wait_ge(iotas, 4)

            @block.tensor
            def _(pe):
                pe.sem_inc(used, 2)

                def step(i, s, first, last):
                    n = 2 * i + s
                    pe.wait_ge(val_ready, n + 1)
                    for e in range(EXPERTS):
                        mm = pe.matmul(slot_ps[:, e], hot_lo[s][:, e], val[s][:, e].rearrange("p c h -> p (c h)"),
                                       start=(first and e == 0), stop=last, skip_group_check=True)
                    mm.then_inc(used, 1)

                turns(pe, NTILE, step)

            @block.vector
            def _(v):
                v.wait_ge(iotas, 4)

                def step(i, s, first, last):
                    n = 2 * i + s
                    v.wait_ge(used, n + 1)
                    lo = column(lo1, i, s)[:, :, None].to_broadcast([128, EXPERTS, HALF])
                    v.tensor_tensor(hot_lo[s][:], iota_lo[:, None, :].to_broadcast([128, EXPERTS, HALF]), lo, ALU.is_equal)
                    hi = column(his, i, s)[:, :, None].to_broadcast([128, EXPERTS, HIS])
                    v.tensor_tensor(hot_hi[:], iota_hi[:], hi, ALU.is_equal)
                    v.drain()
                    v.tensor_scalar(val[s][:, :, 0], hot_hi[:], iota_p[:], None, ALU.mult)
                    tile = iota_t[:].rearrange("p (i s) -> p s i", s=2)[:, s, bass.ds(i, 1)]
                    v.tensor_tensor(val[s][:, :, 1], hot_hi[:], tile[:, :, None].to_broadcast([128, EXPERTS, HIS]),
                                    ALU.mult).then_inc(val_ready, 1)
                    v.drain()

                turns(v, NTILE, step)
                v.wait_ge(copied, 1)
                v.scalar_tensor_tensor(kit.slots[:], slotf[:, :, 1], 128.0, slotf[:, :, 0], ALU.mult, ALU.add)

            @block.scalar
            def _(act):
                act.wait_ge(used, NTILE + 2)
                act.copy(slotf[:].rearrange("p e c h -> p e (c h)"), slot_ps[:]).then_inc(copied, 1)


CH = 4
NCHUNK = HIS // CH
WIDE = CH * HALF


def shared_phase(kit, x2t_d, wsg_t, wsu_t, wsd_t, out_d):
    nc = kit.nc
    FT = FSH // 128
    with ExitStack() as ctx:
        wg = kit.sb(ctx, "ws_g", [KP, KC, FSH], F32)
        wu = kit.sb(ctx, "ws_u", [KP, KC, FSH], F32)
        wd = kit.sb(ctx, "ws_d", [128, FT, D], F32)
        xt = [kit.sb(ctx, f"sh_xt{s}", [KP, KC, WIDE], F32) for s in range(2)]
        g = [kit.sb(ctx, f"sh_g{b}", [128, WIDE], F32) for b in range(2)]
        h = [kit.sb(ctx, f"sh_h{s}", [128, FT, WIDE], F32) for s in range(2)]
        o = [kit.sb(ctx, f"sh_o{s}", [HALF, CH, D], F32) for s in range(2)]
        hin = [kit.sb(ctx, f"sh_in{s}", [HALF, CH, D], F32) for s in range(2)]
        g_ps = [kit.ps(ctx, f"sh_g_ps{b}", [128, 512]) for b in range(2)]
        u_ps = [kit.ps(ctx, f"sh_u_ps{b}", [128, 512]) for b in range(2)]
        o_ps = kit.ps(ctx, "sh_o_ps", [HALF, 2, 512])
        sem = lambda name: kit.sem(ctx, name)
        w_in = sem("sh_w_in")
        x_in = [sem(f"sh_x_in{s}") for s in range(2)]
        h_in = [sem(f"sh_h_in{s}") for s in range(2)]
        gu_ready = sem("sh_gu_ready")
        silu_ready = sem("sh_silu_ready")
        h_ready = sem("sh_h_ready")
        down_ready = sem("sh_down_ready")
        o_ready = sem("sh_o_ready")
        o_out = [sem(f"sh_o_out{s}") for s in range(2)]
        sp_turn = sem("sh_sp_turn")
        block = ctx.enter_context(nc.Block())
        cols = x2t_d.rearrange("(c p) (i s t) -> s i p c t", p=KP, s=2, t=WIDE)
        rows = out_d.rearrange("(i s j p) e -> s i p j e", s=2, j=CH, p=HALF)

        @block.sync
        def _(sp):
            sp.dma_start(wg[:], wsg_t.rearrange("(c p) f -> p c f", p=KP)).then_inc(w_in, 16)
            sp.dma_start(wu[:], wsu_t.rearrange("(c p) f -> p c f", p=KP)).then_inc(w_in, 16)
            sp.dma_start(wd[:], wsd_t.rearrange("(f p) e -> p f e", p=128)).then_inc(w_in, 16)
            for s in range(2):
                sp.sem_inc(o_out[s], 16)

            def load(i, s):
                n = 2 * i + s
                sp.wait_ge(gu_ready, FT * n + FT)
                sp.sem_inc(sp_turn, 1)
                sp.dma_start(xt[s][:], cols[s][i]).then_inc(x_in[s], 16)
                sp.wait_ge(o_ready, n + 1)
                sp.sem_inc(sp_turn, 1)
                sp.dma_start(hin[s][:], rows[s][i]).then_inc(h_in[s], 16)

            def step(i, s, first, last):
                if not last:
                    load(*((i, 1) if s == 0 else (i + 1, 0)))
                sp.wait_ge(o_ready, 2 * i + s + 1 + 2)
                sp.sem_inc(sp_turn, 1)
                sp.dma_start(rows[s][i], o[s][:]).then_inc(o_out[s], 16)

            load(0, 0)
            turns(sp, NPAIR, step)
            for s in range(2):
                sp.wait_ge(o_out[s], 16 * (NPAIR // 2 + 1))

        @block.tensor
        def _(pe):
            pe.sem_inc(gu_ready, 2 * FT)
            pe.sem_inc(down_ready, 2)
            pe.wait_ge(w_in, 48)

            def gate_up(i, s):
                n = 2 * i + s
                pe.wait_ge(x_in[s], 16 * i + 16)
                for f in range(FT):
                    b = (s * FT + f) % 2
                    pe.wait_ge(h_ready, FT * n + f + 1)
                    for ps, w in ((g_ps[b], wg), (u_ps[b], wu)):
                        for c in range(KC):
                            mm = pe.matmul(ps[:, 0:WIDE], w[:, c, f * 128:f * 128 + 128], xt[s][:, c],
                                           start=(c == 0), stop=(c == KC - 1))
                    mm.then_inc(gu_ready, 1)

            def down(i, s):
                n = 2 * i + s
                pe.wait_ge(h_ready, FT * n + FT + 2)
                pe.wait_ge(o_ready, n + 1 + 1)
                for j in range(CH):
                    for f in range(FT):
                        mm = pe.matmul(o_ps[:, j // 2, j % 2 * D:j % 2 * D + D], h[s][:, f, j * HALF:j * HALF + HALF],
                                       wd[:, f], start=(f == 0), stop=(f == FT - 1))
                mm.then_inc(down_ready, 1)

            def step(i, s, first, last):
                if not last:
                    gate_up(*((i, 1) if s == 0 else (i + 1, 0)))
                down(i, s)

            gate_up(0, 0)
            turns(pe, NPAIR, step)

        @block.scalar
        def _(act):
            with act.Fori(0, NPAIR // 2) as i:
                for s in range(2):
                    n = 2 * i + s
                    for f in range(FT):
                        b = (s * FT + f) % 2
                        act.wait_ge(gu_ready, FT * n + f + 1 + 2 * FT)
                        act.wait_ge(h_ready, FT * n + f + 1)
                        act.activation(g[b][:], g_ps[b][:, 0:WIDE], ACT.Silu).then_inc(silu_ready, 1)

        @block.vector
        def _(v):
            v.sem_inc(h_ready, 2)
            v.sem_inc(o_ready, 2)

            def gated(i, s):
                n = 2 * i + s
                v.wait_ge(down_ready, n + 1)
                for f in range(FT):
                    b = (s * FT + f) % 2
                    v.wait_ge(silu_ready, FT * n + f + 1)
                    v.tensor_tensor(h[s][:, f], u_ps[b][:, 0:WIDE], g[b][:], ALU.mult).then_inc(h_ready, 1)

            def step(i, s, first, last):
                n = 2 * i + s
                if not last:
                    gated(*((i, 1) if s == 0 else (i + 1, 0)))
                v.wait_ge(down_ready, n + 1 + 2)
                v.wait_ge(h_in[s], 16 * i + 16)
                v.wait_ge(o_out[s], 16 * i + 16)
                v.tensor_tensor(o[s][:].rearrange("p (a b) e -> p a (b e)", a=2), o_ps[:, :, 0:2 * D],
                                hin[s][:].rearrange("p (a b) e -> p a (b e)", a=2), ALU.add).then_inc(o_ready, 1)

            gated(0, 0)
            turns(v, NPAIR, step)


def expert_phase(kit, x2_d, wg_t, wu_t, wd_t, out_d):
    nc = kit.nc
    FT = FEXP // 128
    LOCAL = 2 * NCHUNK
    SEED = NCHUNK + 2
    with ExitStack() as ctx:
        wg = [kit.sb(ctx, f"we_g{x}", [KP, KC, FEXP], F32) for x in range(2)]
        wu = [kit.sb(ctx, f"we_u{x}", [KP, KC, FEXP], F32) for x in range(2)]
        wd = [kit.sb(ctx, f"we_d{x}", [128, FT, D], F32) for x in range(2)]
        idx = [kit.sb(ctx, f"idx{x}", [HALF, HIS], I32) for x in range(2)]
        xg = [kit.sb(ctx, f"ex_xg{s}", [HALF, CH, ROW], F32) for s in range(2)]
        xt = [kit.sb(ctx, f"ex_xt{s}", [KP, KC, WIDE], F32) for s in range(2)]
        sc = [kit.sb(ctx, f"ex_sc{s}", [HALF, CH], F32) for s in range(2)]
        g = [kit.sb(ctx, f"ex_g{b}", [128, WIDE], F32) for b in range(2)]
        h = [kit.sb(ctx, f"ex_h{s}", [128, FT, WIDE], F32) for s in range(2)]
        o = [kit.sb(ctx, f"ex_o{s}", [HALF, CH, D], F32) for s in range(2)]
        t_ps = kit.ps(ctx, "ex_t_ps", [KP, KC, 512])
        g_ps = [kit.ps(ctx, f"ex_g_ps{b}", [128, 512]) for b in range(2)]
        u_ps = [kit.ps(ctx, f"ex_u_ps{b}", [128, 512]) for b in range(2)]
        o_ps = kit.ps(ctx, "ex_o_ps", [HALF, 2, 512])
        sem = lambda name: kit.sem(ctx, name)
        w_in = [sem(f"ex_w_in{x}") for x in range(2)]
        idx_ready = sem("ex_idx_ready")
        x_in = [sem(f"ex_x_in{s}") for s in range(2)]
        t_ready = sem("ex_t_ready")
        t_copied = sem("ex_t_copied")
        sc_ready = sem("ex_sc_ready")
        gu_ready = sem("ex_gu_ready")
        silu_ready = sem("ex_silu_ready")
        h_ready = sem("ex_h_ready")
        down_ready = sem("ex_down_ready")
        o_ready = sem("ex_o_ready")
        added = [sem(f"ex_added{s}") for s in range(2)]
        o_free = sem("ex_o_free")
        pool_turn = sem("ex_pool_turn")
        sp_turn = sem("ex_sp_turn")
        block = ctx.enter_context(nc.Block())

        def turn(engine, step):
            with engine.Fori(0, EXPERTS // 2 - 1) as i:
                for k in range(LOCAL):
                    step(i, k, False)
            for k in range(LOCAL):
                step(EXPERTS // 2 - 1, k, k == LOCAL - 1)

        @block.sync
        def _(sp):
            by_pair = lambda a, p: a.rearrange("(i x) (c p) f -> x i p c f", x=2, p=p)
            with sp.Fori(0, EXPERTS // 2) as i:
                for x in range(2):
                    sp.wait_ge(down_ready, NCHUNK * (2 * i + x) + SEED - NCHUNK)
                    sp.sem_inc(sp_turn, 1)
                    sp.dma_start(wg[x][:], by_pair(wg_t, KP)[x][i]).then_inc(w_in[x], 16)
                    sp.dma_start(wu[x][:], by_pair(wu_t, KP)[x][i]).then_inc(w_in[x], 16)
                    sp.dma_start(wd[x][:], by_pair(wd_t, 128)[x][i]).then_inc(w_in[x], 16)

        @block.gpsimd
        def _(pool):
            def take_slots(i, x):
                one = kit.slots[:].rearrange("p (i x) h -> p x i h", x=2)[:, x, bass.ds(i, 1)].rearrange("p i h -> p (i h)")
                nc.gpsimd.tensor_copy(idx[x][:], one).then_inc(idx_ready, 1)
                pool.wait_ge(idx_ready, 2 * i + x + 1)
                pool.sem_inc(pool_turn, 1)

            def gather(k):
                x, q = divmod(k % LOCAL, NCHUNK)
                for j in range(CH):
                    nc.gpsimd.indirect_dma_start(
                        out=xg[k % 2][:, j], out_offset=None, in_=x2_d,
                        in_offset=bass.IndirectOffsetOnAxis(ap=idx[x][:, q * CH + j:q * CH + j + 1], axis=0))\
                        .then_inc(x_in[k % 2], 16)

            def scatter_add(k):
                x, q = divmod(k % LOCAL, NCHUNK)
                for j in range(CH):
                    nc.gpsimd.indirect_dma_start(
                        out=out_d, out_offset=bass.IndirectOffsetOnAxis(ap=idx[x][:, q * CH + j:q * CH + j + 1], axis=0),
                        in_=o[k % 2][:, j], in_offset=None, compute_op=ALU.add).then_inc(added[k % 2], 16)

            def step(i, k, last):
                n = LOCAL * i + k
                if not (type(i) is int and k + 2 >= LOCAL):
                    if k + 2 == NCHUNK:
                        take_slots(i, 1)
                    elif k + 2 == LOCAL:
                        take_slots(i + 1, 0)
                    pool.wait_ge(t_ready, n + 1)
                    pool.wait_ge(sc_ready, n + 1)
                    pool.sem_inc(pool_turn, 1)
                    gather(k + 2)
                pool.wait_ge(o_ready, n + 1 + 1)
                pool.sem_inc(pool_turn, 1)
                scatter_add(k)
                pool.wait_ge(added[k % 2], CH * 16 * (LOCAL // 2 * i + k // 2 + 1))
                pool.sem_inc(o_free, 1)

            take_slots(0, 0)
            gather(0)
            gather(1)
            turn(pool, step)

        @block.tensor
        def _(pe):
            pe.sem_inc(down_ready, SEED)

            def transpose_x(i, k):
                n = LOCAL * i + k
                s = k % 2
                pe.wait_ge(x_in[s], CH * 16 * (LOCAL // 2 * i + k // 2 + 1))
                for c in range(KC):
                    for j in range(CH):
                        mm = pe.transpose(t_ps[:, c, j * HALF:j * HALF + HALF], xg[s][:, j, c * KP:c * KP + KP],
                                          kit.ident[0:HALF, 0:HALF])
                mm.then_inc(t_ready, 1)

            def step(i, k, last):
                n = LOCAL * i + k
                s, x = k % 2, k // NCHUNK
                if k % NCHUNK == 0:
                    pe.wait_ge(w_in[x], 48 * i + 48)
                pe.wait_ge(t_copied, n + 1)
                for f in range(FT):
                    b = f % 2
                    pe.wait_ge(h_ready, FT * n + f + 1)
                    for ps, w in ((g_ps[b], wg[x]), (u_ps[b], wu[x])):
                        for c in range(KC):
                            mm = pe.matmul(ps[:, 0:WIDE], w[:, c, f * 128:f * 128 + 128], xt[s][:, c],
                                           start=(c == 0), stop=(c == KC - 1))
                    mm.then_inc(gu_ready, 1)
                if not last:
                    if k + 1 == LOCAL:
                        transpose_x(i + 1, 0)
                    else:
                        transpose_x(i, k + 1)
                pe.wait_ge(h_ready, FT * n + FT + 2)
                pe.wait_ge(o_ready, n + 1)
                for j in range(CH):
                    for f in range(FT):
                        mm = pe.matmul(o_ps[:, j // 2, j % 2 * D:j % 2 * D + D], h[s][:, f, j * HALF:j * HALF + HALF],
                                       wd[x][:, f], start=(f == 0), stop=(f == FT - 1))
                mm.then_inc(down_ready, 1)

            transpose_x(0, 0)
            turn(pe, step)

        @block.scalar
        def _(act):
            def copy_x(i, k):
                act.wait_ge(t_ready, LOCAL * i + k + 1)
                for c in range(KC):
                    ins = act.copy(xt[k % 2][:, c], t_ps[:, c, 0:WIDE])
                ins.then_inc(t_copied, 1)

            def step(i, k, last):
                n = LOCAL * i + k
                for f in range(FT):
                    b = f % 2
                    act.wait_ge(gu_ready, FT * n + f + 1)
                    act.wait_ge(h_ready, FT * n + f + 1)
                    act.activation(g[b][:], g_ps[b][:, 0:WIDE], ACT.Silu).then_inc(silu_ready, 1)
                if not last:
                    copy_x(*((i + 1, 0) if k + 1 == LOCAL else (i, k + 1)))

            copy_x(0, 0)
            turn(act, step)

        @block.vector
        def _(v):
            v.sem_inc(h_ready, 2)
            v.sem_inc(o_ready, 1)
            v.sem_inc(o_free, 2)

            def step(i, k, last):
                n = LOCAL * i + k
                s, x = k % 2, k // NCHUNK
                v.wait_ge(x_in[s], CH * 16 * (LOCAL // 2 * i + k // 2 + 1))
                mine = xg[s][:, :, D:ROW].rearrange("p j (i x) -> p x j i", x=2)[:, x][:, :, bass.ds(i, 1)]
                v.tensor_scalar(sc[s][:, :, None], mine, 1.0 / LIFT, None, ALU.mult).then_inc(sc_ready, 1)
                v.wait_ge(down_ready, n - 1 + SEED)
                for f in range(FT):
                    b = f % 2
                    v.wait_ge(silu_ready, FT * n + f + 1)
                    v.tensor_tensor(h[s][:, f], u_ps[b][:, 0:WIDE], g[b][:], ALU.mult).then_inc(h_ready, 1)
                v.wait_ge(down_ready, n + 1 + SEED)
                v.wait_ge(o_free, n + 1)
                for j in range(CH):
                    ins = v.tensor_scalar(o[s][:, j], o_ps[:, j // 2, j % 2 * D:j % 2 * D + D], sc[s][:, j:j + 1], None,
                                          ALU.mult)
                ins.then_inc(o_ready, 1)

            turn(v, step)


def build(nc, A, O):
    with ExitStack() as ctx:
        kit = Kit(nc, ctx)
        kit.scal = kit.sb(ctx, "scalars", [128, NSCAL], F32)
        kit.ident = kit.sb(ctx, "ident", [128, 128], F32)
        kit.identb = kit.sb(ctx, "identb", [128, 128], BF16)
        kit.w_in = kit.sb(ctx, "w_in", [128, KC, 3 * D], BF16)
        kit.w_out = kit.sb(ctx, "w_out", [128, 3, D], BF16)
        dram = lambda name, shape, dt: nc.dram_tensor(name, shape, dt, kind="Internal").ap()
        h_d = dram("h_tokens", (NTOK, D), F32)
        xt_d = dram("x_columns", (D, NTOK), F32)
        qk_d = dram("qk_columns", (2 * D, NTOK), F32)
        v_d = dram("v_tokens", (NTOK, D), F32)
        qb_d = dram("q_whole", (NPAIR, 128, 3 * PAIR), BF16)
        kb_d = dram("k_whole", (NPAIR, 128, 3 * PAIR), BF16)
        vb_d = dram("v_whole", (NPAIR, HALF, 4 * HEADS * 32), BF16)
        r_d = dram("row_factors", (NPAIR, 48 * HALF), F32)
        ctx_d = dram("context_t", (NPAIR, 128, 3 * PAIR), F32)
        mneg_d = dram("row_maxima", (NPAIR, 48, HALF), BF16)
        kit.logits = kit.sb(ctx, "logits", [128, NTILE, EXPERTS], F32)
        x2_d = dram("x2_rows", (NTOK, ROW), F32)
        x2t_d = dram("x2_columns", (D, NTOK), F32)
        lt_d = dram("logits_t", (EXPERTS, NTOK), F32)
        thr_d = dram("threshold_rows", (128, 2), F32)
        kit.slots = kit.sb(ctx, "slots", [HALF, EXPERTS, HIS], I32)
        setup_phase(kit, A["w_in_t"], A["w_out_t"])
        kit.clear_semaphores()
        tokenize_phase(kit, A["patches"], A["txt"], A["chan_w"], h_d, qk_d, v_d, xt_d)
        kit.clear_semaphores()
        score_range_phase(kit, qk_d, v_d, qb_d, kb_d, vb_d, mneg_d)
        kit.clear_semaphores()
        row_sum_phase(kit, qb_d, kb_d, r_d)
        kit.clear_semaphores()
        context_phase(kit, qb_d, kb_d, vb_d, r_d, ctx_d)
        kit.clear_semaphores()
        mixer_out_phase(kit, ctx_d, xt_d, h_d, A["gate_wt"], x2_d, x2t_d, lt_d, O)
        kit.clear_semaphores()
        route_phase(kit, lt_d, x2_d, thr_d)
        kit.clear_semaphores()
        shared_phase(kit, x2t_d, A["wsg_t"], A["wsu_t"], A["wsd_t"], O)
        kit.clear_semaphores()
        expert_phase(kit, x2_d, A["wg_t"], A["wu_t"], A["wd_t"], O)

def kernel(x, txt, L0_tok_channel_weights, L0_attn_w_in, L0_attn_w_out, L0_ffn_gate_weight, L0_ffn_Wg, L0_ffn_Wu,
           L0_ffn_Wd, L0_ffn_Ws_g, L0_ffn_Ws_u, L0_ffn_Ws_d):
    import numpy as _np
    import concourse.bacc as _bacc
    from concourse import mybir as _mybir
    from concourse.bass_utils import run_bass_kernel_spmd as _run

    flat = _np.ascontiguousarray
    patches = x.reshape(BATCH, CHAN, GRID, PATCH, GRID, PATCH).transpose(0, 2, 4, 1, 3, 5)
    laid = dict(
        patches=flat(patches).reshape(BATCH * NPATCH, CHAN * PATCH * PATCH),
        txt=flat(txt),
        chan_w=flat(L0_tok_channel_weights),
        w_in_t=flat(L0_attn_w_in.T),
        w_out_t=flat(L0_attn_w_out.T),
        gate_wt=flat(L0_ffn_gate_weight.T),
        wg_t=flat(L0_ffn_Wg.transpose(0, 2, 1)),
        wu_t=flat(L0_ffn_Wu.transpose(0, 2, 1)),
        wd_t=flat(L0_ffn_Wd.transpose(0, 2, 1)),
        wsg_t=flat(L0_ffn_Ws_g.T),
        wsu_t=flat(L0_ffn_Ws_u.T),
        wsd_t=flat(L0_ffn_Ws_d.T),
    )
    nc = _bacc.Bacc("TRN2", target_bir_lowering=False, num_devices=1)
    arrays, A = {}, {}
    for name, a in laid.items():
        arrays[f"in_{name}_dram"] = a
        A[name] = nc.dram_tensor(f"in_{name}_dram", a.shape, _mybir.dt.from_np(a.dtype), kind="ExternalInput").ap()
    out = nc.dram_tensor("out_0_dram", (BATCH, SEQ, D), F32, kind="ExternalOutput").ap()
    build(nc, A, out.rearrange("b t e -> (b t) e"))
    r = _run(nc, [arrays], core_ids=[0])
    return r.results[0]["out_0_dram"]
```

```python
from contextlib import ExitStack

import concourse.bass as bass
from concourse import mybir

F32 = mybir.dt.float32
BF16 = mybir.dt.bfloat16
I16 = mybir.dt.int16
I32 = mybir.dt.int32
F32R = mybir.dt.float32r
ALU = mybir.AluOpType
ACT = mybir.ActivationFunctionType
AX = mybir.AxisListType
RMAX = bass.bass_isa.ReduceOp.max

BATCH, CHAN, IMG, PATCH, D = 64, 12, 224, 16, 192
GRID = IMG // PATCH
NPATCH = GRID * GRID
NTXT = 32
SEQ = NPATCH + NTXT
NTOK = BATCH * SEQ
HALF = SEQ // 2
REST = NPATCH - HALF
PAIR = 2 * SEQ
NPAIR = BATCH // 2
HEADS, DH = 12, 16
KC, KP = 2, 96
QUAD, QT, QP = BATCH // 4, 7, 112
QMAX = 127.0
TINY = 1e-8
EPS = 1e-5

(S_W, S_WO, S_Q, S_K, S_V, C_Q, C_K, C_V, C_X, S_X, C_S, S_S, S_SV, NEG_SS, X1, X2, X3, C_A, S_CTX, C_CTX,
 S_Y, C_Y, S_RN, U_S, U_CTX, U_Y, TMP0, TMP1, TMP2, TMP3, MSUM) = range(31)
NSCAL = 32


def sliding(i, s, g, groups):
    return (i, s, g) if g < groups else (i + s, 1 - s, g - groups)


def turns(engine, pairs, step):
    step(0, 0, True, False)
    with engine.Fori(0, pairs // 2 - 1) as i:
        step(i, 1, False, False)
        step(i + 1, 0, False, False)
    step(pairs // 2 - 1, 1, False, True)


class Share:

    def __init__(self, members, groups):
        self.members, self.groups = members, groups

    def __contains__(self, g):
        return g in self.members

    def done(self, n, g):
        q, r = divmod(g, self.groups)
        return len(self.members) * (n + q + 1) + sum(m <= r for m in self.members)




class Kit:

    def __init__(self, nc, ctx):
        self.nc, self.ctx = nc, ctx
        self.used = []

    def sb(self, ctx, name, shape, dt):
        return ctx.enter_context(self.nc.sbuf_tensor(name, shape, dt))

    def ps(self, ctx, name, shape, dt=F32):
        return ctx.enter_context(self.nc.psum_tensor(name, shape, dt))

    def sem(self, ctx, name):
        self.used.append(ctx.enter_context(self.nc.semaphore(name)))
        return self.used[-1]

    def clear_semaphores(self):
        with self.nc.Block() as block:
            @block.sync
            def _(sp):
                for sem in self.used:
                    sp.sem_clear(sem)
        self.used = []


def quant_scalars(v, scal, raw_max, unit, scale, factor):
    def col(k):
        return scal[:, k:k + 1]
    v.drain()
    v.tensor_scalar(col(TMP0), raw_max, 1.0 if unit is None else col(unit), TINY, ALU.mult, ALU.max)
    v.drain()
    v.tensor_scalar(col(scale), col(TMP0), 1.0 / QMAX, None, ALU.mult)
    v.drain()
    v.reciprocal(col(TMP1), col(scale))
    v.drain()
    v.tensor_scalar(col(factor), col(TMP1), 1.0 if unit is None else col(unit), None, ALU.mult)
    v.drain()


def setup_phase(kit, w_in_t, w_out_t):
    nc = kit.nc
    with ExitStack() as ctx:
        wraw = kit.sb(ctx, "w_in_raw", [128, KC, 3 * D], F32)
        wint = kit.sb(ctx, "w_in_int16", [128, KC, 3 * D], I16)
        woraw = kit.sb(ctx, "w_out_raw", [128, 3, D], F32)
        woint = kit.sb(ctx, "w_out_int16", [128, 3, D], I16)
        wmax = kit.sb(ctx, "w_max", [128, 2], F32)
        gmax = kit.sb(ctx, "w_max_all", [128, 2], F32)
        zeroed = kit.sem(ctx, "setup_zeroed")
        loaded = kit.sem(ctx, "setup_loaded")
        wmax_ready = kit.sem(ctx, "wmax_ready")
        gmax_ready = kit.sem(ctx, "gmax_ready")
        ident_zero = kit.sem(ctx, "ident_zero")
        block = ctx.enter_context(nc.Block())

        @block.sync
        def _(sp):
            sp.wait_ge(zeroed, 2)
            sp.dma_start(wraw[0:KP], w_in_t.rearrange("(c p) e -> p c e", p=KP)).then_inc(loaded, 16)
            for j in range(4):
                src = w_out_t.rearrange("(c j d) o -> j d c o", c=3, j=4)[j]
                sp.dma_start(woraw[32 * j:32 * j + DH], src).then_inc(loaded, 16)

        @block.gpsimd
        def _(pool):
            nc.gpsimd.memset(kit.ident[:], 0.0).then_inc(ident_zero, 1)
            pool.wait_ge(ident_zero, 1)
            nc.gpsimd.affine_select(out=kit.ident[:], in_=kit.ident[:], compare_op=ALU.not_equal, fill=1.0,
                                    base=0, pattern=[[-1, 128]], channel_multiplier=1).then_inc(ident_zero, 1)
            nc.gpsimd.memset(kit.identb[:], 0.0).then_inc(ident_zero, 1)
            pool.wait_ge(ident_zero, 3)
            nc.gpsimd.affine_select(out=kit.identb[:], in_=kit.identb[:], compare_op=ALU.not_equal, fill=1.0,
                                    base=0, pattern=[[-1, 128]], channel_multiplier=1).then_inc(ident_zero, 1)
            pool.wait_ge(wmax_ready, 1)
            nc.gpsimd.partition_all_reduce(gmax[:], wmax[:], 128, RMAX).then_inc(gmax_ready, 1)
            pool.wait_ge(ident_zero, 4)

        @block.vector
        def _(v):
            nc.vector.memset(wraw[:], 0.0).then_inc(zeroed, 1)
            nc.vector.memset(woraw[:], 0.0).then_inc(zeroed, 1)
            v.wait_ge(loaded, 80)
            v.tensor_reduce(wmax[:, 0:1], wraw[:], AX.XY, ALU.max, apply_absolute_value=True)
            v.tensor_reduce(wmax[:, 1:2], woraw[:], AX.XY, ALU.max, apply_absolute_value=True).then_inc(wmax_ready, 1)
            v.wait_ge(gmax_ready, 1)
            quant_scalars(v, kit.scal, gmax[:, 0:1], None, S_W, TMP2)
            v.tensor_scalar(wint[:], wraw[:], kit.scal[:, TMP2:TMP2 + 1], None, ALU.mult)
            quant_scalars(v, kit.scal, gmax[:, 1:2], None, S_WO, TMP2)
            v.tensor_scalar(woint[:], woraw[:], kit.scal[:, TMP2:TMP2 + 1], None, ALU.mult)
            v.drain()
            v.tensor_copy(kit.w_in[:], wint[:])
            v.tensor_copy(kit.w_out[:], woint[:])


def tokenize_phase(kit, patches, txt, chan_w, h_d, qk_d, v_d, xt_d):
    nc = kit.nc
    with ExitStack() as ctx:
        xin = kit.sb(ctx, "patch_in", [QP, QT, CHAN * 256], F32)
        pooled = [kit.sb(ctx, f"pooled{b}", [QP, QT, CHAN], F32) for b in range(2)]
        pooled_t = kit.sb(ctx, "pooled_t", [CHAN, QT * QP], F32)
        cw = kit.sb(ctx, "chan_weights", [CHAN, D], F32)
        w_in = kit.sb(ctx, "w_in_f32", [128, KC, 3 * D], F32)
        h = [kit.sb(ctx, f"h{s}", [HALF, 4, D], F32) for s in range(2)]
        xn = [kit.sb(ctx, f"xn{s}", [HALF, 4, D], F32) for s in range(2)]
        xt = [kit.sb(ctx, f"xt{s}", [KP, KC, PAIR], F32) for s in range(2)]
        qk = [kit.sb(ctx, f"qk{s}", [KP, 4, PAIR], F32) for s in range(2)]
        vv = [kit.sb(ctx, f"vv{s}", [HALF, 4, D], F32) for s in range(2)]
        stats = [kit.sb(ctx, f"stats{s}", [HALF, 4, 6], F32) for s in range(2)]
        mv = [kit.sb(ctx, f"mv{s}", [HALF, 4, 2], F32) for s in range(2)]
        ve = [kit.sb(ctx, f"ve{s}", [HALF, 4], F32) for s in range(2)]
        sd = [kit.sb(ctx, f"sd{s}", [HALF, 4], F32) for s in range(2)]
        r0 = kit.sb(ctx, "r0", [HALF, 4], F32)
        r1 = kit.sb(ctx, "r1", [HALF, 4], F32)
        rstd = kit.sb(ctx, "rstd", [HALF, 4], F32)
        mx = kit.sb(ctx, "mx", [128, 4, NPAIR], F32)
        mx4 = kit.sb(ctx, "mx4", [128, 4], F32)
        gmx = kit.sb(ctx, "gmx", [128, 4], F32)
        pt_ps = kit.ps(ctx, "pt_ps", [CHAN, 2, 512])
        h_ps = kit.ps(ctx, "h_ps", [HALF, 2, 512])
        xt_ps = kit.ps(ctx, "xt_ps", [KP, 2, 512])
        qv_ps = kit.ps(ctx, "qv_ps", [HALF, 2, 512])

        sem = lambda name: kit.sem(ctx, name)
        x_in = [sem(f"x_in{t}") for t in range(QT)]
        pooled_ready = sem("pooled_ready")
        pt_ready = sem("pt_ready")
        pt_copied = sem("pt_copied")
        w_loaded, w_ready = sem("w_loaded"), sem("w_ready")
        h_mixed = sem("h_mixed")
        h_copied = sem("h_copied")
        txt_in = [sem(f"txt_in{s}") for s in range(2)]
        var_ready, sd_ready = sem("var_ready"), sem("sd_ready")
        xn_ready = sem("xn_ready")
        xt_ready = sem("xt_ready")
        xt_copied = sem("xt_copied")
        qv_ready = sem("qv_ready")
        qv_copied = sem("qv_copied")
        maxed = sem("maxed")
        h_out, xt_out, qk_out, v_out = [[sem(f"{n}_out{s}") for s in range(2)] for n in ("h", "xt", "qk", "v")]
        mx_ready, gmx_ready = sem("mx_ready"), sem("gmx_ready")
        block = ctx.enter_context(nc.Block())

        patch_tiles = patches.rearrange("(q t p) x -> t q p x", t=QT, p=QP)
        txt_pairs = txt.rearrange("(i s m) t e -> s i t m e", s=2, m=2)
        rows = lambda a: a.rearrange("(i s m t) e -> s i t m e", s=2, m=4, t=HALF)
        cols = lambda a: a.rearrange("(m p) (i s t) -> s i p m t", p=KP, s=2, t=PAIR)

        @block.sync
        def _(sp):
            sp.dma_start(cw[:], chan_w).then_inc(w_loaded, 16)
            with sp.Fori(0, QUAD) as i:
                for t in range(QT):
                    sp.wait_ge(pooled_ready, QT * i + t + 1)
                    sp.dma_start(xin[:, t], patch_tiles[t][i]).then_inc(x_in[t], 16)

        @block.gpsimd
        def _(pool):
            pool.wait_ge(mx_ready, 1)
            nc.gpsimd.partition_all_reduce(gmx[:], mx4[:], 128, RMAX).then_inc(gmx_ready, 1)

        @block.vector
        def _(v):
            v.sem_inc(pooled_ready, QT)
            v.sem_inc(xn_ready, 2)
            v.sem_inc(maxed, 2)
            nc.vector.memset(mx[:], 0.0)
            v.tensor_copy(w_in[0:KP], kit.w_in[0:KP]).then_inc(w_ready, 1)

            def pool_tile(q, odd, t):
                v.wait_ge(x_in[t], 16 * q + 16)
                if t == 0:
                    v.wait_ge(pt_ready, q + 1)
                v.tensor_reduce(pooled[odd][:, t], xin[:, t].rearrange("p (c x) -> p c x", c=CHAN), AX.X, ALU.add)\
                    .then_inc(pooled_ready, 1)

            def norm_stats(i, s):
                v.wait_ge(h_copied, 2 * i + s + 2)
                v.wait_ge(txt_in[s], 16 * i + 16)
                for m in range(4):
                    v.bn_stats(stats[s][:, m], h[s][:, m])
                v.drain()
                for m in range(4):
                    v.bn_aggr(mv[s][:, m], stats[s][:, m])
                v.drain()
                v.tensor_scalar(ve[s][:], mv[s][:, :, 1], EPS, None, ALU.add).then_inc(var_ready, 1)

            def norm_rows(i, s):
                v.wait_ge(sd_ready, 2 * i + s + 1)
                v.reciprocal(r0[:], sd[s][:])
                v.drain()
                v.tensor_tensor(r1[:], r0[:], r0[:], ALU.mult)
                v.drain()
                v.tensor_tensor(r1[:], r1[:], ve[s][:], ALU.mult)
                v.drain()
                v.tensor_scalar(r1[:], r1[:], -0.5, 1.5, ALU.mult, ALU.add)
                v.drain()
                v.tensor_tensor(rstd[:], r0[:], r1[:], ALU.mult)
                v.drain()
                v.wait_ge(xt_ready, 2 * i + s + 1)
                for m in range(4):
                    ins = v.tensor_scalar(xn[s][:, m], h[s][:, m], mv[s][:, m, 0:1], rstd[:, m:m + 1],
                                          ALU.subtract, ALU.mult)
                ins.then_inc(xn_ready, 1)

            def maxima(i, s):
                def col(k, p):
                    return mx[0:p, k].rearrange("p (i s) -> p s i", s=2)[:, s, bass.ds(i, 1)]
                v.wait_ge(qv_copied, 6 * (2 * i + s) + 6 + 2)
                v.tensor_reduce(col(0, KP), qk[s][:, 0:2], AX.XY, ALU.max, apply_absolute_value=True)
                v.tensor_reduce(col(1, KP), qk[s][:, 2:4], AX.XY, ALU.max, apply_absolute_value=True)
                v.tensor_reduce(col(2, HALF), vv[s][:], AX.XY, ALU.max, apply_absolute_value=True)
                v.tensor_reduce(col(3, HALF), xn[s][:], AX.XY, ALU.max, apply_absolute_value=True).then_inc(maxed, 1)

            for t in range(QT):
                pool_tile(0, 0, t)

            def turn(i, odd, first, last):
                def pool_next(*tiles):
                    for t in tiles if not last else ():
                        pool_tile(i + 1, 1 - odd, t)
                pool_next(0, 1, 2)
                if not first:
                    maxima(i - 1, 0)
                pool_next(3)
                norm_stats(i, 0)
                norm_stats(i, 1)
                if not first:
                    maxima(i - 1, 1)
                pool_next(4)
                norm_rows(i, 0)
                pool_next(5, 6)
                norm_rows(i, 1)

            turn(0, 0, True, False)
            with v.Fori(0, QUAD // 2 - 1) as j:
                turn(2 * j + 1, 1, False, False)
                turn(2 * j + 2, 0, False, False)
            turn(QUAD - 1, 1, False, True)
            maxima(QUAD - 1, 0)
            maxima(QUAD - 1, 1)
            v.drain()
            v.tensor_reduce(mx4[:], mx[:], AX.X, ALU.max).then_inc(mx_ready, 1)
            v.wait_ge(gmx_ready, 1)
            for k, (unit, scale, factor) in enumerate([(S_W, S_Q, C_Q), (S_W, S_K, C_K), (S_W, S_V, C_V),
                                                       (None, S_X, C_X)]):
                quant_scalars(v, kit.scal, gmx[:, k:k + 1], unit, scale, factor)

        @block.tensor
        def _(pe):
            def transpose_pooled(q, odd):
                pe.wait_ge(pt_copied, q + 1)
                for t in range(QT):
                    pe.wait_ge(pooled_ready, QT * q + t + 1 + QT)
                    mm = pe.transpose(pt_ps[:, t // 4, t % 4 * QP:t % 4 * QP + QP], pooled[odd][:, t],
                                      kit.ident[0:QP, 0:QP])
                mm.then_inc(pt_ready, 1)

            def mix(i, s):
                pe.wait_ge(pt_copied, i + 2)
                pe.wait_ge(h_copied, 2 * i + s + 1)
                for m in range(4):
                    a = NPATCH * (2 * s + m // 2) + HALF * (m % 2)
                    k = REST if m % 2 else HALF
                    mm = pe.matmul(h_ps[0:k, m // 2, m % 2 * D:m % 2 * D + D], pooled_t[:, a:a + k], cw[:],
                                   start=True, stop=True)
                mm.then_inc(h_mixed, 1)

            def transpose_x(i, s):
                pe.wait_ge(xn_ready, 2 * i + s + 1 + 2)
                pe.wait_ge(xt_copied, 2 * i + s + 1)
                for m in range(4):
                    for c in range(KC):
                        mm = pe.transpose(xt_ps[:, c, m * HALF:m * HALF + HALF], xn[s][:, m, c * KP:c * KP + KP],
                                          kit.ident[0:HALF, 0:HALF])
                mm.then_inc(xt_ready, 1)

            def project_qk(i, s):
                use = 6 * (2 * i + s)
                pe.wait_ge(xt_copied, 2 * i + s + 1 + 1)
                for m in range(4):
                    pe.wait_ge(qv_copied, use + m + 1)
                    for c in range(KC):
                        mm = pe.matmul(qv_ps[0:KP, m % 2, 0:PAIR], w_in[0:KP, c, m * KP:m * KP + KP], xt[s][:, c],
                                       start=(c == 0), stop=(c == KC - 1))
                    mm.then_inc(qv_ready, 1)

            def project_v(i, s):
                use = 6 * (2 * i + s)
                for m in range(4):
                    if m % 2 == 0:
                        pe.wait_ge(qv_copied, use + 4 + m // 2 + 1)
                    for c in range(KC):
                        mm = pe.matmul(qv_ps[:, m // 2, m % 2 * D:m % 2 * D + D],
                                       xt[s][:, c, m * HALF:m * HALF + HALF],
                                       w_in[0:KP, c, 2 * D:3 * D], start=(c == 0), stop=(c == KC - 1))
                    if m % 2:
                        mm.then_inc(qv_ready, 1)

            def turn(i, odd, more=True):
                transpose_x(i, 0)
                project_qk(i, 0)
                project_v(i, 0)
                transpose_x(i, 1)
                if more:
                    transpose_pooled(i + 1, 1 - odd)
                project_qk(i, 1)
                if more:
                    mix(i + 1, 0)
                project_v(i, 1)
                if more:
                    mix(i + 1, 1)

            pe.sem_inc(pt_ready, 2)
            pe.sem_inc(xt_ready, 2)
            pe.wait_ge(w_loaded, 16)
            pe.wait_ge(w_ready, 1)
            transpose_pooled(0, 0)
            mix(0, 0)
            mix(0, 1)
            turn(0, 0)
            with pe.Fori(0, QUAD // 2 - 1) as j:
                turn(2 * j + 1, 1)
                turn(2 * j + 2, 0)
            turn(QUAD - 1, 1, False)

        @block.scalar
        def _(act):
            def copy_pooled(q):
                act.wait_ge(pt_ready, q + 1 + 2)
                act.copy(pooled_t[:, 0:4 * QP], pt_ps[:, 0, 0:4 * QP])
                act.copy(pooled_t[:, 4 * QP:], pt_ps[:, 1, 0:3 * QP]).then_inc(pt_copied, 1)

            def load_text(i, s):
                act.wait_ge(h_out[s], 16 * i + 16)
                act.wait_ge(xn_ready, 2 * i + s + 1)
                act.dma_start(h[s][REST:HALF, 1:4:2], txt_pairs[s][i]).then_inc(txt_in[s], 16)

            def copy_h(i, s):
                n = 2 * i + s
                act.wait_ge(h_mixed, n + 1)
                hp = h_ps[:, :, 0:2 * D].rearrange("p b (m e) -> p b m e", m=2)
                act.copy(h[s][:, 0:4:2], hp[:, :, 0])
                act.copy(h[s][0:REST, 1:4:2], hp[0:REST, :, 1]).then_inc(h_copied, 1)

            def store_h(i, s):
                act.wait_ge(h_copied, 2 * i + s + 2)
                act.wait_ge(txt_in[s], 16 * i + 16)
                act.dma_start(rows(h_d)[s][i], h[s][:]).then_inc(h_out[s], 16)

            def root(i, s):
                act.wait_ge(var_ready, 2 * i + s + 1)
                act.activation(sd[s][:], ve[s][:], ACT.Sqrt).then_inc(sd_ready, 1)

            def copy_xt(i, s):
                act.wait_ge(xt_ready, 2 * i + s + 1 + 2)
                act.wait_ge(xt_out[s], 16 * i + 16)
                act.copy(xt[s][:, 0], xt_ps[:, 0, 0:PAIR])
                act.copy(xt[s][:, 1], xt_ps[:, 1, 0:PAIR]).then_inc(xt_copied, 1)
                act.wait_ge(xt_copied, 2 * i + s + 2)
                act.dma_start(cols(xt_d)[s][i], xt[s][:]).then_inc(xt_out[s], 16)

            def copy_qk(i, s):
                n = 2 * i + s
                act.wait_ge(maxed, n + 1)
                act.wait_ge(qk_out[s], 16 * i + 16)
                for m in range(4):
                    act.wait_ge(qv_ready, 6 * n + m + 1)
                    act.copy(qk[s][:, m], qv_ps[0:KP, m % 2, 0:PAIR]).then_inc(qv_copied, 1)
                act.wait_ge(qv_copied, 6 * n + 4 + 2)
                act.dma_start(cols(qk_d)[s][i], qk[s][:]).then_inc(qk_out[s], 16)

            def copy_v(i, s):
                n = 2 * i + s
                act.wait_ge(v_out[s], 16 * i + 16)
                for m in range(2):
                    act.wait_ge(qv_ready, 6 * n + 4 + m + 1)
                    act.copy(vv[s][:, 2 * m:2 * m + 2].rearrange("p m e -> p (m e)"), qv_ps[:, m, 0:2 * D])\
                        .then_inc(qv_copied, 1)
                act.wait_ge(qv_copied, 6 * n + 6 + 2)
                act.dma_start(rows(v_d)[s][i], vv[s][:]).then_inc(v_out[s], 16)

            def turn(i, more=True):
                root(i, 0)
                root(i, 1)
                store_h(i, 0)
                store_h(i, 1)
                copy_xt(i, 0)
                copy_qk(i, 0)
                copy_v(i, 0)
                copy_xt(i, 1)
                if more:
                    load_text(i + 1, 0)
                    load_text(i + 1, 1)
                    copy_pooled(i + 1)
                copy_qk(i, 1)
                if more:
                    copy_h(i + 1, 0)
                copy_v(i, 1)
                if more:
                    copy_h(i + 1, 1)

            for o in (h_out, xt_out, qk_out, v_out):
                for s in range(2):
                    act.sem_inc(o[s], 16)
            act.sem_inc(pt_copied, 1)
            act.sem_inc(h_copied, 1)
            act.sem_inc(xt_copied, 1)
            act.sem_inc(qv_copied, 2)
            load_text(0, 0)
            load_text(0, 1)
            copy_pooled(0)
            copy_h(0, 0)
            copy_h(0, 1)
            with act.Fori(0, QUAD - 1) as i:
                turn(i)
            turn(QUAD - 1, False)
            for o in (h_out, xt_out, qk_out, v_out):
                for s in range(2):
                    act.wait_ge(o[s], 16 * (QUAD + 1))


def score_range_phase(kit, qk_d, v_d, qb_d, kb_d, vb_d, mneg_d):
    nc = kit.nc
    W3 = 3 * PAIR
    with ExitStack() as ctx:
        qf = [kit.sb(ctx, f"qf{s}", [128, 3, PAIR], F32) for s in range(2)]
        kf = [kit.sb(ctx, f"kf{s}", [128, 3, PAIR], F32) for s in range(2)]
        vf = [kit.sb(ctx, f"vf{s}", [HALF, 4, D], F32) for s in range(2)]
        q16 = kit.sb(ctx, "q16", [128, 3, PAIR], I16)
        k16 = kit.sb(ctx, "k16", [128, 3, PAIR], I16)
        v16 = kit.sb(ctx, "v16", [HALF, 4, D], I16)
        qb = [kit.sb(ctx, f"qb{s}", [128, 3, PAIR], BF16) for s in range(2)]
        kb = [kit.sb(ctx, f"kb{s}", [128, 3, PAIR], BF16) for s in range(2)]
        vb = [kit.sb(ctx, f"vb{s}", [HALF, 4, HEADS, 32], BF16) for s in range(2)]
        rowmax = kit.sb(ctx, "rowmax", [HALF, NPAIR, 3, 4, 2, 2], F32)
        absmax = kit.sb(ctx, "absmax", [HALF, NPAIR, 3, 4, 2, 2], F32)
        amax1 = kit.sb(ctx, "amax1", [128, 1], F32)
        gamax = kit.sb(ctx, "gamax", [128, 1], F32)
        xb = kit.sb(ctx, "xb", [128, 3], BF16)
        m16 = kit.sb(ctx, "m16", [HALF, NPAIR * 48], I16)
        mb = kit.sb(ctx, "mb", [HALF, NPAIR * 48], BF16)
        mt = kit.sb(ctx, "mt", [48, NPAIR, HALF], BF16)
        xrow = kit.sb(ctx, "xrow", [NPAIR, 3, W3], BF16)
        sem = lambda name: kit.sem(ctx, name)
        qk_in, v_in, qkv_out = [[sem(f"{n}{s}") for s in range(2)] for n in ("qk_in", "v_in", "qkv_out")]
        zeroed, pool_turn = sem("zeroed"), sem("pool_turn")
        rounded = sem("rounded")
        cast = sem("cast")
        scored = sem("scored")
        s_ready = sem("s_ready")
        s_used = sem("s_used")
        amax_ready, gamax_ready, mb_ready, mt_psum, mt_ready, mt_out, pads_out, xrow_ready = [sem(n) for n in (
            "amax_ready", "gamax_ready", "mb_ready", "mt_psum", "mt_ready", "mt_out", "pads_out", "xrow_ready")]
        with ExitStack() as pctx:
            s_ps = [kit.ps(pctx, f"s_ps{b}", [HALF, 4, 512]) for b in range(2)]
            block = pctx.enter_context(nc.Block())

            heads = qk_d.rearrange("(w c j d) (i s t) -> w j s i d c t", w=2, c=3, j=4, s=2, t=PAIR)
            vrows = v_d.rearrange("(i s m t) e -> s i t m e", s=2, m=4, t=HALF)
            by_pair = lambda a: a.rearrange("(i s) p x -> s i p x", s=2)

            @block.sync
            def _(sp):
                def load(i, s):
                    sp.wait_ge(rounded, 3 * (2 * i + s) + 3)
                    for w, dst in enumerate((qf, kf)):
                        for j in range(4):
                            sp.dma_start(dst[s][32 * j:32 * j + DH], heads[w, j, s][i]).then_inc(qk_in[s], 16)
                    sp.dma_start(vf[s][:], vrows[s][i]).then_inc(v_in[s], 16)

                def store(i, s):
                    sp.wait_ge(cast, 3 * (2 * i + s) + 3 + 3)
                    sp.dma_start(by_pair(qb_d)[s][i], qb[s][:].rearrange("p c t -> p (c t)")).then_inc(qkv_out[s], 16)
                    sp.dma_start(by_pair(kb_d)[s][i], kb[s][:].rearrange("p c t -> p (c t)")).then_inc(qkv_out[s], 16)
                    sp.dma_start(by_pair(vb_d)[s][i], vb[s][:].rearrange("p m h d -> p (m h d)"))\
                        .then_inc(qkv_out[s], 16)

                for s in range(2):
                    sp.sem_inc(qkv_out[s], 48)
                sp.wait_ge(zeroed, 4)
                load(0, 0)
                with sp.Fori(0, NPAIR // 2 - 1) as i:
                    load(i, 1)
                    store(i, 0)
                    load(i + 1, 0)
                    store(i, 1)
                load(NPAIR // 2 - 1, 1)
                store(NPAIR // 2 - 1, 0)
                store(NPAIR // 2 - 1, 1)
                for s in range(2):
                    sp.wait_ge(qkv_out[s], 48 * (NPAIR // 2 + 1))

            @block.scalar
            def _(act):
                act.sem_inc(rounded, 6)
                sc = lambda k, p=128: kit.scal[0:p, k:k + 1]
                with act.Fori(0, NPAIR // 2) as i:
                    for s in range(2):
                        n = 2 * i + s
                        act.wait_ge(qk_in[s], 128 * i + 128)
                        act.wait_ge(cast, 3 * n + 1)
                        act.activation(q16[:], qf[s][:], ACT.Copy, scale=sc(C_Q)).then_inc(rounded, 1)
                        act.wait_ge(cast, 3 * n + 2)
                        act.activation(k16[:], kf[s][:], ACT.Copy, scale=sc(C_K)).then_inc(rounded, 1)
                        act.wait_ge(v_in[s], 16 * i + 16)
                        act.wait_ge(cast, 3 * n + 3)
                        act.activation(v16[:], vf[s][:], ACT.Copy, scale=sc(C_V, HALF)).then_inc(rounded, 1)

            @block.gpsimd
            def _(pool):
                pool.sem_inc(cast, 3)
                pool.wait_ge(zeroed, 6)
                with pool.Fori(0, NPAIR // 2) as i:
                    for s in range(2):
                        n = 2 * i + s
                        pool.wait_ge(scored, n + 1)
                        pool.wait_ge(qkv_out[s], 48 * i + 48)
                        pool.wait_ge(rounded, 3 * n + 1 + 6)
                        pool.sem_inc(pool_turn, 1)
                        nc.gpsimd.tensor_copy(qb[s][:], q16[:]).then_inc(cast, 1)
                        pool.wait_ge(rounded, 3 * n + 2 + 6)
                        pool.sem_inc(pool_turn, 1)
                        nc.gpsimd.tensor_copy(kb[s][:], k16[:]).then_inc(cast, 1)
                        pool.wait_ge(rounded, 3 * n + 3 + 6)
                        pool.sem_inc(pool_turn, 1)
                        nc.gpsimd.tensor_copy(vb[s][:, :, :, 0:DH],
                                              v16[:].rearrange("p m (h d) -> p m h d", h=HEADS)).then_inc(cast, 1)

            @block.tensor
            def _(pe):
                pe.sem_inc(scored, 2)
                with pe.Fori(0, NPAIR // 2) as i:
                    for s in range(2):
                        n = 2 * i + s
                        pe.wait_ge(cast, 3 * n + 2 + 3)
                        for g in range(6):
                            m, c = g // 3, g % 3
                            pe.wait_ge(s_used, 6 * n + g + 1)
                            for half in range(2):
                                for j in range(4):
                                    r = slice(32 * j, 32 * j + DH)
                                    a = m * SEQ + half * HALF
                                    mm = pe.matmul(s_ps[g % 2][:, j, half * SEQ:half * SEQ + SEQ], qb[s][r, c, a:a + HALF],
                                                   kb[s][r, c, m * SEQ:m * SEQ + SEQ], start=True, stop=True)
                            mm.then_inc(s_ready, 1)
                        pe.wait_ge(s_ready, 6 * n + 6)
                        pe.sem_inc(scored, 1)

            @block.vector
            def _(v):
                for t in (qf, kf, vb):
                    for s in range(2):
                        nc.vector.memset(t[s][:], 0.0).then_inc(zeroed, 1)
                v.sem_inc(s_used, 2)
                with v.Fori(0, NPAIR // 2) as i:
                    for s in range(2):
                        for g in range(6):
                            m, c = g // 3, g % 3
                            v.wait_ge(s_ready, 6 * (2 * i + s) + g + 1)
                            src = s_ps[g % 2][:, :, 0:PAIR].rearrange("p j (h k) -> p j h k", h=2)
                            out = [t[:].rearrange("p (i s) c j m h -> p s c m i j h", s=2)[:, s, c, m][:, bass.ds(i, 1)]
                                   for t in (rowmax, absmax)]
                            v.tensor_reduce(out[0], src, AX.X, ALU.max)
                            v.tensor_reduce(out[1], src, AX.X, ALU.max, apply_absolute_value=True).then_inc(s_used, 1)

        with ExitStack() as pctx:
            mt_ps = [kit.ps(pctx, f"mt_ps{b}", [48, 1024], BF16) for b in range(4)]
            block = pctx.enter_context(nc.Block())

            @block.gpsimd
            def _(pool):
                pool.wait_ge(amax_ready, 1)
                nc.gpsimd.partition_all_reduce(gamax[:], amax1[:], 128, RMAX).then_inc(gamax_ready, 1)

            @block.vector
            def _(v):
                sc = lambda k, p=128: kit.scal[0:p, k:k + 1]
                nc.vector.memset(amax1[:], 0.0)
                nc.vector.memset(xrow[:], 1.0)
                v.drain()
                v.tensor_reduce(amax1[0:HALF], absmax[:].rearrange("p n c j m h -> p (n c j m h)"), AX.X, ALU.max)\
                    .then_inc(amax_ready, 1)
                v.tensor_tensor(sc(U_S), sc(S_Q), sc(S_K), ALU.mult)
                v.drain()
                v.tensor_scalar(sc(U_S), sc(U_S), 0.25, None, ALU.mult)
                v.wait_ge(gamax_ready, 1)
                quant_scalars(v, kit.scal, gamax[:], U_S, S_S, C_S)
                v.tensor_scalar(sc(TMP0), sc(C_S), -1.0, None, ALU.mult)
                v.reciprocal(sc(TMP1), sc(C_S))
                v.drain()
                v.tensor_scalar(m16[:], rowmax[:].rearrange("p n c j m h -> p (n c j m h)"), sc(TMP0, HALF), None,
                                ALU.mult)
                v.drain()
                v.tensor_copy(mb[:], m16[:]).then_inc(mb_ready, 1)
                for k in range(3):
                    v.drain()
                    v.tensor_copy(xb[:, k:k + 1], sc(TMP1))
                    v.drain()
                    v.tensor_copy(sc(TMP2), xb[:, k:k + 1])
                    v.drain()
                    v.tensor_tensor(sc(TMP1), sc(TMP1), sc(TMP2), ALU.subtract)
                    v.tensor_scalar(xrow[:, k], xrow[:, k], sc(TMP2, NPAIR), None, ALU.mult).then_inc(xrow_ready, 1)
                for b in range(4):
                    v.wait_ge(mt_psum, b + 1)
                    v.tensor_copy(mt[:, 8 * b:8 * b + 8].rearrange("p n t -> p (n t)"), mt_ps[b][:, 0:8 * HALF])\
                        .then_inc(mt_ready, 1)

            @block.tensor
            def _(pe):
                pe.wait_ge(mb_ready, 1)
                for n in range(NPAIR):
                    mm = pe.transpose(mt_ps[n // 8][:, n % 8 * HALF:n % 8 * HALF + HALF], mb[:, 48 * n:48 * n + 48],
                                      kit.identb[0:HALF, 0:HALF])
                    if n % 8 == 7:
                        mm.then_inc(mt_psum, 1)

            @block.sync
            def _(sp):
                sp.wait_ge(mt_ready, 4)
                sp.dma_start(mneg_d.rearrange("n a t -> a n t"), mt[:]).then_inc(mt_out, 16)
                sp.wait_ge(mt_out, 16)
                for j in range(4):
                    src = mneg_d.rearrange("n (c j a) t -> j n c (a t)", c=3, j=4)[j]
                    for r in range(3):
                        sp.dma_start(qb_d[:, 32 * j + DH + r].rearrange("n (c t) -> n c t", c=3), src)\
                            .then_inc(pads_out, 16)
                sp.wait_ge(xrow_ready, 3)
                for j in range(4):
                    sp.dma_start(kb_d[:, 32 * j + DH:32 * j + DH + 3], xrow[:]).then_inc(pads_out, 16)
                sp.wait_ge(pads_out, 16 * 16)


def row_sum_phase(kit, qb_d, kb_d, r_d):
    nc = kit.nc
    GROUPS = 6
    by_act, by_dve = Share((0, 1, 3, 4), GROUPS), Share((2, 5), GROUPS)
    with ExitStack() as ctx:
        qb = [kit.sb(ctx, f"rs_qb{s}", [128, 3, PAIR], BF16) for s in range(2)]
        kb = [kit.sb(ctx, f"rs_kb{s}", [128, 3, PAIR], BF16) for s in range(2)]
        t16 = [kit.sb(ctx, f"rs_t{b}", [HALF, 4, PAIR], I16) for b in range(6)]
        e32 = [kit.sb(ctx, f"rs_e{b}", [HALF, 4, PAIR], F32) for b in range(3)]
        rowsum = kit.sb(ctx, "rowsum", [HALF, NPAIR, 3, 4, 2, 2], F32)
        rinv = kit.sb(ctx, "rinv", [HALF, NPAIR * 48], F32)
        pmax1 = kit.sb(ctx, "pmax1", [128, 1], F32)
        pmax = kit.sb(ctx, "pmax", [128, 1], F32)
        rt = kit.sb(ctx, "rt", [48, NPAIR, HALF], F32)
        sem = lambda name: kit.sem(ctx, name)
        qk_in = [sem(f"rs_qk_in{s}") for s in range(2)]
        scored = sem("rs_scored")
        s_ready = sem("rs_s_ready")
        act_rounded = sem("act_rounded")
        dve_rounded = sem("dve_rounded")
        exped = sem("exped")
        summed = sem("summed")
        pmax_ready, pmax_all, r_ready, rt_psum, rt_ready, rt_out = [sem(n) for n in (
            "pmax_ready", "pmax_all", "r_ready", "rt_psum", "rt_ready", "rt_out")]

        def wait_rounded(eng, n, g):
            share, done = (by_act, act_rounded) if g % GROUPS in by_act else (by_dve, dve_rounded)
            eng.wait_ge(done, share.done(n, g))

        with ExitStack() as pctx:
            s_ps = [kit.ps(pctx, f"rs_s_ps{b}", [HALF, 4, 512]) for b in range(2)]
            block = pctx.enter_context(nc.Block())
            by_pair = lambda a: a.rearrange("(i s) p x -> s i p x", s=2)

            @block.sync
            def _(sp):
                with sp.Fori(0, NPAIR // 2) as i:
                    for s in range(2):
                        sp.wait_ge(scored, 2 * i + s + 1)
                        sp.dma_start(qb[s][:].rearrange("p c t -> p (c t)"), by_pair(qb_d)[s][i]).then_inc(qk_in[s], 16)
                        sp.dma_start(kb[s][:].rearrange("p c t -> p (c t)"), by_pair(kb_d)[s][i]).then_inc(qk_in[s], 16)

            @block.tensor
            def _(pe):
                pe.sem_inc(scored, 2)
                with pe.Fori(0, NPAIR // 2) as i:
                    for s in range(2):
                        n = 2 * i + s
                        pe.wait_ge(qk_in[s], 32 * i + 32)
                        for g in range(GROUPS):
                            m, c = g // 3, g % 3
                            wait_rounded(pe, n, g - 2)
                            for half in range(2):
                                for j in range(4):
                                    r = slice(32 * j, 32 * j + DH + 3)
                                    a = m * SEQ + half * HALF
                                    mm = pe.matmul(s_ps[g % 2][:, j, half * SEQ:half * SEQ + SEQ], qb[s][r, c, a:a + HALF],
                                                   kb[s][r, c, m * SEQ:m * SEQ + SEQ], start=True, stop=True)
                            mm.then_inc(s_ready, 1)
                        pe.wait_ge(s_ready, GROUPS * n + GROUPS)
                        pe.sem_inc(scored, 1)

            @block.scalar
            def _(act):
                def round_scores(i, s, g):
                    n = 2 * i + s
                    act.wait_ge(s_ready, GROUPS * n + g + 1)
                    act.wait_ge(exped, GROUPS * n + g + 1)
                    act.activation(t16[g][:], s_ps[g % 2][:, :, 0:PAIR], ACT.Copy, scale=kit.scal[0:HALF, C_S:C_S + 1])\
                        .then_inc(act_rounded, 1)

                def step(i, s, first, last):
                    n = 2 * i + s
                    for g in range(GROUPS):
                        i2, s2, g2 = sliding(i, s, g + 1, GROUPS)
                        if g2 in by_act and not (last and g + 1 == GROUPS):
                            round_scores(i2, s2, g2)
                        wait_rounded(act, n, g)
                        act.wait_ge(summed, GROUPS * n + g + 1)
                        act.activation(e32[g % 3][:], t16[g][:], ACT.Exp, scale=kit.scal[0:HALF, S_S:S_S + 1])\
                            .then_inc(exped, 1)

                act.sem_inc(act_rounded, len(by_act.members))
                act.sem_inc(exped, 6)
                round_scores(0, 0, 0)
                turns(act, NPAIR, step)

            @block.vector
            def _(v):
                def round_scores(i, s, g):
                    n = 2 * i + s
                    v.wait_ge(s_ready, GROUPS * n + g + 1)
                    v.wait_ge(exped, GROUPS * n + g + 1)
                    v.tensor_scalar(t16[g][:], s_ps[g % 2][:, :, 0:PAIR], kit.scal[0:HALF, C_S:C_S + 1], None,
                                    ALU.mult).then_inc(dve_rounded, 1)

                def step(i, s, first, last):
                    for g in range(GROUPS):
                        i2, s2, g2 = sliding(i, s, g + 2, GROUPS)
                        if g2 in by_dve and not (last and g + 2 >= GROUPS):
                            round_scores(i2, s2, g2)
                        m, c = g // 3, g % 3
                        v.wait_ge(exped, GROUPS * (2 * i + s) + g + 1 + 6)
                        out = rowsum[:].rearrange("p (i s) c j m h -> p s c m i j h", s=2)[:, s, c, m][:, bass.ds(i, 1)]
                        v.tensor_reduce(out, e32[g % 3][:].rearrange("p j (h k) -> p j h k", h=2), AX.X, ALU.add)\
                            .then_inc(summed, 1)

                v.sem_inc(dve_rounded, len(by_dve.members))
                v.sem_inc(summed, 3)
                turns(v, NPAIR, step)

        with ExitStack() as pctx:
            rt_ps = [kit.ps(pctx, f"rt_ps{b}", [48, 512]) for b in range(8)]
            block = pctx.enter_context(nc.Block())

            @block.gpsimd
            def _(pool):
                pool.wait_ge(pmax_ready, 1)
                nc.gpsimd.partition_all_reduce(pmax[:], pmax1[:], 128, RMAX).then_inc(pmax_all, 1)

            @block.vector
            def _(v):
                sc = lambda k, p=128: kit.scal[0:p, k:k + 1]
                nc.vector.memset(pmax1[:], 0.0)
                v.reciprocal(rinv[:], rowsum[:].rearrange("p n c j m h -> p (n c j m h)"))
                v.drain()
                v.tensor_reduce(pmax1[0:HALF], rinv[:], AX.X, ALU.max).then_inc(pmax_ready, 1)
                v.wait_ge(pmax_all, 1)
                quant_scalars(v, kit.scal, pmax[:], None, U_CTX, C_A)
                v.tensor_tensor(sc(U_CTX), sc(U_CTX), sc(S_V), ALU.mult)
                v.tensor_scalar(rinv[:], rinv[:], sc(C_A, HALF), None, ALU.mult).then_inc(r_ready, 1)
                for b in range(8):
                    v.wait_ge(rt_psum, b + 1)
                    v.tensor_copy(rt[:, 4 * b:4 * b + 4].rearrange("p n t -> p (n t)"), rt_ps[b][:, 0:4 * HALF])\
                        .then_inc(rt_ready, 1)

            @block.tensor
            def _(pe):
                pe.wait_ge(r_ready, 1)
                for n in range(NPAIR):
                    mm = pe.transpose(rt_ps[n // 4][:, n % 4 * HALF:n % 4 * HALF + HALF], rinv[:, 48 * n:48 * n + 48],
                                      kit.ident[0:HALF, 0:HALF])
                    if n % 4 == 3:
                        mm.then_inc(rt_psum, 1)

            @block.sync
            def _(sp):
                sp.wait_ge(rt_ready, 8)
                sp.dma_start(r_d.rearrange("n (a t) -> a n t", t=HALF), rt[:]).then_inc(rt_out, 16)
                sp.wait_ge(rt_out, 16)


def context_phase(kit, qb_d, kb_d, vb_d, r_d, ctx_d):
    nc = kit.nc
    GROUPS = 8
    LAG = 3
    by_act, by_dve = Share((0, 1, 2, 3, 4, 6, 7), GROUPS), Share((5,), GROUPS)
    with ExitStack() as ctx:
        qb = [kit.sb(ctx, f"cx_qb{s}", [128, 3, PAIR], BF16) for s in range(2)]
        kb = [kit.sb(ctx, f"cx_kb{s}", [128, 3, PAIR], BF16) for s in range(2)]
        vb = [kit.sb(ctx, f"cx_vb{s}", [HALF, 4, HEADS, 32], BF16) for s in range(2)]
        rb = [kit.sb(ctx, f"cx_r{s}", [HALF, HEADS, 2, SEQ], F32) for s in range(2)]
        t16 = [kit.sb(ctx, f"cx_t{b}", [HALF, 3, 2, SEQ], I16) for b in range(4)]
        e32 = [kit.sb(ctx, f"cx_e{b}", [HALF, 3, 2, SEQ], F32) for b in range(2)]
        a16 = [kit.sb(ctx, f"cx_a16{b}", [HALF, 3, 2, SEQ], I16) for b in range(2)]
        ab = [kit.sb(ctx, f"cx_ab{b}", [HALF, 3, 2, SEQ], BF16) for b in range(4)]
        cx = [kit.sb(ctx, f"cx_out{s}", [128, 3, 2, SEQ], F32) for s in range(2)]
        cmax = kit.sb(ctx, "cmax", [128, NPAIR], F32)
        cmax1 = kit.sb(ctx, "cmax1", [128, 1], F32)
        cmaxg = kit.sb(ctx, "cmaxg", [128, 1], F32)
        s_ps = [kit.ps(ctx, f"cx_s_ps{b}", [HALF, 3, 512]) for b in range(2)]
        c_ps = [kit.ps(ctx, f"cx_c_ps{b}", [128, 512]) for b in range(2)]
        sem = lambda name: kit.sem(ctx, name)
        qk_in, v_in, r_in = [[sem(f"cx_{n}_in{s}") for s in range(2)] for n in ("qk", "v", "r")]
        cx_out = [sem(f"cx_stored{s}") for s in range(2)]
        s_ready = sem("cx_s_ready")
        act_rounded, dve_rounded = sem("cx_act_rounded"), sem("cx_dve_rounded")
        sp_turn = sem("sp_turn")
        exped = sem("cx_exped")
        weighted = sem("cx_weighted")
        cast = sem("cx_cast")
        applied = sem("cx_applied")
        c_copied = sem("cx_c_copied")
        measured = sem("cx_measured")
        cmax_ready, cmaxg_ready = sem("cmax_ready"), sem("cmaxg_ready")
        block = ctx.enter_context(nc.Block())
        by_pair = lambda a: a.rearrange("(i s) p x -> s i p x", s=2)
        PAIRG = GROUPS + 2

        def wait_rounded(eng, n, g):
            share, done = (by_act, act_rounded) if g % GROUPS in by_act else (by_dve, dve_rounded)
            eng.wait_ge(done, share.done(n, g))

        @block.sync
        def _(sp):
            def load(i, s):
                n = 2 * i + s
                done = GROUPS * (n - 2) + GROUPS + PAIRG
                sp.wait_ge(s_ready, done)
                sp.sem_inc(sp_turn, 1)
                sp.dma_start(qb[s][:].rearrange("p c t -> p (c t)"), by_pair(qb_d)[s][i]).then_inc(qk_in[s], 16)
                sp.dma_start(kb[s][:].rearrange("p c t -> p (c t)"), by_pair(kb_d)[s][i]).then_inc(qk_in[s], 16)
                sp.wait_ge(weighted, done)
                sp.sem_inc(sp_turn, 1)
                row = r_d.rearrange("(i s) x -> s i x", s=2)[s][bass.ds(i, 1)]
                sp.dma_start(rb[s][:].rearrange("p h m q -> p (h m q)"), row.to_broadcast([HALF, HEADS * PAIR]))\
                    .then_inc(r_in[s], 16)
                sp.wait_ge(applied, done)
                sp.sem_inc(sp_turn, 1)
                sp.dma_start(vb[s][:].rearrange("p m h d -> p (m h d)"), by_pair(vb_d)[s][i]).then_inc(v_in[s], 16)

            def store(i, s):
                sp.wait_ge(c_copied, 6 * (2 * i + s) + 6 + 2)
                sp.sem_inc(sp_turn, 1)
                sp.dma_start(by_pair(ctx_d)[s][i], cx[s][:].rearrange("p c m q -> p (c m q)")).then_inc(cx_out[s], 16)

            for s in range(2):
                sp.sem_inc(cx_out[s], 16)
            load(0, 0)
            with sp.Fori(0, NPAIR // 2 - 1) as i:
                load(i, 1)
                store(i, 0)
                load(i + 1, 0)
                store(i, 1)
            load(NPAIR // 2 - 1, 1)
            store(NPAIR // 2 - 1, 0)
            store(NPAIR // 2 - 1, 1)
            for s in range(2):
                sp.wait_ge(cx_out[s], 16 * (NPAIR // 2 + 1))

        @block.tensor
        def _(pe):
            def scores(i, s, g):
                n = 2 * i + s
                if g == 0:
                    pe.wait_ge(qk_in[s], 32 * i + 32)
                m = g // 4
                wait_rounded(pe, n, g - 2)
                for half in range(2):
                    for b in range(3):
                        c, j = divmod(3 * (g % 4) + b, 4)
                        r = slice(32 * j, 32 * j + DH + 3)
                        a = m * SEQ + half * HALF
                        mm = pe.matmul(s_ps[g % 2][:, b, half * SEQ:half * SEQ + SEQ], kb[s][r, c, a:a + HALF],
                                       qb[s][r, c, m * SEQ:m * SEQ + SEQ], start=True, stop=True)
                mm.then_inc(s_ready, 1)

            def apply(i, s, g):
                n = 2 * i + s
                m = g // 4
                if g == 0:
                    pe.wait_ge(v_in[s], 16 * i + 16)
                pe.wait_ge(cast, GROUPS * n + g + 1 + 2)
                for b in range(3):
                    head = 3 * (g % 4) + b
                    c, j = divmod(head, 4)
                    if j == 0:
                        pe.wait_ge(c_copied, 6 * n + 3 * m + c + 1)
                    for half in range(2):
                        mm = pe.matmul(c_ps[(3 * m + c) % 2][32 * j:32 * j + 32, 0:SEQ], vb[s][:, 2 * m + half, head],
                                       ab[g % 4][:, b, half], start=(half == 0), stop=(half == 1))
                mm.then_inc(applied, 1)

            def step(i, s, first, last):
                for g in range(GROUPS):
                    if not (last and g + 2 >= GROUPS):
                        scores(*sliding(i, s, g + 2, GROUPS))
                    if g >= LAG:
                        apply(i, s, g - LAG)
                    elif not first:
                        apply(i - 1 + s, 1 - s, g - LAG + GROUPS)

            pe.sem_inc(applied, PAIRG)
            pe.sem_inc(s_ready, PAIRG)
            scores(0, 0, 0)
            scores(0, 0, 1)
            turns(pe, NPAIR, step)
            for g in range(GROUPS - LAG, GROUPS):
                apply(NPAIR // 2 - 1, 1, g)

        @block.scalar
        def _(act):
            def round_scores(i, s, g):
                act.wait_ge(s_ready, GROUPS * (2 * i + s) + g + 1 + PAIRG)
                act.wait_ge(exped, GROUPS * (2 * i + s) + g + 1)
                act.activation(t16[g % 4][:].rearrange("p b h q -> p b (h q)"), s_ps[g % 2][:, :, 0:PAIR], ACT.Copy,
                               scale=kit.scal[0:HALF, C_S:C_S + 1]).then_inc(act_rounded, 1)

            def copy_chunk(n, s, chunk):
                m, c = divmod(chunk, 3)
                act.wait_ge(applied, GROUPS * n + 4 * m + c + 2 + PAIRG)
                act.copy(cx[s][:, c, m], c_ps[chunk % 2][:, 0:SEQ]).then_inc(c_copied, 1)

            def step(i, s, first, last):
                n = 2 * i + s
                for g in range(GROUPS):
                    i2, s2, g2 = sliding(i, s, g + 1, GROUPS)
                    if g2 in by_act and not (last and g + 1 == GROUPS):
                        round_scores(i2, s2, g2)
                    wait_rounded(act, n, g)
                    act.wait_ge(weighted, GROUPS * n + g - 2 + 1 + PAIRG)
                    act.activation(e32[g % 2][:], t16[g % 4][:], ACT.Exp, scale=kit.scal[0:HALF, S_S:S_S + 1])\
                        .then_inc(exped, 1)
                    if g < 3 and not first:
                        copy_chunk(n - 1, 1 - s, 3 + g)
                    if g == 4:
                        act.wait_ge(cx_out[s], 16 * i + 16)
                        act.wait_ge(measured, n + 1)
                    if 4 <= g < 7:
                        copy_chunk(n, s, g - 4)

            act.sem_inc(act_rounded, len(by_act.members))
            act.sem_inc(exped, 4)
            act.sem_inc(c_copied, 2)
            round_scores(0, 0, 0)
            turns(act, NPAIR, step)
            for chunk in range(3, 6):
                copy_chunk(NPAIR - 1, 1, chunk)

        @block.vector
        def _(v):
            def round_scores(i, s, g):
                n = 2 * i + s
                v.wait_ge(s_ready, GROUPS * n + g + 1 + PAIRG)
                v.wait_ge(exped, GROUPS * n + g + 1)
                v.tensor_scalar(t16[g % 4][:].rearrange("p b h q -> p b (h q)"), s_ps[g % 2][:, :, 0:PAIR],
                                kit.scal[0:HALF, C_S:C_S + 1], None, ALU.mult).then_inc(dve_rounded, 1)

            def measure(i, s):
                n = 2 * i + s
                v.wait_ge(c_copied, 6 * n + 6 + 2)
                v.tensor_reduce(cmax[:].rearrange("p (i s) -> p s i", s=2)[:, s, bass.ds(i, 1)], cx[s][:], AX.XYZ, ALU.max,
                                apply_absolute_value=True).then_inc(measured, 1)

            def cast_weights(count, g):
                v.wait_ge(weighted, count + 1 + PAIRG)
                v.wait_ge(applied, count - 4 + 1 + PAIRG)
                v.tensor_copy(ab[g % 4][:], a16[g % 2][:]).then_inc(cast, 1)

            def step(i, s, first, last):
                n = 2 * i + s
                for g in range(GROUPS):
                    i2, s2, g2 = sliding(i, s, g + 2, GROUPS)
                    if g2 in by_dve and not (last and g + 2 >= GROUPS):
                        round_scores(i2, s2, g2)
                    v.wait_ge(exped, GROUPS * n + g + 1 + 4)
                    v.wait_ge(r_in[s], 16 * i + 16)
                    v.wait_ge(cast, GROUPS * n + g + 1)
                    head = 3 * (g % 4)
                    for half in range(2):
                        last_mul = v.tensor_tensor(a16[g % 2][:, :, half], e32[g % 2][:, :, half],
                                                   rb[s][:, head:head + 3, g // 4], ALU.mult)
                    last_mul.then_inc(weighted, 1)
                    if not (first and g == 0):
                        cast_weights(GROUPS * n - 1 + g, (g - 1) % GROUPS)
                    if g == 4 and not first:
                        measure(*((i, 0) if s else (i - 1, 1)))

            v.sem_inc(dve_rounded, len(by_dve.members))
            v.sem_inc(weighted, PAIRG)
            v.sem_inc(cast, 2)
            v.sem_inc(measured, 2)
            nc.vector.memset(cmax1[:], 0.0)
            turns(v, NPAIR, step)
            cast_weights(GROUPS * NPAIR - 1, GROUPS - 1)
            measure(NPAIR // 2 - 1, 1)
            v.drain()
            v.tensor_reduce(cmax1[:], cmax[:], AX.X, ALU.max).then_inc(cmax_ready, 1)
            v.wait_ge(cmaxg_ready, 1)
            quant_scalars(v, kit.scal, cmaxg[:], U_CTX, S_CTX, C_CTX)

        @block.gpsimd
        def _(pool):
            pool.wait_ge(cmax_ready, 1)
            nc.gpsimd.partition_all_reduce(cmaxg[:], cmax1[:], 128, RMAX).then_inc(cmaxg_ready, 1)



def norm_columns(v, out, var, tmp):
    v.reciprocal(out, out)
    v.drain()
    v.tensor_tensor(tmp, out, out, ALU.mult)
    v.drain()
    v.tensor_tensor(tmp, tmp, var, ALU.mult)
    v.drain()
    v.tensor_scalar(tmp, tmp, -0.5, 1.5, ALU.mult, ALU.add)
    v.drain()
    v.tensor_tensor(out, out, tmp, ALU.mult)
    v.drain()


TU = 3
NTILE = NTOK // 128
NTURN = NTILE // TU
EXPERTS, FEXP, FSH = 16, 4 * D, 2 * D
TOPK = NTOK // EXPERTS * 2
ROW = D + EXPERTS


def mixer_out_phase(kit, ctx_d, xt_d, h_d, gate_wt, x2_d, x2t_d, lt_d, out_d):
    nc = kit.nc
    with ExitStack() as ctx:
        y = kit.sb(ctx, "y_all", [KP, KC, NTOK], F32)
        sem = lambda name: kit.sem(ctx, name)
        sp_turn = sem("mo_sp_turn")
        by_pair = lambda a: a.rearrange("(i s) p x -> s i p x", s=2)
        cols = lambda a: a.rearrange("(m p) (i s t) -> s i p m t", p=KP, s=2, t=PAIR)

        def ycols(i, s, size, c=None):
            t = y[:].rearrange("p c (i s t) -> p s c i t", s=2, t=size)[:, s]
            t = t[:, :, bass.ds(i, 1)] if c is None else t[:, c, bass.ds(i, 1)]
            return t

        with ExitStack() as c1:
            cf = [kit.sb(c1, f"mo_c{s}", [128, 3 * PAIR], F32) for s in range(2)]
            c16 = [kit.sb(c1, f"mo_c16{s}", [128, 3 * PAIR], I16) for s in range(2)]
            cb = [kit.sb(c1, f"mo_cb{s}", [128, 3, PAIR], BF16) for s in range(2)]
            ymax = kit.sb(c1, "ymax", [128, NPAIR], F32)
            ymax1 = kit.sb(c1, "ymax1", [128, 1], F32)
            ymaxg = kit.sb(c1, "ymaxg", [128, 1], F32)
            y_ps = [kit.ps(c1, f"y_ps{s}", [KP, KC, 512]) for s in range(2)]
            c_in = [sem(f"mo_c_in{s}") for s in range(2)]
            rounded = sem("mo_rounded")
            cast = sem("mo_cast")
            y_ready = sem("y_ready")
            y_copied = sem("y_copied")
            ymax_ready, ymax_all = sem("ymax_ready"), sem("ymax_all")
            block = c1.enter_context(nc.Block())

            @block.sync
            def _(sp):
                with sp.Fori(0, NPAIR // 2) as i:
                    for s in range(2):
                        sp.wait_ge(rounded, 2 * i + s + 1)
                        sp.sem_inc(sp_turn, 1)
                        sp.dma_start(cf[s][:], by_pair(ctx_d)[s][i]).then_inc(c_in[s], 16)

            @block.scalar
            def _(act):
                act.sem_inc(rounded, 2)
                act.sem_inc(y_copied, 2)

                def round_context(i, s):
                    act.wait_ge(c_in[s], 16 * i + 16)
                    act.wait_ge(cast, 2 * i + s + 1)
                    act.activation(c16[s][:], cf[s][:], ACT.Copy, scale=kit.scal[:, C_CTX:C_CTX + 1]).then_inc(rounded, 1)

                def step(i, s, first, last):
                    if not last:
                        round_context(*((i, 1) if s == 0 else (i + 1, 0)))
                    act.wait_ge(y_ready, 2 * i + s + 1 + 2)
                    act.copy(ycols(i, s, PAIR).rearrange("p c i t -> p c (i t)"), y_ps[s][:, :, 0:PAIR])\
                        .then_inc(y_copied, 1)

                round_context(0, 0)
                turns(act, NPAIR, step)

            @block.vector
            def _(v):
                v.sem_inc(cast, 2)
                nc.vector.memset(ymax[:], 0.0)

                def cast_context(i, s):
                    n = 2 * i + s
                    v.wait_ge(rounded, n + 1 + 2)
                    v.wait_ge(y_ready, n + 1)
                    v.tensor_copy(cb[s][:].rearrange("p c t -> p (c t)"), c16[s][:]).then_inc(cast, 1)

                def step(i, s, first, last):
                    if not last:
                        cast_context(*((i, 1) if s == 0 else (i + 1, 0)))
                    v.wait_ge(y_copied, 2 * i + s + 1 + 2)
                    v.tensor_reduce(ymax[0:KP].rearrange("p (i s) -> p s i", s=2)[:, s, bass.ds(i, 1)],
                                    ycols(i, s, PAIR).rearrange("p c i t -> p c (i t)"), AX.XY, ALU.max,
                                    apply_absolute_value=True)

                cast_context(0, 0)
                turns(v, NPAIR, step)
                v.drain()
                v.tensor_reduce(ymax1[:], ymax[:], AX.X, ALU.max).then_inc(ymax_ready, 1)
                v.wait_ge(ymax_all, 1)
                v.tensor_tensor(kit.scal[:, U_Y:U_Y + 1], kit.scal[:, S_CTX:S_CTX + 1], kit.scal[:, S_WO:S_WO + 1],
                                ALU.mult)
                quant_scalars(v, kit.scal, ymaxg[:], U_Y, S_Y, C_Y)

            @block.tensor
            def _(pe):
                pe.sem_inc(y_ready, 2)
                with pe.Fori(0, NPAIR // 2) as i:
                    for s in range(2):
                        n = 2 * i + s
                        pe.wait_ge(cast, n + 1 + 2)
                        pe.wait_ge(y_copied, n + 1)
                        for o in range(KC):
                            for c in range(3):
                                mm = pe.matmul(y_ps[s][:, o, 0:PAIR], kit.w_out[:, c, o * KP:o * KP + KP], cb[s][:, c],
                                               start=(c == 0), stop=(c == 2))
                        mm.then_inc(y_ready, 1)

            @block.gpsimd
            def _(pool):
                pool.wait_ge(ymax_ready, 1)
                nc.gpsimd.partition_all_reduce(ymaxg[:], ymax1[:], 128, RMAX).then_inc(ymax_all, 1)

        mean = kit.sb(ctx, "bn_mean", [KP, KC, 2], F32)
        amp = kit.sb(ctx, "bn_amp", [KP, KC], F32)
        with ExitStack() as c2:
            xf = [kit.sb(c2, f"mo_x{s}", [KP, KC, PAIR], F32) for s in range(2)]
            x16 = [kit.sb(c2, f"mo_x16{s}", [KP, KC, PAIR], I16) for s in range(2)]
            xs = [kit.sb(c2, f"mo_xs{s}", [KP, KC, PAIR], F32) for s in range(2)]
            y16 = [kit.sb(c2, f"mo_y16{s}", [KP, KC, PAIR], I16) for s in range(2)]
            bst = kit.sb(c2, "mo_bst", [KP, KC, NPAIR, 6], F32)
            hi = kit.sb(c2, "mo_hi", [KP, KC, NPAIR], F32)
            lo = kit.sb(c2, "mo_lo", [KP, KC, NPAIR], F32)
            ext = kit.sb(c2, "mo_ext", [KP, 3, KC], F32)
            vep = kit.sb(c2, "mo_vep", [KP, KC], F32)
            tmp = kit.sb(c2, "mo_tmp", [KP, KC], F32)
            rmax1 = kit.sb(c2, "rmax1", [128, 1], F32)
            rmaxg = kit.sb(c2, "rmaxg", [128, 1], F32)
            x_in = [sem(f"mo_x_in{s}") for s in range(2)]
            x_round = sem("mo_x_round")
            x_scaled = sem("mo_x_scaled")
            r_done = sem("mo_r_done")
            vep_ready, root_ready = sem("vep_ready"), sem("root_ready")
            rmax_ready, rmax_all = sem("rmax_ready"), sem("rmax_all")
            block = c2.enter_context(nc.Block())

            @block.sync
            def _(sp):
                with sp.Fori(0, NPAIR // 2) as i:
                    for s in range(2):
                        sp.wait_ge(x_round, 2 * i + s + 1)
                        sp.sem_inc(sp_turn, 1)
                        sp.dma_start(xf[s][:], cols(xt_d)[s][i]).then_inc(x_in[s], 16)

            @block.scalar
            def _(act):
                act.sem_inc(x_round, 2)
                with act.Fori(0, NPAIR // 2) as i:
                    for s in range(2):
                        n = 2 * i + s
                        act.wait_ge(x_in[s], 16 * i + 16)
                        act.wait_ge(r_done, n + 1)
                        act.activation(x16[s][:], xf[s][:], ACT.Copy, scale=kit.scal[0:KP, C_X:C_X + 1]).then_inc(x_round, 1)
                        act.wait_ge(x_round, n + 1 + 2)
                        act.activation(xs[s][:], x16[s][:], ACT.Copy, scale=kit.scal[0:KP, S_X:S_X + 1])
                        yc = ycols(i, s, PAIR).rearrange("p c i t -> p c (i t)")
                        act.activation(y16[s][:], yc, ACT.Copy, scale=kit.scal[0:KP, C_Y:C_Y + 1]).then_inc(x_scaled, 1)
                act.wait_ge(vep_ready, 1)
                act.activation(amp[:], vep[:], ACT.Sqrt).then_inc(root_ready, 1)

            @block.vector
            def _(v):
                v.sem_inc(r_done, 2)
                nc.vector.memset(rmax1[:], 0.0)
                with v.Fori(0, NPAIR // 2) as i:
                    for s in range(2):
                        n = 2 * i + s
                        yc = ycols(i, s, PAIR).rearrange("p c i t -> p c (i t)")
                        v.wait_ge(x_scaled, n + 1)
                        v.scalar_tensor_tensor(yc, y16[s][:], kit.scal[0:KP, S_Y:S_Y + 1], xs[s][:], ALU.mult, ALU.add)\
                            .then_inc(r_done, 1)
                        v.drain()
                        for c in range(KC):
                            yi = ycols(i, s, PAIR, c).rearrange("p i t -> p (i t)")
                            v.bn_stats(bst[:, c].rearrange("p (i s) x -> p s i x", s=2)[:, s, bass.ds(i, 1)]
                                       .rearrange("p i x -> p (i x)"), yi)
                        at = lambda t: t[:].rearrange("p c (i s) -> p s c i", s=2)[:, s][:, :, bass.ds(i, 1)]
                        v.tensor_reduce(at(hi), yc, AX.X, ALU.max)
                        v.tensor_reduce(at(lo), yc, AX.X, ALU.min)
                v.drain()
                for c in range(KC):
                    v.bn_aggr(mean[:, c], bst[:, c].rearrange("p n x -> p (n x)"))
                v.tensor_reduce(ext[:, 0], hi[:], AX.X, ALU.max)
                v.tensor_reduce(ext[:, 1], lo[:], AX.X, ALU.min)
                v.drain()
                v.tensor_scalar(vep[:], mean[:, :, 1], EPS, None, ALU.add).then_inc(vep_ready, 1)
                v.tensor_tensor(ext[:, 0], ext[:, 0], mean[:, :, 0], ALU.subtract)
                v.tensor_tensor(ext[:, 1], mean[:, :, 0], ext[:, 1], ALU.subtract)
                v.drain()
                v.tensor_tensor(ext[:, 2], ext[:, 0], ext[:, 1], ALU.max)
                v.wait_ge(root_ready, 1)
                norm_columns(v, amp[:], vep[:], tmp[:])
                v.tensor_tensor(ext[:, 2], ext[:, 2], amp[:], ALU.mult)
                v.drain()
                v.tensor_reduce(rmax1[0:KP], ext[:, 2], AX.X, ALU.max).then_inc(rmax_ready, 1)
                v.wait_ge(rmax_all, 1)
                quant_scalars(v, kit.scal, rmaxg[:], None, S_RN, TMP2)
                v.tensor_scalar(amp[:], amp[:], kit.scal[0:KP, TMP2:TMP2 + 1], None, ALU.mult)

            @block.gpsimd
            def _(pool):
                pool.wait_ge(rmax_ready, 1)
                nc.gpsimd.partition_all_reduce(rmaxg[:], rmax1[:], 128, RMAX).then_inc(rmax_all, 1)

        T = 128 * TU
        with ExitStack() as c3:
            gw = kit.sb(c3, "gate_w", [KP, KC, EXPERTS], F32)
            n16 = kit.sb(c3, "n16", [KP, KC, T], I16)
            nb = [kit.sb(c3, f"nb{s}", [KP, KC, T], BF16) for s in range(2)]
            h1 = [kit.sb(c3, f"h1{s}", [128, TU, D], F32) for s in range(2)]
            hin = [kit.sb(c3, f"hin{s}", [128, TU, D], F32) for s in range(2)]
            x2 = [kit.sb(c3, f"x2{s}", [128, TU, D], F32) for s in range(2)]
            x2t = [kit.sb(c3, f"x2t{s}", [KP, KC, T], F32) for s in range(2)]
            stats = kit.sb(c3, "stats2", [128, TU, 6], F32)
            mv = kit.sb(c3, "mv2", [128, TU, 2], F32)
            ve = kit.sb(c3, "ve2", [128, TU], F32)
            rs = kit.sb(c3, "rs2", [128, TU], F32)
            tmp = kit.sb(c3, "tmp2", [128, TU], F32)
            n_ps = [kit.ps(c3, f"n_ps{s}", [128, TU * D], BF16) for s in range(2)]
            t_ps = [kit.ps(c3, f"t_ps{c}", [KP, 512]) for c in range(KC)]
            g_ps = kit.ps(c3, "g_ps", [EXPERTS, T])
            l_ps = kit.ps(c3, "l_ps", [128, TU * EXPERTS])
            lt = [kit.sb(c3, f"lt{s}", [EXPERTS, T], F32) for s in range(2)]
            h_in = [sem(f"h_in{s}") for s in range(2)]
            gw_in = sem("gw_in")
            nb_ready = sem("nb_ready")
            n_ready = sem("n_ready")
            h1_ready = sem("h1_ready")
            ve_ready, root2 = sem("ve2_ready"), sem("root2")
            x2_ready = sem("x2_ready")
            t_ready = sem("t_ready")
            t_copied = sem("t_copied")
            g_ready = sem("g_ready")
            g_copied = sem("g_copied")
            l_ready = sem("l_ready")
            l_copied = sem("l_copied")
            pe_turn = sem("pe_turn")
            h1_out, x2_out, x2t_out, lt_out = [[sem(f"{n}_out{s}") for s in range(2)] for n in ("h1", "x2", "x2t", "lt")]
            block = c3.enter_context(nc.Block())
            tiles = lambda a: a.rearrange("(i s m p) e -> s i p m e", s=2, m=TU, p=128)

            @block.sync
            def _(sp):
                sp.dma_start(gw[:], gate_wt.rearrange("(c p) e -> p c e", p=KP)).then_inc(gw_in, 16)
                for o in (h1_out, x2_out, x2t_out, lt_out):
                    for s in range(2):
                        sp.sem_inc(o[s], 16)

                def load(i, s):
                    sp.wait_ge(h1_ready, 2 * i + s + 1)
                    sp.sem_inc(sp_turn, 1)
                    sp.dma_start(hin[s][:], tiles(h_d)[s][i]).then_inc(h_in[s], 16)

                def step(i, s, more):
                    n = 2 * i + s
                    sp.wait_ge(h1_ready, n + 1 + 2)
                    sp.sem_inc(sp_turn, 1)
                    sp.dma_start(tiles(out_d)[s][i], h1[s][:]).then_inc(h1_out[s], 16)
                    if more:
                        load(i + 1, s)
                    sp.wait_ge(x2_ready, n + 1)
                    sp.sem_inc(sp_turn, 1)
                    sp.dma_start(tiles(x2_d)[s][i][:, :, 0:D], x2[s][:]).then_inc(x2_out[s], 16)
                    sp.wait_ge(t_copied, n + 1 + 1)
                    sp.sem_inc(sp_turn, 1)
                    sp.dma_start(x2t_d.rearrange("(m p) (i s t) -> s i p m t", p=KP, s=2, t=T)[s][i], x2t[s][:])\
                        .then_inc(x2t_out[s], 16)
                    sp.wait_ge(g_copied, n + 1 + 2)
                    sp.sem_inc(sp_turn, 1)
                    sp.dma_start(lt_d.rearrange("e (i s t) -> s i e t", s=2, t=T)[s][i], lt[s][:]).then_inc(lt_out[s], 16)

                load(0, 0)
                load(0, 1)
                with sp.Fori(0, NTURN // 2 - 1) as i:
                    step(i, 0, True)
                    step(i, 1, True)
                step(NTURN // 2 - 1, 0, False)
                step(NTURN // 2 - 1, 1, False)
                for o in (h1_out, x2_out, x2t_out, lt_out):
                    for s in range(2):
                        sp.wait_ge(o[s], 16 * (NTURN // 2 + 1))

            @block.tensor
            def _(pe):
                pe.sem_inc(n_ready, 2)
                pe.sem_inc(t_ready, 2)
                pe.sem_inc(l_ready, 2)
                pe.wait_ge(gw_in, 16)

                def turn_back(i, s):
                    n = 2 * i + s
                    pe.wait_ge(nb_ready, n + 1 + 2)
                    pe.wait_ge(h1_ready, n + 1)
                    for m in range(TU):
                        for c in range(KC):
                            mm = pe.transpose(n_ps[s][:, m * D + c * KP:m * D + c * KP + KP],
                                              nb[s][:, c, m * 128:m * 128 + 128], kit.identb[0:KP, 0:KP])
                    mm.then_inc(n_ready, 1)

                def gate(i, s):
                    n = 2 * i + s
                    pe.wait_ge(x2_ready, n + 1)
                    pe.wait_ge(t_copied, n + 1)
                    for c in range(KC):
                        for m in range(TU):
                            mm = pe.transpose(t_ps[c][:, m * 128:m * 128 + 128], x2[s][:, m, c * KP:c * KP + KP], kit.ident[:])
                    mm.then_inc(t_ready, 1)
                    pe.wait_ge(t_copied, n + 1 + 1)
                    pe.wait_ge(g_copied, n + 1 + 1)
                    for c in range(KC):
                        mm = pe.matmul(g_ps[:], gw[:, c], x2t[s][:, c], start=(c == 0), stop=(c == KC - 1))
                    mm.then_inc(g_ready, 1)
                    pe.wait_ge(g_copied, n + 1 + 2)
                    pe.wait_ge(l_copied, n + 1)
                    pe.sem_inc(pe_turn, 1)
                    for m in range(TU):
                        mm = pe.transpose(l_ps[:, m * EXPERTS:m * EXPERTS + EXPERTS], lt[s][:, m * 128:m * 128 + 128],
                                          kit.ident[0:EXPERTS, 0:EXPERTS])
                    mm.then_inc(l_ready, 1)

                def step(i, s, first, last):
                    if not last:
                        turn_back(*((i, 1) if s == 0 else (i + 1, 0)))
                    gate(i, s)

                turn_back(0, 0)
                turns(pe, NTURN, step)

            @block.scalar
            def _(act):
                act.sem_inc(t_copied, 1)
                act.sem_inc(g_copied, 2)
                act.sem_inc(l_copied, 1)

                def root(i, s):
                    act.wait_ge(ve_ready, 2 * i + s + 1)
                    act.activation(rs[:], ve[:], ACT.Sqrt).then_inc(root2, 1)

                def step(i, s, first, last):
                    n = 2 * i + s
                    act.wait_ge(t_ready, n + 1 + 2)
                    act.wait_ge(x2t_out[s], 16 * i + 16)
                    for c in range(KC):
                        ins = act.copy(x2t[s][:, c], t_ps[c][:, 0:T])
                    ins.then_inc(t_copied, 1)
                    if not last:
                        root(*((i, 1) if s == 0 else (i + 1, 0)))
                    act.wait_ge(g_ready, n + 1)
                    act.wait_ge(lt_out[s], 16 * i + 16)
                    act.wait_ge(l_ready, n + 1)
                    act.copy(lt[s][:], g_ps[:]).then_inc(g_copied, 1)
                    act.wait_ge(l_ready, n + 1 + 2)
                    lg = kit.logits[:].rearrange("p (i s m) e -> p s i (m e)", s=2, m=TU)[:, s, bass.ds(i, 1)]
                    act.copy(lg.rearrange("p i x -> p (i x)"), l_ps[:]).then_inc(l_copied, 1)

                root(0, 0)
                turns(act, NTURN, step)

            @block.vector
            def _(v):
                v.sem_inc(nb_ready, 2)
                v.sem_inc(h1_ready, 2)

                def quantise(i, s):
                    n = 2 * i + s
                    for c in range(KC):
                        yi = ycols(i, s, T, c).rearrange("p i t -> p (i t)")
                        v.tensor_scalar(n16[:, c], yi, mean[:, c, 0:1], amp[:, c:c + 1], ALU.subtract, ALU.mult)
                    v.drain()
                    v.wait_ge(n_ready, n + 1)
                    v.tensor_copy(nb[s][:], n16[:]).then_inc(nb_ready, 1)
                    v.drain()

                def step(i, s, first, last):
                    n = 2 * i + s
                    v.wait_ge(n_ready, n + 1 + 2)
                    v.wait_ge(h_in[s], 16 * i + 16)
                    v.wait_ge(h1_out[s], 16 * i + 16)
                    v.scalar_tensor_tensor(h1[s][:].rearrange("p m e -> p (m e)"), n_ps[s][:], kit.scal[:, S_RN:S_RN + 1],
                                           hin[s][:].rearrange("p m e -> p (m e)"), ALU.mult, ALU.add).then_inc(h1_ready, 1)
                    v.drain()
                    for m in range(TU):
                        v.bn_stats(stats[:, m], h1[s][:, m])
                    v.drain()
                    for m in range(TU):
                        v.bn_aggr(mv[:, m], stats[:, m])
                    v.drain()
                    v.tensor_scalar(ve[:], mv[:, :, 1], EPS, None, ALU.add).then_inc(ve_ready, 1)
                    if not last:
                        quantise(*((i, 1) if s == 0 else (i + 1, 0)))
                    v.wait_ge(root2, n + 1)
                    norm_columns(v, rs[:], ve[:], tmp[:])
                    v.wait_ge(x2_out[s], 16 * i + 16)
                    v.wait_ge(t_ready, n + 1)
                    for m in range(TU):
                        ins = v.tensor_scalar(x2[s][:, m], h1[s][:, m], mv[:, m, 0:1], rs[:, m:m + 1],
                                              ALU.subtract, ALU.mult)
                    ins.then_inc(x2_ready, 1)

                quantise(0, 0)
                turns(v, NTURN, step)


SEGS = 128 // EXPERTS
SEG = NTOK // SEGS
HIS = TOPK // HALF
LIFT = 2.0 ** 64
LOWEST = 2.0 ** -63


def sigmoid_scores(v, t):
    v.tensor_scalar(t, t, 3e38, 1.0, ALU.min, ALU.add)
    v.drain()
    v.reciprocal(t, t)
    v.drain()
    v.tensor_scalar(t, t, LIFT, None, ALU.mult)
    v.drain()
    return v.scalar_tensor_tensor(t, t, LOWEST, t, ALU.is_ge, ALU.mult)


def route_phase(kit, lt_d, x2_d, thr_d):
    nc = kit.nc
    with ExitStack() as ctx:
        sc = kit.sb(ctx, "scores", [128, NTILE, EXPERTS], F32)
        thr = kit.sb(ctx, "thresholds", [128, 128, 2], F32)
        with ExitStack() as c1:
            st = kit.sb(c1, "scores_t", [128, SEG], F32)
            mask = kit.sb(c1, "rt_mask", [128, SEG], BF16)
            same = kit.sb(c1, "same_expert", [128, 128], F32)
            cnt = kit.sb(c1, "rt_count", [128, 1], F32)
            res = kit.sb(c1, "rt_result", [128, 2], F32)
            cand = kit.sb(c1, "rt_cand", [128, 1], F32)
            step = kit.sb(c1, "rt_step", [128, 1], F32)
            got = kit.sb(c1, "rt_got", [128, 1], F32)
            tot_ps = kit.ps(c1, "rt_total", [128, 1])
            sem = lambda name: kit.sem(c1, name)
            lt_in, same_ready = sem("rt_lt_in"), sem("rt_same_ready")
            exped, scored, lifted = sem("rt_exped"), sem("rt_scored"), sem("rt_lifted")
            counted, totalled, found = sem("rt_counted"), sem("rt_totalled"), sem("rt_found")
            stored, thr_out, thr_in = sem("rt_stored"), sem("rt_thr_out"), sem("rt_thr_in")
            block = c1.enter_context(nc.Block())
            PROBES = 8 + 23 + 1

            @block.sync
            def _(sp):
                sp.dma_start(st[:], lt_d.rearrange("e (g t) -> (e g) t", g=SEGS)).then_inc(lt_in, 16)
                sp.wait_ge(lifted, 1)
                sp.dma_start(x2_d.rearrange("(t p) e -> p t e", p=128)[:, :, D:ROW], sc[:]).then_inc(stored, 16)
                sp.wait_ge(found, 1)
                sp.dma_start(thr_d, res[:]).then_inc(thr_out, 16)
                sp.wait_ge(thr_out, 16)
                row = thr_d.rearrange("(x p) c -> x (p c)", x=1)
                sp.dma_start(thr[:].rearrange("p e c -> p (e c)"), row.to_broadcast([128, 2 * 128])).then_inc(thr_in, 16)
                sp.wait_ge(thr_in, 16)
                sp.wait_ge(stored, 16)

            @block.gpsimd
            def _(pool):
                nc.gpsimd.memset(same[:], 1.0).then_inc(same_ready, 1)
                pool.wait_ge(same_ready, 1)
                v3 = same[:].rearrange("p (e g) -> p e g", g=SEGS)
                nc.gpsimd.affine_select(out=v3, in_=v3, compare_op=ALU.is_ge, fill=0.0, base=0,
                                        pattern=[[-SEGS, EXPERTS], [0, SEGS]], channel_multiplier=1).then_inc(same_ready, 1)
                pool.wait_ge(same_ready, 2)
                nc.gpsimd.affine_select(out=v3, in_=v3, compare_op=ALU.is_ge, fill=0.0, base=SEGS - 1,
                                        pattern=[[SEGS, EXPERTS], [0, SEGS]], channel_multiplier=-1).then_inc(same_ready, 1)

            @block.scalar
            def _(act):
                act.wait_ge(lt_in, 16)
                act.activation(st[:], st[:], ACT.Exp, scale=-1.0).then_inc(exped, 1)
                act.activation(sc[:].rearrange("p t e -> p (t e)"), kit.logits[:].rearrange("p t e -> p (t e)"), ACT.Exp,
                               scale=-1.0).then_inc(exped, 1)

            @block.tensor
            def _(pe):
                pe.wait_ge(same_ready, 3)
                with pe.Fori(0, PROBES) as i:
                    pe.wait_ge(counted, i + 1)
                    pe.matmul(tot_ps[:], same[:], cnt[:], start=True, stop=True).then_inc(totalled, 1)

            @block.vector
            def _(v):
                v.wait_ge(exped, 2)
                sigmoid_scores(v, st[:]).then_inc(scored, 1)
                sigmoid_scores(v, sc[:].rearrange("p t e -> p (t e)")).then_inc(lifted, 1)
                nc.vector.memset(res[:], 0.0)
                nc.vector.memset(cand[:], LOWEST)
                v.drain()

                def probe(n):
                    v.tensor_scalar(mask[:], st[:], cand[:], None, ALU.is_ge, ALU.add, accum_out=cnt[:]).then_inc(counted, 1)
                    v.wait_ge(totalled, n + 1)
                    v.tensor_scalar(got[:], tot_ps[:], TOPK - 0.5, cand[:], ALU.is_ge, ALU.mult)
                    v.drain()
                    v.tensor_tensor(res[:, 0:1], res[:, 0:1], got[:], ALU.max)
                    v.drain()

                probe(0)
                for k, bits in enumerate((64, 32, 16, 8, 4, 2, 1)):
                    v.tensor_scalar(cand[:], res[:, 0:1], 2.0 ** bits, None, ALU.mult)
                    v.drain()
                    probe(k + 1)
                v.tensor_scalar(step[:], res[:, 0:1], 0.5, None, ALU.mult)
                v.drain()
                with v.Fori(0, 23) as i:
                    v.tensor_tensor(cand[:], res[:, 0:1], step[:], ALU.add)
                    v.drain()
                    v.tensor_scalar(step[:], step[:], 0.5, None, ALU.mult)
                    probe(i + 8)
                v.tensor_scalar(mask[:], st[:], res[:, 0:1], None, ALU.is_gt, ALU.add, accum_out=cnt[:]).then_inc(counted, 1)
                v.wait_ge(totalled, PROBES)
                v.tensor_scalar(res[:, 1:2], tot_ps[:], -1.0, float(TOPK), ALU.mult, ALU.add).then_inc(found, 1)

        kit.clear_semaphores()

        lo1, his = kit.slot_lo, kit.slot_hi
        with ExitStack() as c2:
            above = kit.sb(c2, "rt_above", [128, NTILE, EXPERTS], BF16)
            tie = kit.sb(c2, "rt_tie", [128, NTILE, EXPERTS], BF16)
            early = kit.sb(c2, "rt_early", [128, NTILE, EXPERTS], BF16)
            hi16 = kit.sb(c2, "rt_hi16", [128, NTILE, EXPERTS], I16)
            tri = kit.sb(c2, "rt_tri", [128, 128], BF16)
            ones = kit.sb(c2, "rt_ones", [128, 128], BF16)
            tot = kit.sb(c2, "rt_tot", [NTILE, EXPERTS], F32)
            before = kit.sb(c2, "rt_before", [NTILE, NTILE, EXPERTS], BF16)
            PIECES, PIECE = 4, NTILE * EXPERTS // 4
            rank_ps = kit.ps(c2, "rank_ps", [128, PIECES, 512])
            t_ps = kit.ps(c2, "rt_tot_ps", [NTILE, EXPERTS])
            sem = lambda name: kit.sem(c2, name)
            tri_ready, masked, summed = sem("rt_tri_ready"), sem("rt_masked"), sem("rt_summed")
            tot_copied, spread, ranked = sem("rt_tot_copied"), sem("rt_spread"), sem("rt_ranked")
            block = c2.enter_context(nc.Block())

            @block.gpsimd
            def _(pool):
                nc.gpsimd.memset(ones[:], 1.0).then_inc(tri_ready, 1)
                nc.gpsimd.memset(tri[:], 1.0).then_inc(tri_ready, 1)
                pool.wait_ge(tri_ready, 2)
                nc.gpsimd.affine_select(out=tri[:], in_=tri[:], compare_op=ALU.is_ge, fill=0.0, base=-1,
                                        pattern=[[1, 128]], channel_multiplier=-1).then_inc(tri_ready, 1)
                for r in range(2):
                    pool.wait_ge(tot_copied, r + 1)
                    nc.gpsimd.affine_select(out=before[:], in_=tot[:, None, :].to_broadcast([NTILE, NTILE, EXPERTS]),
                                            compare_op=ALU.is_ge, fill=0.0, base=-1,
                                            pattern=[[1, NTILE], [0, EXPERTS]], channel_multiplier=-1).then_inc(spread, 1)

            @block.scalar
            def _(act):
                for r in range(2):
                    act.wait_ge(summed, r + 1)
                    act.copy(tot[:], t_ps[:]).then_inc(tot_copied, 1)

            @block.tensor
            def _(pe):
                pe.wait_ge(tri_ready, 3)
                for r, m in enumerate((tie, above)):
                    pe.wait_ge(masked, r + 1)
                    for e in range(EXPERTS):
                        mm = pe.matmul(t_ps[:, e:e + 1], m[:, :, e], ones[:, 0:1], start=True, stop=True)
                    mm.then_inc(summed, 1)
                    pe.wait_ge(spread, r + 1)
                    for b in range(PIECES):
                        w = slice(b * PIECE, b * PIECE + PIECE)
                        pe.matmul(rank_ps[:, b, 0:PIECE], tri[:], m[:].rearrange("p t e -> p (t e)")[:, w],
                                  start=True, stop=False)
                        mm = pe.matmul(rank_ps[:, b, 0:PIECE], ones[0:NTILE], before[:].rearrange("p t e -> p (t e)")[:, w],
                                       start=False, stop=True)
                    mm.then_inc(ranked, 1)

            @block.vector
            def _(v):
                def per_expert(c):
                    one = thr[:].rearrange("p (e g) c -> p g c e", g=SEGS)[:, 0, c:c + 1]
                    return one.to_broadcast([128, NTILE, EXPERTS])
                pieces = lambda t: t[:].rearrange("p t e -> p (t e)").rearrange("p (b w) -> p b w", b=PIECES)
                v.tensor_tensor(tie[:], sc[:], per_expert(0), ALU.is_equal).then_inc(masked, 1)
                v.tensor_tensor(above[:], sc[:], per_expert(0), ALU.is_gt)
                v.wait_ge(ranked, 1)
                v.tensor_copy(pieces(hi16), rank_ps[:, :, 0:PIECE])
                v.drain()
                v.tensor_tensor(early[:], hi16[:], per_expert(1), ALU.is_lt)
                v.drain()
                v.tensor_tensor(early[:], early[:], tie[:], ALU.mult)
                v.drain()
                v.tensor_tensor(above[:], above[:], early[:], ALU.add).then_inc(masked, 1)
                v.wait_ge(ranked, 2)
                v.tensor_scalar(pieces(hi16), rank_ps[:, :, 0:PIECE], 1.0 / HALF, 0.5 / HALF - 0.5, ALU.mult, ALU.add)
                v.drain()
                v.tensor_copy(his[:], hi16[:])
                v.scalar_tensor_tensor(pieces(lo1), pieces(hi16), -float(HALF), rank_ps[:, :, 0:PIECE], ALU.mult, ALU.add)
                v.drain()
                v.scalar_tensor_tensor(lo1[:], lo1[:], 1.0, above[:], ALU.add, ALU.mult)


TOP12 = -4096


def split_float32(v, x, top, lo, hi):
    v.tensor_scalar(top.bitcast(I32), x.bitcast(I32), TOP12, None, ALU.bitwise_and)
    v.drain()
    v.tensor_tensor(lo, x, top, ALU.subtract)
    return v.tensor_copy(hi, top)


def split_product(pe, out, w_lo, w_hi, x_lo, x_hi, first, last):
    pe.matmul(out, w_lo, x_hi, start=first, stop=False)
    pe.matmul(out, w_hi, x_lo, start=False, stop=False)
    return pe.matmul(out, w_hi, x_hi, start=False, stop=last)


CH = 4
NCHUNK = HIS // CH
WIDE = CH * HALF


def shared_phase(kit, x2t_d, wsg_t, wsu_t, wsd_t, out_d):
    nc = kit.nc
    FT = FSH // 128
    HOTS = 7
    with ExitStack() as ctx:
        wg = kit.sb(ctx, "ws_g", [KP, KC, FSH], F32)
        wu = kit.sb(ctx, "ws_u", [KP, KC, FSH], F32)
        wd = kit.sb(ctx, "ws_d", [128, FT, D], F32)
        xt = [kit.sb(ctx, f"sh_xt{s}", [KP, KC, WIDE], F32) for s in range(2)]
        g = [kit.sb(ctx, f"sh_g{b}", [128, WIDE], F32) for b in range(2)]
        h = [kit.sb(ctx, f"sh_h{s}", [128, FT, WIDE], F32) for s in range(2)]
        o = [kit.sb(ctx, f"sh_o{s}", [HALF, CH, D], F32) for s in range(2)]
        hin = [kit.sb(ctx, f"sh_in{s}", [HALF, CH, D], F32) for s in range(2)]
        zeros = kit.sb(ctx, "sh_zeros", [128, EXPERTS * 2 * HIS], BF16)
        iota_hi = kit.sb(ctx, "iota_hi", [128, EXPERTS, HIS], BF16)
        iota_lo = kit.sb(ctx, "iota_lo", [128, HALF], BF16)
        iota_p = kit.sb(ctx, "iota_p", [128, 1], F32)
        iota_t = kit.sb(ctx, "iota_t", [128, NTILE], F32)
        hot_hi = kit.sb(ctx, "hot_hi", [128, EXPERTS, HIS], BF16)
        hot_lo = [kit.sb(ctx, f"hot_lo{b}", [128, EXPERTS, HALF], BF16) for b in range(HOTS)]
        val = [kit.sb(ctx, f"hot_val{b}", [128, EXPERTS, 2, HIS], BF16) for b in range(HOTS)]
        slotf = kit.sb(ctx, "slot_f32", [HALF, EXPERTS, 2, HIS], F32)
        g_ps = [kit.ps(ctx, f"sh_g_ps{b}", [128, 512]) for b in range(2)]
        u_ps = [kit.ps(ctx, f"sh_u_ps{b}", [128, 512]) for b in range(2)]
        o_ps = kit.ps(ctx, "sh_o_ps", [HALF, 2, 512])
        slot_ps = kit.ps(ctx, "slot_ps", [HALF, EXPERTS, 2 * HIS])
        sem = lambda name: kit.sem(ctx, name)
        w_in = sem("sh_w_in")
        x_in = [sem(f"sh_x_in{s}") for s in range(2)]
        h_in = [sem(f"sh_h_in{s}") for s in range(2)]
        gu_ready = sem("sh_gu_ready")
        silu_ready = sem("sh_silu_ready")
        h_ready = sem("sh_h_ready")
        down_ready = sem("sh_down_ready")
        o_ready = sem("sh_o_ready")
        o_out = [sem(f"sh_o_out{s}") for s in range(2)]
        sp_turn = sem("sh_sp_turn")
        iotas, zeros_ready = sem("sh_iotas"), sem("sh_zeros_ready")
        hot_ready = sem("sh_hot_ready")
        hot_used = sem("sh_hot_used")
        slots_copied = sem("sh_slots_copied")
        block = ctx.enter_context(nc.Block())
        cols = x2t_d.rearrange("(c p) (i s t) -> s i p c t", p=KP, s=2, t=WIDE)
        rows = out_d.rearrange("(i s j p) e -> s i p j e", s=2, j=CH, p=HALF)

        def tiles_of(i, s, first, last):
            if first:
                return [(u, u) for u in range(4)]
            if last:
                return [(n, n % HOTS) for n in range(NTILE - 5, NTILE)]
            base = 7 * i + (4 if s else 0)
            return [(base + u, ((4 if s else 0) + u) % HOTS) for u in range(3 if s else 4)]

        @block.sync
        def _(sp):
            sp.dma_start(wg[:], wsg_t.rearrange("(c p) f -> p c f", p=KP)).then_inc(w_in, 16)
            sp.dma_start(wu[:], wsu_t.rearrange("(c p) f -> p c f", p=KP)).then_inc(w_in, 16)
            sp.dma_start(wd[:], wsd_t.rearrange("(f p) e -> p f e", p=128)).then_inc(w_in, 16)
            for s in range(2):
                sp.sem_inc(o_out[s], 16)

            def load_x(i, s):
                sp.wait_ge(gu_ready, FT * (2 * i + s) + FT)
                sp.sem_inc(sp_turn, 1)
                sp.dma_start(xt[s][:], cols[s][i]).then_inc(x_in[s], 16)

            def step(i, s, first, last):
                n = 2 * i + s
                if not (type(i) is int and n + 2 >= NPAIR):
                    load_x(i + 1, s)
                sp.wait_ge(o_ready, n + 1)
                sp.sem_inc(sp_turn, 1)
                sp.dma_start(hin[s][:], rows[s][i]).then_inc(h_in[s], 16)
                sp.wait_ge(o_ready, n + 1 + 2)
                sp.sem_inc(sp_turn, 1)
                sp.dma_start(rows[s][i], o[s][:]).then_inc(o_out[s], 16)

            load_x(0, 0)
            load_x(0, 1)
            with sp.Fori(0, NPAIR // 2 - 1) as i:
                for s in range(2):
                    step(i, s, False, False)
            for s in range(2):
                step(NPAIR // 2 - 1, s, False, s == 1)
            for s in range(2):
                sp.wait_ge(o_out[s], 16 * (NPAIR // 2 + 1))

        @block.tensor
        def _(pe):
            pe.sem_inc(gu_ready, 2 * FT)
            pe.sem_inc(down_ready, 2)
            pe.sem_inc(hot_used, HOTS)
            pe.wait_ge(w_in, 48)

            def gate_up(i, s):
                n = 2 * i + s
                pe.wait_ge(x_in[s], 16 * i + 16)
                for f in range(FT):
                    b = (s * FT + f) % 2
                    pe.wait_ge(h_ready, FT * n + f + 1)
                    for ps, w in ((g_ps[b], wg), (u_ps[b], wu)):
                        for c in range(KC):
                            mm = pe.matmul(ps[:, 0:WIDE], w[:, c, f * 128:f * 128 + 128], xt[s][:, c],
                                           start=(c == 0), stop=(c == KC - 1))
                    mm.then_inc(gu_ready, 1)

            def down(i, s):
                n = 2 * i + s
                pe.wait_ge(h_ready, FT * n + FT + 2)
                pe.wait_ge(o_ready, n + 1 + 1)
                for j in range(CH):
                    for f in range(FT):
                        mm = pe.matmul(o_ps[:, j // 2, j % 2 * D:j % 2 * D + D], h[s][:, f, j * HALF:j * HALF + HALF],
                                       wd[:, f], start=(f == 0), stop=(f == FT - 1))
                mm.then_inc(down_ready, 1)

            def place(tiles, last):
                for n, b in tiles:
                    pe.wait_ge(hot_ready, n + 1)
                    for e in range(EXPERTS):
                        mm = pe.matmul(slot_ps[:, e], hot_lo[b][:, e], val[b][:, e].rearrange("p c h -> p (c h)"),
                                       start=False, stop=(last and n == NTILE - 1), skip_group_check=True)
                    mm.then_inc(hot_used, 1)

            def step(i, s, first, last):
                if not last:
                    gate_up(*((i, 1) if s == 0 else (i + 1, 0)))
                if not first:
                    place(tiles_of(i - 1 + s, 1 - s, False, False), False)
                down(i, s)
                if last:
                    place(tiles_of(i, s, False, True), True)

            gate_up(0, 0)
            pe.wait_ge(zeros_ready, 1)
            pe.matmul(slot_ps[:].rearrange("p e x -> p (e x)"), zeros[:, 0:HALF], zeros[:], start=True, stop=False,
                      skip_group_check=True)
            turns(pe, NPAIR, step)

        @block.scalar
        def _(act):
            with act.Fori(0, NPAIR // 2) as i:
                for s in range(2):
                    n = 2 * i + s
                    for f in range(FT):
                        b = (s * FT + f) % 2
                        act.wait_ge(gu_ready, FT * n + f + 1 + 2 * FT)
                        act.wait_ge(h_ready, FT * n + f + 1)
                        act.activation(g[b][:], g_ps[b][:, 0:WIDE], ACT.Silu).then_inc(silu_ready, 1)
            act.wait_ge(hot_used, NTILE + HOTS)
            act.copy(slotf[:].rearrange("p e c h -> p e (c h)"), slot_ps[:]).then_inc(slots_copied, 1)

        @block.gpsimd
        def _(pool):
            io = dict(allow_small_or_imprecise_dtypes=True)
            nc.gpsimd.iota(iota_hi[:], pattern=[[0, EXPERTS], [1, HIS]], base=0, channel_multiplier=0, **io).then_inc(iotas, 1)
            nc.gpsimd.iota(iota_lo[:], pattern=[[1, HALF]], base=1, channel_multiplier=0, **io).then_inc(iotas, 1)
            nc.gpsimd.iota(iota_p[:], pattern=[[0, 1]], base=0, channel_multiplier=1, **io).then_inc(iotas, 1)
            nc.gpsimd.iota(iota_t[:], pattern=[[1, NTILE]], base=0, channel_multiplier=0, **io).then_inc(iotas, 1)
            pool.wait_ge(iotas, 4)

        @block.vector
        def _(v):
            v.sem_inc(h_ready, 2)
            v.sem_inc(o_ready, 2)
            nc.vector.memset(zeros[:], 0.0).then_inc(zeros_ready, 1)

            def one_hots(n, b):
                v.wait_ge(hot_used, n + 1)
                column = lambda t: t[:, bass.ds(n, 1)].rearrange("p i e -> p (i e)")[:, :, None]
                v.tensor_tensor(hot_lo[b][:], iota_lo[:, None, :].to_broadcast([128, EXPERTS, HALF]),
                                column(kit.slot_lo).to_broadcast([128, EXPERTS, HALF]), ALU.is_equal)
                v.tensor_tensor(hot_hi[:], iota_hi[:], column(kit.slot_hi).to_broadcast([128, EXPERTS, HIS]), ALU.is_equal)
                v.drain()
                v.tensor_scalar(val[b][:, :, 0], hot_hi[:], iota_p[:], None, ALU.mult)
                v.tensor_tensor(val[b][:, :, 1], hot_hi[:], iota_t[:, bass.ds(n, 1)][:, :, None].to_broadcast([128, EXPERTS, HIS]),
                                ALU.mult).then_inc(hot_ready, 1)
                v.drain()

            def gated(i, s, f):
                n = 2 * i + s
                if f == 0:
                    v.wait_ge(down_ready, n + 1)
                b = (s * FT + f) % 2
                v.wait_ge(silu_ready, FT * n + f + 1)
                v.tensor_tensor(h[s][:, f], u_ps[b][:, 0:WIDE], g[b][:], ALU.mult).then_inc(h_ready, 1)

            def step(i, s, first, last):
                n = 2 * i + s
                tiles = tiles_of(i, s, first, last)
                for f in range(FT):
                    if not last:
                        gated(*((i, 1) if s == 0 else (i + 1, 0)), f)
                    one_hots(*tiles[f])
                for t in tiles[FT:]:
                    one_hots(*t)
                v.wait_ge(down_ready, n + 1 + 2)
                v.wait_ge(h_in[s], 16 * i + 16)
                v.wait_ge(o_out[s], 16 * i + 16)
                v.tensor_tensor(o[s][:].rearrange("p (a b) e -> p a (b e)", a=2), o_ps[:, :, 0:2 * D],
                                hin[s][:].rearrange("p (a b) e -> p a (b e)", a=2), ALU.add).then_inc(o_ready, 1)

            for f in range(FT):
                gated(0, 0, f)
            v.wait_ge(iotas, 4)
            turns(v, NPAIR, step)
            v.wait_ge(slots_copied, 1)
            v.scalar_tensor_tensor(kit.slots[:], slotf[:, :, 1], 128.0, slotf[:, :, 0], ALU.mult, ALU.add)


def expert_phase(kit, x2_d, wg_t, wu_t, wd_t, out_d):
    nc = kit.nc
    FT = FEXP // 128
    LOCAL = 2 * NCHUNK
    SEED = NCHUNK + 2
    with ExitStack() as ctx:
        wg = [kit.sb(ctx, f"we_g{x}", [KP, KC, FEXP], F32) for x in range(2)]
        wu = [kit.sb(ctx, f"we_u{x}", [KP, KC, FEXP], F32) for x in range(2)]
        wd = [kit.sb(ctx, f"we_d{x}", [128, FT, D], F32) for x in range(2)]
        idx = [kit.sb(ctx, f"idx{x}", [HALF, HIS], I32) for x in range(2)]
        xg = [kit.sb(ctx, f"ex_xg{s}", [HALF, CH, ROW], F32) for s in range(2)]
        wgl, wgh, wul, wuh = [[kit.sb(ctx, f"we_{n}{x}", [KP, KC, FEXP], F32R) for x in range(2)]
                              for n in ("g_lo", "g_hi", "u_lo", "u_hi")]
        xt = kit.sb(ctx, "ex_xt", [KP, KC, WIDE], F32)
        xtl = [kit.sb(ctx, f"ex_xt_lo{s}", [KP, KC, WIDE], F32R) for s in range(2)]
        xth = [kit.sb(ctx, f"ex_xt_hi{s}", [KP, KC, WIDE], F32R) for s in range(2)]
        top = kit.sb(ctx, "ex_top", [KP, KC, WIDE], F32)
        sc = [kit.sb(ctx, f"ex_sc{s}", [HALF, CH], F32) for s in range(2)]
        g = [kit.sb(ctx, f"ex_g{b}", [128, WIDE], F32) for b in range(2)]
        h = [kit.sb(ctx, f"ex_h{s}", [128, FT, WIDE], F32) for s in range(2)]
        o = [kit.sb(ctx, f"ex_o{s}", [HALF, CH, D], F32) for s in range(2)]
        t_ps = kit.ps(ctx, "ex_t_ps", [KP, KC, 512])
        g_ps = [kit.ps(ctx, f"ex_g_ps{b}", [128, 512]) for b in range(2)]
        u_ps = [kit.ps(ctx, f"ex_u_ps{b}", [128, 512]) for b in range(2)]
        o_ps = kit.ps(ctx, "ex_o_ps", [HALF, 2, 512])
        sem = lambda name: kit.sem(ctx, name)
        w_in = [sem(f"ex_w_in{x}") for x in range(2)]
        w_split = sem("ex_w_split")
        x_split = sem("ex_x_split")
        idx_ready = sem("ex_idx_ready")
        x_in = [sem(f"ex_x_in{s}") for s in range(2)]
        t_ready = sem("ex_t_ready")
        t_copied = sem("ex_t_copied")
        sc_ready = sem("ex_sc_ready")
        gu_ready = sem("ex_gu_ready")
        silu_ready = sem("ex_silu_ready")
        h_ready = sem("ex_h_ready")
        down_ready = sem("ex_down_ready")
        o_ready = sem("ex_o_ready")
        added = [sem(f"ex_added{s}") for s in range(2)]
        o_free = sem("ex_o_free")
        pool_turn = sem("ex_pool_turn")
        sp_turn = sem("ex_sp_turn")
        block = ctx.enter_context(nc.Block())

        def turn(engine, step):
            with engine.Fori(0, EXPERTS // 2 - 1) as i:
                for k in range(LOCAL):
                    step(i, k, False)
            for k in range(LOCAL):
                step(EXPERTS // 2 - 1, k, k == LOCAL - 1)

        @block.sync
        def _(sp):
            by_pair = lambda a, p: a.rearrange("(i x) (c p) f -> x i p c f", x=2, p=p)
            with sp.Fori(0, EXPERTS // 2) as i:
                for x in range(2):
                    sp.wait_ge(down_ready, NCHUNK * (2 * i + x) + SEED - NCHUNK)
                    sp.sem_inc(sp_turn, 1)
                    sp.dma_start(wg[x][:], by_pair(wg_t, KP)[x][i]).then_inc(w_in[x], 16)
                    sp.dma_start(wu[x][:], by_pair(wu_t, KP)[x][i]).then_inc(w_in[x], 16)
                    sp.dma_start(wd[x][:], by_pair(wd_t, 128)[x][i]).then_inc(w_in[x], 16)

        @block.gpsimd
        def _(pool):
            def take_slots(i, x):
                one = kit.slots[:].rearrange("p (i x) h -> p x i h", x=2)[:, x, bass.ds(i, 1)].rearrange("p i h -> p (i h)")
                nc.gpsimd.tensor_copy(idx[x][:], one).then_inc(idx_ready, 1)
                pool.wait_ge(idx_ready, 2 * i + x + 1)
                pool.sem_inc(pool_turn, 1)

            def gather(k):
                x, q = divmod(k % LOCAL, NCHUNK)
                for j in range(CH):
                    nc.gpsimd.indirect_dma_start(
                        out=xg[k % 2][:, j], out_offset=None, in_=x2_d,
                        in_offset=bass.IndirectOffsetOnAxis(ap=idx[x][:, q * CH + j:q * CH + j + 1], axis=0))\
                        .then_inc(x_in[k % 2], 16)

            def scatter_add(k):
                x, q = divmod(k % LOCAL, NCHUNK)
                for j in range(CH):
                    nc.gpsimd.indirect_dma_start(
                        out=out_d, out_offset=bass.IndirectOffsetOnAxis(ap=idx[x][:, q * CH + j:q * CH + j + 1], axis=0),
                        in_=o[k % 2][:, j], in_offset=None, compute_op=ALU.add).then_inc(added[k % 2], 16)

            def step(i, k, last):
                n = LOCAL * i + k
                if not (type(i) is int and k + 2 >= LOCAL):
                    if k + 2 == NCHUNK:
                        take_slots(i, 1)
                    elif k + 2 == LOCAL:
                        take_slots(i + 1, 0)
                    pool.wait_ge(t_ready, n + 1)
                    pool.wait_ge(sc_ready, n + 1)
                    pool.sem_inc(pool_turn, 1)
                    gather(k + 2)
                pool.wait_ge(o_ready, n + 1 + 1)
                pool.sem_inc(pool_turn, 1)
                scatter_add(k)
                pool.wait_ge(added[k % 2], CH * 16 * (LOCAL // 2 * i + k // 2 + 1))
                pool.sem_inc(o_free, 1)

            take_slots(0, 0)
            gather(0)
            gather(1)
            turn(pool, step)

        @block.tensor
        def _(pe):
            pe.sem_inc(down_ready, SEED)

            def transpose_x(i, k):
                n = LOCAL * i + k
                s = k % 2
                pe.wait_ge(x_in[s], CH * 16 * (LOCAL // 2 * i + k // 2 + 1))
                for c in range(KC):
                    for j in range(CH):
                        mm = pe.transpose(t_ps[:, c, j * HALF:j * HALF + HALF], xg[s][:, j, c * KP:c * KP + KP],
                                          kit.ident[0:HALF, 0:HALF])
                mm.then_inc(t_ready, 1)

            def step(i, k, last):
                n = LOCAL * i + k
                s, x = k % 2, k // NCHUNK
                if k % NCHUNK == 0:
                    pe.wait_ge(w_split, 2 * i + x + 1)
                pe.wait_ge(x_split, n + 1 + 1)
                for f in range(FT):
                    b = f % 2
                    pe.wait_ge(h_ready, FT * n + f + 1)
                    for ps, wl, wh in ((g_ps[b], wgl[x], wgh[x]), (u_ps[b], wul[x], wuh[x])):
                        for c in range(KC):
                            cut = slice(f * 128, f * 128 + 128)
                            mm = split_product(pe, ps[:, 0:WIDE], wl[:, c, cut], wh[:, c, cut], xtl[s][:, c], xth[s][:, c],
                                               c == 0, c == KC - 1)
                    mm.then_inc(gu_ready, 1)
                if not last:
                    if k + 1 == LOCAL:
                        transpose_x(i + 1, 0)
                    else:
                        transpose_x(i, k + 1)
                pe.wait_ge(h_ready, FT * n + FT + 2)
                pe.wait_ge(o_ready, n + 1)
                for j in range(CH):
                    for f in range(FT):
                        mm = pe.matmul(o_ps[:, j // 2, j % 2 * D:j % 2 * D + D], h[s][:, f, j * HALF:j * HALF + HALF],
                                       wd[x][:, f], start=(f == 0), stop=(f == FT - 1))
                mm.then_inc(down_ready, 1)

            transpose_x(0, 0)
            turn(pe, step)

        @block.scalar
        def _(act):
            def copy_x(i, k):
                act.wait_ge(t_ready, LOCAL * i + k + 1)
                act.wait_ge(x_split, LOCAL * i + k + 1)
                for c in range(KC):
                    ins = act.copy(xt[:, c], t_ps[:, c, 0:WIDE])
                ins.then_inc(t_copied, 1)

            def step(i, k, last):
                n = LOCAL * i + k
                for f in range(FT):
                    b = f % 2
                    act.wait_ge(gu_ready, FT * n + f + 1)
                    act.wait_ge(h_ready, FT * n + f + 1)
                    act.activation(g[b][:], g_ps[b][:, 0:WIDE], ACT.Silu).then_inc(silu_ready, 1)
                if not last:
                    copy_x(*((i + 1, 0) if k + 1 == LOCAL else (i, k + 1)))

            copy_x(0, 0)
            turn(act, step)

        @block.vector
        def _(v):
            v.sem_inc(h_ready, 2)
            v.sem_inc(o_ready, 1)
            v.sem_inc(o_free, 2)
            v.sem_inc(x_split, 1)

            def split_x(i, k):
                v.drain()
                v.wait_ge(t_copied, LOCAL * i + k + 1)
                split_float32(v, xt[:], top[:], xtl[k % 2][:], xth[k % 2][:]).then_inc(x_split, 1)

            def split_weights(i, x, which, part):
                v.drain()
                v.wait_ge(w_in[x], 48 * i + 48)
                w, wl, wh = ((wg, wgl, wgh), (wu, wul, wuh))[which]
                cut = slice(part * FEXP // 3, (part + 1) * FEXP // 3)
                ins = split_float32(v, w[x][:, :, cut], top[:, :, 0:FEXP // 3], wl[x][:, :, cut], wh[x][:, :, cut])
                if which == 1 and part == 2:
                    ins.then_inc(w_split, 1)

            def step(i, k, last):
                n = LOCAL * i + k
                s, x = k % 2, k // NCHUNK
                v.wait_ge(x_in[s], CH * 16 * (LOCAL // 2 * i + k // 2 + 1))
                mine = xg[s][:, :, D:ROW].rearrange("p j (i x) -> p x j i", x=2)[:, x][:, :, bass.ds(i, 1)]
                v.tensor_scalar(sc[s][:, :, None], mine, 1.0 / LIFT, None, ALU.mult).then_inc(sc_ready, 1)
                v.wait_ge(down_ready, n - 1 + SEED)
                for f in range(FT):
                    b = f % 2
                    v.wait_ge(silu_ready, FT * n + f + 1)
                    v.tensor_tensor(h[s][:, f], u_ps[b][:, 0:WIDE], g[b][:], ALU.mult).then_inc(h_ready, 1)
                    if k % NCHUNK >= 2 and f % 2 and not (type(i) is int and x == 1):
                        split_weights(i + x, 1 - x, k % 2, f // 2)
                if not last:
                    split_x(*((i + 1, 0) if k + 1 == LOCAL else (i, k + 1)))
                v.wait_ge(down_ready, n + 1 + SEED)
                v.wait_ge(o_free, n + 1)
                for j in range(CH):
                    ins = v.tensor_scalar(o[s][:, j], o_ps[:, j // 2, j % 2 * D:j % 2 * D + D], sc[s][:, j:j + 1], None,
                                          ALU.mult)
                ins.then_inc(o_ready, 1)

            for part in range(6):
                split_weights(0, 0, part // 3, part % 3)
            split_x(0, 0)
            turn(v, step)


def build(nc, A, O):
    with ExitStack() as ctx:
        kit = Kit(nc, ctx)
        kit.scal = kit.sb(ctx, "scalars", [128, NSCAL], F32)
        kit.ident = kit.sb(ctx, "ident", [128, 128], F32)
        kit.identb = kit.sb(ctx, "identb", [128, 128], BF16)
        kit.w_in = kit.sb(ctx, "w_in", [128, KC, 3 * D], BF16)
        kit.w_out = kit.sb(ctx, "w_out", [128, 3, D], BF16)
        dram = lambda name, shape, dt: nc.dram_tensor(name, shape, dt, kind="Internal").ap()
        h_d = dram("h_tokens", (NTOK, D), F32)
        xt_d = dram("x_columns", (D, NTOK), F32)
        qk_d = dram("qk_columns", (2 * D, NTOK), F32)
        v_d = dram("v_tokens", (NTOK, D), F32)
        qb_d = dram("q_whole", (NPAIR, 128, 3 * PAIR), BF16)
        kb_d = dram("k_whole", (NPAIR, 128, 3 * PAIR), BF16)
        vb_d = dram("v_whole", (NPAIR, HALF, 4 * HEADS * 32), BF16)
        r_d = dram("row_factors", (NPAIR, 48 * HALF), F32)
        ctx_d = dram("context_t", (NPAIR, 128, 3 * PAIR), F32)
        mneg_d = dram("row_maxima", (NPAIR, 48, HALF), BF16)
        kit.logits = kit.sb(ctx, "logits", [128, NTILE, EXPERTS], F32)
        x2_d = dram("x2_rows", (NTOK, ROW), F32)
        x2t_d = dram("x2_columns", (D, NTOK), F32)
        lt_d = dram("logits_t", (EXPERTS, NTOK), F32)
        thr_d = dram("threshold_rows", (128, 2), F32)
        kit.slot_lo = kit.sb(ctx, "slot_lo", [128, NTILE, EXPERTS], BF16)
        kit.slot_hi = kit.sb(ctx, "slot_hi", [128, NTILE, EXPERTS], BF16)
        kit.slots = kit.sb(ctx, "slots", [HALF, EXPERTS, HIS], I32)
        setup_phase(kit, A["w_in_t"], A["w_out_t"])
        kit.clear_semaphores()
        tokenize_phase(kit, A["patches"], A["txt"], A["chan_w"], h_d, qk_d, v_d, xt_d)
        kit.clear_semaphores()
        score_range_phase(kit, qk_d, v_d, qb_d, kb_d, vb_d, mneg_d)
        kit.clear_semaphores()
        row_sum_phase(kit, qb_d, kb_d, r_d)
        kit.clear_semaphores()
        context_phase(kit, qb_d, kb_d, vb_d, r_d, ctx_d)
        kit.clear_semaphores()
        mixer_out_phase(kit, ctx_d, xt_d, h_d, A["gate_wt"], x2_d, x2t_d, lt_d, O)
        kit.clear_semaphores()
        route_phase(kit, lt_d, x2_d, thr_d)
        kit.clear_semaphores()
        shared_phase(kit, x2t_d, A["wsg_t"], A["wsu_t"], A["wsd_t"], O)
        kit.clear_semaphores()
        expert_phase(kit, x2_d, A["wg_t"], A["wu_t"], A["wd_t"], O)

def kernel(x, txt, L0_tok_channel_weights, L0_attn_w_in, L0_attn_w_out, L0_ffn_gate_weight, L0_ffn_Wg, L0_ffn_Wu,
           L0_ffn_Wd, L0_ffn_Ws_g, L0_ffn_Ws_u, L0_ffn_Ws_d):
    import numpy as _np
    import concourse.bacc as _bacc
    from concourse import mybir as _mybir
    from concourse.bass_utils import run_bass_kernel_spmd as _run

    flat = _np.ascontiguousarray
    patches = x.reshape(BATCH, CHAN, GRID, PATCH, GRID, PATCH).transpose(0, 2, 4, 1, 3, 5)
    laid = dict(
        patches=flat(patches).reshape(BATCH * NPATCH, CHAN * PATCH * PATCH),
        txt=flat(txt),
        chan_w=flat(L0_tok_channel_weights),
        w_in_t=flat(L0_attn_w_in.T),
        w_out_t=flat(L0_attn_w_out.T),
        gate_wt=flat(L0_ffn_gate_weight.T),
        wg_t=flat(L0_ffn_Wg.transpose(0, 2, 1)),
        wu_t=flat(L0_ffn_Wu.transpose(0, 2, 1)),
        wd_t=flat(L0_ffn_Wd.transpose(0, 2, 1)),
        wsg_t=flat(L0_ffn_Ws_g.T),
        wsu_t=flat(L0_ffn_Ws_u.T),
        wsd_t=flat(L0_ffn_Ws_d.T),
    )
    nc = _bacc.Bacc("TRN2", target_bir_lowering=False, num_devices=1)
    arrays, A = {}, {}
    for name, a in laid.items():
        arrays[f"in_{name}_dram"] = a
        A[name] = nc.dram_tensor(f"in_{name}_dram", a.shape, _mybir.dt.from_np(a.dtype), kind="ExternalInput").ap()
    out = nc.dram_tensor("out_0_dram", (BATCH, SEQ, D), F32, kind="ExternalOutput").ap()
    build(nc, A, out.rearrange("b t e -> (b t) e"))
    r = _run(nc, [arrays], core_ids=[0])
    return r.results[0]["out_0_dram"]
```
